# Optimizing a Trainium2 kernel written in Bass

```python
import numpy as np
import jax
import jax.numpy as jnp

def _softmax(x, axis=-1):
    return jax.nn.softmax(x, axis=axis)

def _gelu(x):
    return jax.nn.gelu(x, approximate=True)

def _silu(x):
    return jax.nn.silu(x)

def _sigmoid(x):
    return jax.nn.sigmoid(x)

def _layernorm(x, axis=-1, eps=1e-05):
    m = jnp.mean(x, axis=axis, keepdims=True)
    v = jnp.var(x, axis=axis, keepdims=True)
    return (x - m) / jnp.sqrt(v + eps)

def _scatter_add(tgt, idx, src, axis=0):
    return tgt.at[idx].add(src)

def _segment_sum(src, seg, n):
    return jax.ops.segment_sum(src, seg, n)
kernel_name = 'mk_hybrid_d1_jaxref_r8_2a3c00'

def setup_inputs(seed: int=0):
    np.random.seed(seed)
    _w = jnp.asarray

    def _L0_attn_a_setup():
        import jax, jax.numpy as jnp
        import numpy as np
        N_HEAD = 16
        HEAD_SIZE = 128
        EMBED = 128
        MULTI_HEAD_SIZE = HEAD_SIZE // N_HEAD
        B, S = (4, 256)
        key = jax.random.key(seed)
        k1, k2, k3, k4 = jax.random.split(key, 4)
        x = jax.random.normal(k1, (B, S, EMBED), dtype=jnp.float32)
        w_qkv = jax.random.normal(k2, (3 * HEAD_SIZE, EMBED), dtype=jnp.float32) * 0.02
        w_proj = jax.random.normal(k3, (EMBED, HEAD_SIZE), dtype=jnp.float32) * 0.02
        b_proj = jax.random.normal(k4, (EMBED,), dtype=jnp.float32) * 0.02
        return {'x': x, 'w_qkv': w_qkv, 'w_proj': w_proj, 'b_proj': b_proj}
    _L0_attn_a_in = _L0_attn_a_setup()

    def _L0_attn_b_setup():
        import jax, jax.numpy as jnp
        import numpy as np
        import math
        D_MODEL = 128
        D_STATE = 128
        D_CONV = 4
        EXPAND = 2
        HEADDIM = 64
        NGROUPS = 1
        D_INNER = EXPAND * D_MODEL
        D_SSM = D_INNER
        NHEADS = D_SSM // HEADDIM
        CONV_DIM = D_SSM + 2 * NGROUPS * D_STATE
        D_IN_PROJ = 2 * D_INNER + 2 * NGROUPS * D_STATE + NHEADS
        EPS = 1e-05
        DT_MIN, DT_MAX = (0.001, 0.1)

        def _mamba2_forward(u, W_in, conv_w, conv_b, dt_bias, A_log, D, norm_w, W_out):
            b, L, _ = u.shape
            zxbcdt = jnp.einsum('bld,ed->ble', u, W_in)
            z = zxbcdt[..., :D_SSM]
            xBC = zxbcdt[..., D_SSM:D_SSM + CONV_DIM]
            dt = zxbcdt[..., D_SSM + CONV_DIM:]
            dt = jax.nn.softplus(dt + dt_bias)
            xp = jnp.pad(xBC, ((0, 0), (D_CONV - 1, 0), (0, 0)))
            conv = conv_b
            for w in range(D_CONV):
                conv = conv + xp[:, w:w + L, :] * conv_w[:, w]
            xBC = jax.nn.silu(conv)
            x = xBC[..., :D_SSM].reshape(b, L, NHEADS, HEADDIM)
            B = xBC[..., D_SSM:D_SSM + D_STATE]
            C = xBC[..., D_SSM + D_STATE:]
            A = -jnp.exp(A_log)
            dA = jnp.exp(dt * A)
            dtx = dt[..., None] * x

            def step(h, inp):
                dA_t, dtx_t, B_t, C_t = inp
                h = h * dA_t[:, :, None, None] + jnp.einsum('bhp,bn->bhpn', dtx_t, B_t)
                y_t = jnp.einsum('bhpn,bn->bhp', h, C_t)
                return (h, y_t)
            h0 = jnp.zeros((b, NHEADS, HEADDIM, D_STATE), dtype=u.dtype)
            inputs = (jnp.moveaxis(dA, 1, 0), jnp.moveaxis(dtx, 1, 0), jnp.moveaxis(B, 1, 0), jnp.moveaxis(C, 1, 0))
            _, y = jax.lax.scan(step, h0, inputs)
            y = jnp.moveaxis(y, 0, 1) + x * D[None, None, :, None]
            y = y.reshape(b, L, D_SSM)
            g = y * jax.nn.silu(z)
            g = g * jax.lax.rsqrt(jnp.mean(g * g, axis=-1, keepdims=True) + EPS) * norm_w
            return jnp.einsum('ble,de->bld', g, W_out)
        key = jax.random.key(seed)
        ks = jax.random.split(key, 8)
        u = jax.random.normal(ks[0], (2, 512, D_MODEL), dtype=jnp.float32)
        W_in = jax.random.normal(ks[1], (D_IN_PROJ, D_MODEL), dtype=jnp.float32) * 0.02
        conv_w = jax.random.normal(ks[2], (CONV_DIM, D_CONV), dtype=jnp.float32) * 0.1
        conv_b = jnp.zeros((CONV_DIM,), dtype=jnp.float32)
        dt = jnp.exp(jax.random.uniform(ks[3], (NHEADS,)) * (math.log(DT_MAX) - math.log(DT_MIN)) + math.log(DT_MIN))
        dt_bias = dt + jnp.log(-jnp.expm1(-dt))
        A_log = jnp.log(jax.random.uniform(ks[4], (NHEADS,), minval=1.0, maxval=16.0))
        D = jnp.ones((NHEADS,), dtype=jnp.float32)
        norm_w = jnp.ones((D_SSM,), dtype=jnp.float32)
        W_out = jax.random.normal(ks[5], (D_MODEL, D_INNER), dtype=jnp.float32) * 0.02
        return {'u': u, 'W_in': W_in, 'conv_w': conv_w, 'conv_b': conv_b, 'dt_bias': dt_bias, 'A_log': A_log, 'D': D, 'norm_w': norm_w, 'W_out': W_out}
    _L0_attn_b_in = _L0_attn_b_setup()

    def _L0_ffn_setup():
        import jax, jax.numpy as jnp
        import numpy as np
        ALPHA = 1.702
        LIMIT = 7.0
        EPS = 1e-05
        E = 16
        K = 4

        def _swiglu(h):
            x_glu = jnp.minimum(h[..., ::2], LIMIT)
            x_lin = jnp.clip(h[..., 1::2], LIMIT, LIMIT)
            return x_glu * jax.nn.sigmoid(ALPHA * x_glu) * (x_lin + 1.0)
        key = jax.random.key(seed)
        ks = jax.random.split(key, 7)
        B, T, H, I = (1, 256, 128, 128)
        x = jax.random.normal(ks[0], (B, T, H), jnp.float32)
        scale = jnp.ones((H,), jnp.float32)
        gate_w = jax.random.normal(ks[1], (E, H), jnp.float32) * 0.02
        gate_b = jnp.zeros((E,), jnp.float32)
        mlp1_w = jax.random.normal(ks[2], (E, 2 * I, H), jnp.float32) * 0.02
        mlp1_b = jax.random.normal(ks[3], (E, 2 * I), jnp.float32) * 0.02
        mlp2_w = jax.random.normal(ks[4], (E, H, I), jnp.float32) * 0.02
        mlp2_b = jax.random.normal(ks[5], (E, H), jnp.float32) * 0.02
        return dict(x=x, scale=scale, gate_w=gate_w, gate_b=gate_b, mlp1_w=mlp1_w, mlp1_b=mlp1_b, mlp2_w=mlp2_w, mlp2_b=mlp2_b)
    _L0_ffn_in = _L0_ffn_setup()
    _d = {'L0_attn_a_x': _L0_attn_a_in['x'], 'L0_attn_a_w_qkv': _L0_attn_a_in['w_qkv'], 'L0_attn_a_w_proj': _L0_attn_a_in['w_proj'], 'L0_attn_a_b_proj': _L0_attn_a_in['b_proj'], 'L0_attn_b_W_in': _L0_attn_b_in['W_in'], 'L0_attn_b_conv_w': _L0_attn_b_in['conv_w'], 'L0_attn_b_conv_b': _L0_attn_b_in['conv_b'], 'L0_attn_b_dt_bias': _L0_attn_b_in['dt_bias'], 'L0_attn_b_A_log': _L0_attn_b_in['A_log'], 'L0_attn_b_D': _L0_attn_b_in['D'], 'L0_attn_b_norm_w': _L0_attn_b_in['norm_w'], 'L0_attn_b_W_out': _L0_attn_b_in['W_out'], 'L0_ffn_scale': _L0_ffn_in['scale'], 'L0_ffn_gate_w': _L0_ffn_in['gate_w'], 'L0_ffn_gate_b': _L0_ffn_in['gate_b'], 'L0_ffn_mlp1_w': _L0_ffn_in['mlp1_w'], 'L0_ffn_mlp1_b': _L0_ffn_in['mlp1_b'], 'L0_ffn_mlp2_w': _L0_ffn_in['mlp2_w'], 'L0_ffn_mlp2_b': _L0_ffn_in['mlp2_b']}
    _x0 = _d['L0_attn_a_x']
    _d['L0_attn_a_x'] = jax.random.normal(jax.random.fold_in(jax.random.key(seed), 1), (8, 512, 128), dtype=_x0.dtype)
    del _x0
    return _d

def reference(L0_attn_a_x, L0_attn_a_w_qkv, L0_attn_a_w_proj, L0_attn_a_b_proj, L0_attn_b_W_in, L0_attn_b_conv_w, L0_attn_b_conv_b, L0_attn_b_dt_bias, L0_attn_b_A_log, L0_attn_b_D, L0_attn_b_norm_w, L0_attn_b_W_out, L0_ffn_scale, L0_ffn_gate_w, L0_ffn_gate_b, L0_ffn_mlp1_w, L0_ffn_mlp1_b, L0_ffn_mlp2_w, L0_ffn_mlp2_b):

    def _L0_attn_a_ref(x, w_qkv, w_proj, b_proj):
        import jax, jax.numpy as jnp
        import numpy as np
        N_HEAD = 16
        HEAD_SIZE = 128
        EMBED = 128
        MULTI_HEAD_SIZE = HEAD_SIZE // N_HEAD
        B, S = (4, 256)
        qkv = jnp.einsum('bse,he->bsh', x, w_qkv)
        q, k, v = jnp.split(qkv, 3, axis=-1)
        scale = 1.0 / np.sqrt(MULTI_HEAD_SIZE).astype(np.float32)
        scores = jnp.einsum('bqh,bkh->bqk', q, k) * scale
        probs = jax.nn.softmax(scores, axis=-1)
        out = jnp.einsum('bqk,bkh->bqh', probs, v)
        Bn, Sn, H = out.shape
        out = jnp.swapaxes(out, 1, 2).reshape(Bn, Sn, H)
        out = jnp.einsum('bsh,eh->bse', out, w_proj) + b_proj
        return out

    def _L0_attn_b_ref(u, W_in, conv_w, conv_b, dt_bias, A_log, D, norm_w, W_out):
        import jax, jax.numpy as jnp
        import numpy as np
        import math
        D_MODEL = 128
        D_STATE = 128
        D_CONV = 4
        EXPAND = 2
        HEADDIM = 64
        NGROUPS = 1
        D_INNER = EXPAND * D_MODEL
        D_SSM = D_INNER
        NHEADS = D_SSM // HEADDIM
        CONV_DIM = D_SSM + 2 * NGROUPS * D_STATE
        D_IN_PROJ = 2 * D_INNER + 2 * NGROUPS * D_STATE + NHEADS
        EPS = 1e-05
        DT_MIN, DT_MAX = (0.001, 0.1)

        def _mamba2_forward(u, W_in, conv_w, conv_b, dt_bias, A_log, D, norm_w, W_out):
            b, L, _ = u.shape
            zxbcdt = jnp.einsum('bld,ed->ble', u, W_in)
            z = zxbcdt[..., :D_SSM]
            xBC = zxbcdt[..., D_SSM:D_SSM + CONV_DIM]
            dt = zxbcdt[..., D_SSM + CONV_DIM:]
            dt = jax.nn.softplus(dt + dt_bias)
            xp = jnp.pad(xBC, ((0, 0), (D_CONV - 1, 0), (0, 0)))
            conv = conv_b
            for w in range(D_CONV):
                conv = conv + xp[:, w:w + L, :] * conv_w[:, w]
            xBC = jax.nn.silu(conv)
            x = xBC[..., :D_SSM].reshape(b, L, NHEADS, HEADDIM)
            B = xBC[..., D_SSM:D_SSM + D_STATE]
            C = xBC[..., D_SSM + D_STATE:]
            A = -jnp.exp(A_log)
            dA = jnp.exp(dt * A)
            dtx = dt[..., None] * x

            def step(h, inp):
                dA_t, dtx_t, B_t, C_t = inp
                h = h * dA_t[:, :, None, None] + jnp.einsum('bhp,bn->bhpn', dtx_t, B_t)
                y_t = jnp.einsum('bhpn,bn->bhp', h, C_t)
                return (h, y_t)
            h0 = jnp.zeros((b, NHEADS, HEADDIM, D_STATE), dtype=u.dtype)
            inputs = (jnp.moveaxis(dA, 1, 0), jnp.moveaxis(dtx, 1, 0), jnp.moveaxis(B, 1, 0), jnp.moveaxis(C, 1, 0))
            _, y = jax.lax.scan(step, h0, inputs)
            y = jnp.moveaxis(y, 0, 1) + x * D[None, None, :, None]
            y = y.reshape(b, L, D_SSM)
            g = y * jax.nn.silu(z)
            g = g * jax.lax.rsqrt(jnp.mean(g * g, axis=-1, keepdims=True) + EPS) * norm_w
            return jnp.einsum('ble,de->bld', g, W_out)
        return _mamba2_forward(u, W_in, conv_w, conv_b, dt_bias, A_log, D, norm_w, W_out)

    def _L0_ffn_ref(x, scale, gate_w, gate_b, mlp1_w, mlp1_b, mlp2_w, mlp2_b):
        import jax, jax.numpy as jnp
        import numpy as np
        ALPHA = 1.702
        LIMIT = 7.0
        EPS = 1e-05
        E = 16
        K = 4

        def _swiglu(h):
            x_glu = jnp.minimum(h[..., ::2], LIMIT)
            x_lin = jnp.clip(h[..., 1::2], LIMIT, LIMIT)
            return x_glu * jax.nn.sigmoid(ALPHA * x_glu) * (x_lin + 1.0)
        t = x * jax.lax.rsqrt(jnp.mean(x * x, axis=-1, keepdims=True) + EPS) * scale
        g = jnp.einsum('bth,eh->bte', t, gate_w) + gate_b
        vals, idx = jax.lax.top_k(g, K)
        w = jax.nn.softmax(vals, axis=-1)
        route = jnp.sum(jax.nn.one_hot(idx, E, dtype=t.dtype) * w[..., None], axis=-2)
        route_e = jnp.moveaxis(route, -1, 0)

        def step(acc, p):
            w1, b1, w2, b2, r = p
            h = jnp.einsum('bth,ih->bti', t, w1) + b1
            s = _swiglu(h)
            y = jnp.einsum('bti,hi->bth', s, w2) + b2
            return (acc + r[..., None] * y, None)
        acc, _ = jax.lax.scan(step, jnp.zeros_like(x), (mlp1_w, mlp1_b, mlp2_w, mlp2_b, route_e))
        return x + acc
    x = L0_attn_a_x
    x = x + _L0_attn_a_ref(_layernorm(x, axis=-1), L0_attn_a_w_qkv, L0_attn_a_w_proj, L0_attn_a_b_proj)
    x = x + _L0_ffn_ref(_layernorm(x, axis=-1), L0_ffn_scale, L0_ffn_gate_w, L0_ffn_gate_b, L0_ffn_mlp1_w, L0_ffn_mlp1_b, L0_ffn_mlp2_w, L0_ffn_mlp2_b)
    x = x + _L0_attn_b_ref(_layernorm(x, axis=-1), L0_attn_b_W_in, L0_attn_b_conv_w, L0_attn_b_conv_b, L0_attn_b_dt_bias, L0_attn_b_A_log, L0_attn_b_D, L0_attn_b_norm_w, L0_attn_b_W_out)
    x = x + _L0_ffn_ref(_layernorm(x, axis=-1), L0_ffn_scale, L0_ffn_gate_w, L0_ffn_gate_b, L0_ffn_mlp1_w, L0_ffn_mlp1_b, L0_ffn_mlp2_w, L0_ffn_mlp2_b)
    return x

_drawn_inputs = setup_inputs


def setup_inputs(seed=0):
    import zlib

    import numpy as np

    out = dict(_drawn_inputs(seed))
    spreads = {'L0_attn_b_conv_b': (0.0, 0.1),
     'L0_attn_b_D': (1.0, 0.2),
     'L0_attn_b_norm_w': (1.0, 0.557),
     'L0_ffn_scale': (1.0, 0.2),
     'L0_ffn_gate_b': (0.0, 0.1)}
    factors = {'L0_attn_a_w_qkv': 8.0,
     'L0_attn_a_w_proj': 8.0,
     'L0_attn_b_dt_bias': 8.0,
     'L0_attn_b_A_log': 8.0,
     'L0_ffn_mlp1_b': 7.119,
     'L0_ffn_mlp2_b': 6.336}
    for name, (base, spread) in spreads.items():
        noise = np.random.default_rng([zlib.crc32(name.encode()), seed]).standard_normal(out[name].shape)
        drawn = base * np.exp(spread * noise) if base else spread * noise
        out[name] = jnp.asarray(drawn.astype(out[name].dtype))
    for name, factor in factors.items():
        out[name] = (out[name] * factor).astype(out[name].dtype)
    return out
```

```python
from contextlib import ExitStack

import numpy as np
import concourse.bass as bass
from concourse import mybir

F32 = mybir.dt.float32
F32R = mybir.dt.float32r
BF16 = mybir.dt.bfloat16
ALU = mybir.AluOpType
ACT = mybir.ActivationFunctionType
AX = mybir.AxisListType

P = 128
NB = 8
SEQ = 512
NT = SEQ // P
D = 128
NE = 16
TOPK = 4
I = 128
HEAD = 8
LN_EPS = 1e-5
ALPHA = 1.702
LIMIT = 7.0
CONV_W = 4
NH = 4
HD = 64
DI = NH * HD
NJ = 4
PARTS = 3
PSTEP = 32
LOWEST = -3.0e38
PE_TILES = (0, 1)
DVE_TILES = (2, 3)


def build(nc, x, w_qkv, w_proj, b_proj, W_in, conv_w, conv_b, dt_bias, A_log, Dskip, norm_w, W_out,
          ffn_scale, gate_w, gate_b, mlp1_w, mlp1_b, mlp2_w, mlp2_b, out):
    with ExitStack() as ctx:
        def sb(name, shape, dt=F32):
            return ctx.enter_context(nc.sbuf_tensor(name, shape, dt))

        def sem(name):
            return ctx.enter_context(nc.semaphore(name))

        X = sb("X", [P, NB, NT, D])
        ffn_hi = sb("ffn_hi", [P, NB, SEQ], F32R)
        ffn_lo = sb("ffn_lo", [P, NB, SEQ], F32R)
        route = sb("route", [PARTS * PSTEP, NB, SEQ], BF16)
        ident = sb("ident", [P, P])
        ident_b = sb("ident_b", [P, P], BF16)
        ones = sb("ones", [P, P])
        zeros = sb("zeros", [P, P])
        upto = sb("upto", [P, P])
        after = sb("after", [P, P])
        pick = sb("pick", [PARTS * PSTEP, NE, P], BF16)
        eps4 = sb("eps4", [P, NT])
        mhalf4 = sb("mhalf4", [P, NT])
        limit_col = sb("limit_col", [P, 1])
        top_col = sb("top_col", [P, 1])
        qkv_rows = sb("qkv_rows", [P, 3, D])
        proj_rows = sb("proj_rows", [P, D])
        gate_rows = sb("gate_rows", [NE, D])
        vec_row = sb("vec_row", [1, 160])
        scale_col = sb("scale_col", [P, 1])
        w1_rows = sb("w1_rows", [P, NE, D])
        w2_rows = sb("w2_rows", [P, NE, I])
        b1_rows = sb("b1_rows", [NE, 2 * I])
        b2_rows = sb("b2_rows", [PARTS * PSTEP, D])
        a_qk = sb("a_qk", [P, D])
        vpg = sb("vpg", [P, 2 * D + NE])
        wvT, wpT, gateT = vpg[:, 0:D], vpg[:, D:2 * D], vpg[:, 2 * D:]
        vecs = sb("vecs", [P, 160])
        w1_hi = sb("w1_hi", [P, NE, I], F32R)
        w1_lo = sb("w1_lo", [P, NE, I], F32R)
        w2_hi = sb("w2_hi", [P, NE, D], F32R)
        w2_lo = sb("w2_lo", [P, NE, D], F32R)
        b1T = sb("b1T", [P, NE])
        b2_parts = sb("b2_parts", [PARTS * PSTEP, PARTS, D], BF16)
        b2_rest = sb("b2_rest", [PARTS * PSTEP, 2, D])
        ln1_st = sb("ln1_st", [P, NT, 6])
        ln1_mv = sb("ln1_mv", [P, NT, 2])
        ln1_ve = sb("ln1_ve", [P, NT])
        ln1_rs = sb("ln1_rs", [P, NT])
        xn = sb("xn", [P, NT, D])
        xnT = sb("xnT", [P, SEQ])
        rt_st = sb("rt_st", [P, NT, 6])
        rt_mv = sb("rt_mv", [P, NT, 2])
        rt_small = sb("rt_small", [P, 8, NT])
        n2 = sb("n2", [P, NT, D])
        t0 = sb("t0", [P, NT, D])
        tT = sb("tT", [P, SEQ])
        logits = sb("logits", [P, NT, NE + TOPK])
        replaced = sb("replaced", [P, NT, NE + TOPK])
        top8 = sb("top8", [P, NT, 8])
        rt_tmp = sb("rt_tmp", [P, 6, NT, NE])
        rt_sum = sb("rt_sum", [P, 2, NT])
        rt_parts = sb("rt_parts", [P, NT, PARTS, PSTEP], BF16)
        in_rows = sb("in_rows", [P, 6, D])
        dt_rows = sb("dt_rows", [NH, D])
        out_rows = sb("out_rows", [P, DI])
        conv_taps = sb("conv_taps", [P, NJ, CONV_W])
        col_rows = sb("col_rows", [NJ + 2, P])
        cols = sb("cols", [P, NJ + 2])
        conv_bias, norm_col = cols[:, 0:NJ], cols[:, NJ:]
        tapT = sb("tapT", [P, len(PE_TILES), CONV_W, P])
        bcT = sb("bcT", [P, len(DVE_TILES), P])
        zT = sb("zT", [P, DI])
        dtT = sb("dtT", [P, NH])
        outT = sb("outT", [P, 2, D])
        skip_diag = sb("skip_diag", [P, 2, P])
        neg_A = sb("neg_A", [P, NH])

        with ExitStack() as stage:
            def own(name, shape, dt=F32):
                return stage.enter_context(nc.sbuf_tensor(name, shape, dt))

            qT = own("qT", [P, SEQ])
            v = own("v", [P, NT, D])
            probs = own("probs", [P, NT, SEQ])
            probsT = own("probsT", [P, NT, NT, P])
            attn = own("attn", [P, NT, D])
            neg_max = own("neg_max", [P, NT])
            row_sum = own("row_sum", [P, NT])
            row_rec = own("row_rec", [P, NT])
        with ExitStack() as stage:
            NR = 4
            act_ring = own("act_ring", [P, 2, SEQ])
            s_ring = own("s_ring", [P, 2, SEQ])
            s_hi = own("s_hi", [P, NR, SEQ], F32R)
            s_lo = own("s_lo", [P, NR, SEQ], F32R)
            acc_sb = own("acc_sb", [P, SEQ])
        with ExitStack() as stage:
            tap_rows = own("tap_rows", [P, len(PE_TILES), CONV_W, D])
            conv_acc = own("conv_acc", [P, len(DVE_TILES), SEQ])
            xs = own("xs", [P, NJ, SEQ])
            zs = own("zs", [P, NT, DI])
            dt_tmp = own("dt_tmp", [P, 7, NT * NH])
            dt_a = own("dt_a", [P, 2, NT, NH])
            decay = own("decay", [P, 2, NT, NH])
            ramp = own("ramp", [P, 2, NH, P])
            segs = own("segs", [P, 2, NH, P])
            cb = own("cb", [P, 2, P])
            gram = own("gram", [P, 2, NH, P])
            xb_tok = own("xb_tok", [P, 2, 3, P])
            to_end = own("to_end", [P, 2, NH])
            xw = own("xw", [P, 2, DI])
            state = own("state", [P, 2, DI])
            state_d = own("state_d", [P, DI])
            y_off = own("y_off", [P, DI])
            y = own("y", [P, 2, DI])
            g = own("g", [P, 2, DI])
            g_sq = own("g_sq", [P, DI])
            g_ss = own("g_ss", [P, NT])
            g_rs = own("g_rs", [P, 2, NT])
            gn = own("gn", [P, 2, DI])
            gT = own("gT", [P, 2, SEQ])

        ps = ctx.enter_context(nc.psum_tensor("ps", [P, 8, 512], F32))

        def bank(i):
            return ps[:, i, :]

        x_first = sem("x_first")
        x_rest = sem("x_rest")
        w_attn = sem("w_attn")
        w_ffn = sem("w_ffn")
        consts = sem("consts")
        prep_ps = sem("prep_ps")
        prep_sb = sem("prep_sb")
        prep2_ps = sem("prep2_ps")
        prep2_sb = sem("prep2_sb")
        prep2_hi = sem("prep2_hi")
        b2_split = sem("b2_split")
        stored = sem("stored")
        gate_pool = sem("gate_pool")
        gate_dve = sem("gate_dve")
        gate_act = sem("gate_act")
        N_CONST = 17

        VB, VG, VDT, VA, VD = 0, D, D + NE, D + NE + NH, D + NE + 2 * NH
        VEND = VD + NH
        b_proj_all = vecs[:, VB:VB + D]
        gate_b_all = vecs[:, VG:VG + NE]

        S1 = {n: sem("attn_" + n) for n in (
            "stats", "aggr", "rstd", "xn", "xnT_ps", "xnT", "q_ps", "q", "v_ps", "v", "scores", "max", "probs",
            "pT_ps", "pT", "o_ps", "rec", "o", "y_ps", "xb", "x1")}

        def router_sems(tag):
            return {n: sem(tag + n) for n in (
                "stats", "aggr", "pool", "n2", "t0", "xn", "t_ps", "t", "t_hi", "stash", "lg_ps", "lg", "max", "cut", "shift",
                "rep", "mask", "exp", "em", "weights", "lo", "rt_ps", "route")}

        R1 = router_sems("router1_")

        def ffn_sems(tag):
            return {n: sem(tag + n) for n in ("h", "rb", "act", "s", "hi", "lo", "out", "acc_sb", "back", "x")}

        F1 = ffn_sems("ffn1_")

        R2 = router_sems("router2_")
        F2 = ffn_sems("ffn2_")
        M = {n: sem("ssm_" + n) for n in (
            "stats", "aggr", "rstd", "xn", "uT_ps", "uT", "cv_ps", "tap", "conv", "xs", "z_ps", "zs", "dt_ps", "dt_x",
            "dt_m", "dt_u", "log", "dt", "a", "dk_ps", "decay", "ramp", "cb_ps", "cb", "xb_ps", "xb", "seg_ps", "segs",
            "gram", "end", "xw", "st_ps", "state_d", "state", "y_ps", "y_off", "y", "g", "sq", "rms", "gn", "gT_ps",
            "gT", "o_ps", "x")}
        w_ssm = sem("w_ssm")
        taps_ready = sem("taps_ready")
        prep3_ps = sem("prep3_ps")
        prep3_sb = sem("prep3_sb")

        block = ctx.enter_context(nc.Block())

        PREP3 = 9
        PH = len(PE_TILES)

        def wait(eng, s, value):
            if isinstance(value, int) and value <= 0:
                return
            eng.wait_ge(s, value)

        def skew(eng, step, count=NB):
            step(-1, True, False, False)
            step(0, True, True, False)
            step(1, True, True, True)
            with eng.Fori(2, count - 1) as i:
                step(i, True, True, True)
            step(count - 1, False, True, True)
            step(count, False, False, True)

        def least(a, cap):
            return min(a, cap) if isinstance(a, int) else a

        @block.sync
        def _(eng):
            eng.dma_start(X[:, 0, :, :], x[0].rearrange("(p r) d -> p r d", r=NT)).then_inc(x_first, 16)
            eng.dma_start(qkv_rows[:, :, :], w_qkv.rearrange("(m p) d -> p m d", p=P)).then_inc(w_attn, 16)
            eng.dma_start(proj_rows[:, :], w_proj).then_inc(w_attn, 16)
            eng.dma_start(gate_rows[:, :], gate_w).then_inc(w_attn, 16)
            for at, src in ((VB, b_proj), (VG, gate_b), (VDT, dt_bias), (VA, A_log), (VD, Dskip)):
                eng.dma_start(vec_row[0:1, at:at + src.shape[0]], src.rearrange("(a n) -> a n", a=1)).then_inc(w_attn, 16)
            eng.dma_start(scale_col[:, :], ffn_scale.rearrange("(p a) -> p a", a=1)).then_inc(w_attn, 16)
            eng.dma_start(X[:, 1:NB, :, :], x[1:NB].rearrange("b (p r) d -> p b r d", r=NT)).then_inc(x_rest, 16)
            eng.dma_start(w1_rows[:, :, :], mlp1_w.rearrange("e (i two) d -> i two e d", two=2)[:, 0]).then_inc(w_ffn, 16)
            eng.dma_start(w2_rows[:, :, :], mlp2_w.rearrange("e h i -> h e i")).then_inc(w_ffn, 16)
            eng.dma_start(b1_rows[:, :], mlp1_b).then_inc(w_ffn, 16)
            eng.dma_start(in_rows[:, :, :], W_in[0:6 * P].rearrange("(m p) d -> p m d", p=P)).then_inc(w_ssm, 16)
            eng.dma_start(dt_rows[:, :], W_in[6 * P:]).then_inc(w_ssm, 16)
            eng.dma_start(out_rows[:, :], W_out).then_inc(w_ssm, 16)
            eng.dma_start(conv_taps[:, :, :], conv_w.rearrange("(j p) w -> p j w", p=P)).then_inc(w_ssm, 16)
            eng.dma_start(col_rows[0:NJ, :], conv_b.rearrange("(j p) -> j p", p=P)).then_inc(w_ssm, 16)
            eng.dma_start(col_rows[NJ:NJ + 2, :], norm_w.rearrange("(j p) -> j p", p=P)).then_inc(w_ssm, 16)
            eng.wait_ge(consts, N_CONST)
            for g in range(PARTS):
                eng.dma_start(b2_rows[g * PSTEP:g * PSTEP + NE, :], mlp2_b).then_inc(w_ffn, 16)
            with eng.Fori(0, NB) as b:
                eng.wait_ge(F2["x"], b + 1)
                eng.dma_start(out[b].rearrange("(p r) d -> p r d", r=NT), X[:, b, :, :]).then_inc(stored, 16)
            eng.wait_ge(stored, 16 * NB)

        @block.gpsimd
        def _(eng):
            c = [0]

            def const(ins):
                ins.then_inc(consts, 1)
                c[0] += 1

            const(eng.memset(ident[:, :], 0.0))
            const(eng.memset(ident_b[:, :], 0.0))
            const(eng.memset(ones[:, :], 1.0))
            const(eng.memset(zeros[:, :], 0.0))
            const(eng.memset(pick[:, :, :], 0.0))
            const(eng.memset(eps4[:, :], LN_EPS))
            const(eng.memset(mhalf4[:, :], -0.5))
            const(eng.memset(limit_col[:, :], LIMIT))
            const(eng.memset(logits[:, :, NE:], LOWEST))
            const(eng.memset(rt_parts[:, :, :, :], 0.0))
            const(eng.memset(b2_rows[:, :], 0.0))
            eng.wait_ge(consts, c[0])
            for m in (ident, ident_b):
                const(eng.affine_select(out=m[:, :], in_=m[:, :], compare_op=ALU.not_equal, fill=1.0, base=0,
                                        pattern=[[-1, P]], channel_multiplier=1))
            const(eng.affine_select(out=upto[:, :], in_=ones[:, :], compare_op=ALU.is_ge, fill=0.0, base=0,
                                    pattern=[[1, P]], channel_multiplier=-1))
            const(eng.affine_select(out=after[:, :], in_=ones[:, :], compare_op=ALU.is_gt, fill=0.0, base=0,
                                    pattern=[[-1, P]], channel_multiplier=1))
            for part in range(PARTS):
                eng.wait_ge(consts, c[0])
                ins = eng.affine_select(out=pick[:, :, :], in_=pick[:, :, :], compare_op=ALU.not_equal, fill=1.0,
                                        base=-part * PSTEP, pattern=[[-1, NE], [0, P]], channel_multiplier=1)
                if part < PARTS - 1:
                    const(ins)
            ins.then_inc(consts, 1)
            assert c[0] + 1 == N_CONST + 1 or True

            def router_chain(R, b):
                n = [0]

                def tt(o, a, bb, op):
                    eng.tensor_tensor(o, a, bb, op).then_inc(R["pool"], 1)
                    n[0] += 1
                    wait(eng, R["pool"], 7 * b + n[0])

                var = rt_mv[:, :, 1]
                wait(eng, R["aggr"], NT * b + NT)
                wait(eng, R["t0"], NT * b)
                tt(rt_small[:, 0, :], var, eps4[:, :], ALU.add)
                tt(rt_small[:, 1, :], rt_small[:, 0, :], mhalf4[:, :], ALU.pow)
                tt(rt_small[:, 2, :], rt_small[:, 1, :], rt_small[:, 1, :], ALU.mult)
                tt(rt_small[:, 3, :], rt_small[:, 2, :], var, ALU.mult)
                tt(rt_small[:, 4, :], rt_small[:, 3, :], eps4[:, :], ALU.add)
                tt(rt_small[:, 5, :], rt_small[:, 4, :], mhalf4[:, :], ALU.pow)
                eng.tensor_tensor(rt_small[:, 6, :], rt_small[:, 5, :], rt_small[:, 1, :],
                                  ALU.mult).then_inc(R["pool"], 1)

            def router_stash(R, b):
                eng.wait_ge(R["t"], b + 1).then_inc(gate_pool, 1)
                eng.wait_ge(R["t_hi"], b + 1).then_inc(gate_pool, 1)
                eng.tensor_tensor(ffn_lo[:, b, :], tT[:, :], ffn_hi[:, b, :].bitcast(F32),
                                  ALU.subtract).then_inc(R["stash"], 1)

            def ln1_chain(b):
                wait(eng, S1["aggr"], NT * b + NT)
                wait(eng, S1["xn"], NT * b)
                eng.tensor_tensor(ln1_ve[:, :], ln1_mv[:, :, 1], eps4[:, :], ALU.add).then_inc(S1["rstd"], 1)
                wait(eng, S1["rstd"], 2 * b + 1)
                eng.tensor_tensor(ln1_rs[:, :], ln1_ve[:, :], mhalf4[:, :], ALU.pow).then_inc(S1["rstd"], 1)

            def add_bias(b):
                eng.wait_ge(S1["xn"], NT * b + NT).then_inc(gate_pool, 1)
                eng.tensor_tensor(X[:, b, :, :], X[:, b, :, :],
                                  b_proj_all.unsqueeze(1).to_broadcast([P, NT, D]), ALU.add).then_inc(S1["xb"], 1)

            eng.wait_ge(consts, N_CONST)
            eng.wait_ge(prep_sb, 3)

            def step(i, first, second, third):
                if third:
                    router_chain(R1, i - 1)
                if first:
                    ln1_chain(i + 1)
                    add_bias(i + 1)
                if third:
                    router_stash(R1, i - 1)
            skew(eng, step)

            def ssm_norm(b):
                wait(eng, M["aggr"], NT * b + NT)
                wait(eng, M["xn"], NT * b)
                eng.tensor_tensor(ln1_ve[:, :], ln1_mv[:, :, 1], eps4[:, :], ALU.add).then_inc(M["rstd"], 1)
                wait(eng, M["rstd"], 2 * b + 1)
                eng.tensor_tensor(ln1_rs[:, :], ln1_ve[:, :], mhalf4[:, :], ALU.pow).then_inc(M["rstd"], 1)

            def ramps(b, c):
                n = NT * b + c
                wait(eng, M["seg_ps"], n - 1)
                wait(eng, M["a"], b + 1)
                eng.tensor_tensor(ramp[:, c % 2, :, :], upto[:, :].unsqueeze(1).to_broadcast([P, NH, P]),
                                  dt_a[:, 1, c, :].unsqueeze(2).to_broadcast([P, NH, P]),
                                  ALU.mult).then_inc(M["ramp"], 1)

            def weigh(b, c):
                n = NT * b + c
                if c < NT - 1:
                    k = (NT - 1) * b + c
                    wait(eng, M["xb"], n + 1)
                    wait(eng, M["st_ps"], k - 1)
                    wait(eng, M["end"], n + 1)
                    eng.tensor_tensor(xw[:, c % 2, :].rearrange("s (h p) -> s h p", h=NH),
                                      xb_tok[:, c % 2, 0:2, :].rearrange("s j (h p) -> s (j h) p", p=HD),
                                      to_end[:, c % 2, :].unsqueeze(2).to_broadcast([P, NH, HD]),
                                      ALU.mult).then_inc(M["xw"], 1)
                if 0 < c < NT - 1:
                    wait(eng, M["state"], (NT - 1) * b + c)
                    eng.tensor_tensor(state_d[:, :].rearrange("n (h p) -> n h p", h=NH),
                                      state[:, (c - 1) % 2, :].rearrange("n (h p) -> n h p", h=NH),
                                      decay[:, 1, c, :].unsqueeze(2).to_broadcast([P, NH, HD]),
                                      ALU.mult).then_inc(M["state_d"], 1)

            def gate(b, c):
                n = NT * b + c
                wait(eng, M["y"], n + 1)
                wait(eng, M["gn"], n - 1)
                wait(eng, M["zs"], 2 * b + c // 2 + 1)
                eng.tensor_tensor(g[:, c % 2, :], y[:, c % 2, :], zs[:, c, :], ALU.mult).then_inc(M["g"], 1)

            def rms(b, c):
                n = NT * b + c
                wait(eng, M["sq"], n + 1)
                eng.tensor_tensor(g_rs[:, 0, c:c + 1], g_ss[:, c:c + 1], eps4[:, 0:1], ALU.add).then_inc(M["rms"], 1)
                wait(eng, M["rms"], 2 * n + 1)
                eng.tensor_tensor(g_rs[:, 1, c:c + 1], g_rs[:, 0, c:c + 1], mhalf4[:, 0:1], ALU.pow).then_inc(M["rms"], 1)

            eng.wait_ge(prep3_sb, PREP3)

            def step(i, first, second, third):
                if third:
                    router_chain(R2, i - 1)
                if third:
                    router_stash(R2, i - 1)
                if second:
                    ramps(i, 0)
                    ramps(i, 1)
                    for c in range(NT):
                        weigh(i, c)
                        if c + 2 < NT:
                            ramps(i, c + 2)
                        gate(i, c)
                        rms(i, c)
                if first:
                    ssm_norm(i + 1)
            skew(eng, step)

        @block.scalar
        def _(eng):
            eng.wait_ge(prep_ps, 1)
            eng.activation(a_qk[:, :], bank(0)[:, 0:D], ACT.Copy, scale=float(HEAD) ** -0.5).then_inc(prep_sb, 1)
            eng.wait_ge(prep_ps, 2)
            eng.activation(vpg[:, :], bank(1)[:, 0:2 * D + NE], ACT.Copy).then_inc(prep_sb, 1)
            eng.wait_ge(prep_ps, 3)
            eng.activation(vecs[:, 0:VEND], bank(2)[:, 0:VEND], ACT.Copy).then_inc(prep_sb, 1)

            def exps(b):
                for r in range(NT):
                    wait(eng, S1["max"], NT * b + r + 1)
                    if r == 0:
                        wait(eng, S1["rec"], b)
                    wait(eng, S1["pT_ps"], NT * (b - 1) + r + 1)
                    eng.activation(probs[:, r, :], bank(r), ACT.Exp, bias=neg_max[:, r:r + 1],
                                   accum_out=row_sum[:, r:r + 1]).then_inc(S1["probs"], 1)

            def pT(b):
                for r in range(NT):
                    wait(eng, S1["pT_ps"], NT * b + r + 1)
                    wait(eng, S1["o_ps"], b)
                    eng.activation(probsT[:, r, :, :], bank(r).rearrange("k (t q) -> k t q", t=NT),
                                   ACT.Copy).then_inc(S1["pT"], 1)

            def xnT_out(b):
                wait(eng, S1["xnT_ps"], b + 1)
                wait(eng, S1["v_ps"], b)
                wait(eng, S1["scores"], NT * b)
                eng.activation(xnT[:, :].rearrange("d (p r) -> d r p", r=NT),
                               bank(4).rearrange("d (r p) -> d r p", r=NT), ACT.Copy).then_inc(S1["xnT"], 1)

            def v_out(b):
                wait(eng, S1["v_ps"], b + 1)
                wait(eng, S1["o_ps"], b)
                eng.activation(v[:, :, :], bank(6).rearrange("k (t h) -> k t h", t=NT), ACT.Copy).then_inc(S1["v"], 1)

            def router_t(R, b):
                wait(eng, R["t_ps"], b + 1)
                wait(eng, R["lg_ps"], b)
                wait(eng, R["stash"], b)
                eng.activation(tT[:, :], bank(6), ACT.Copy, scale=scale_col[:, 0:1]).then_inc(R["t"], 1)
                eng.wait_ge(R["t"], b + 1).then_inc(gate_act, 1)
                eng.activation(ffn_hi[:, b, :], tT[:, :], ACT.Copy).then_inc(R["t_hi"], 1)

            def router_exp(R, b):
                wait(eng, R["shift"], b + 1)
                wait(eng, R["em"], b)
                eng.activation(rt_tmp[:, 1, :, :], rt_tmp[:, 0, :, :], ACT.Exp).then_inc(R["exp"], 1)

            def router_out(R, b, at):
                eng.wait_ge(R["rt_ps"], b + 1).then_inc(gate_act, 1)
                eng.activation(route[:, b, :], bank(at).bitcast(BF16)[0:PARTS * PSTEP, 0:SEQ],
                               ACT.Copy).then_inc(R["route"], 1)

            def step(i, first, second, third):
                if second:
                    exps(i)
                if third:
                    router_t(R1, i - 1)
                if second:
                    pT(i)
                if first:
                    xnT_out(i + 1)
                if third:
                    router_exp(R1, i - 1)
                if first:
                    v_out(i + 1)
                if third:
                    router_out(R1, i - 1, 4)
            skew(eng, step)

            for quad in range(NE // 4):
                eng.wait_ge(prep2_ps, quad + 1)
                eng.activation(w1_hi[:, 4 * quad:4 * quad + 4, :], bank(quad).rearrange("d (e i) -> d e i", e=4),
                               ACT.Copy).then_inc(prep2_hi, 1)
            for quad in range(NE // 4):
                eng.wait_ge(prep2_ps, 4 + quad + 1)
                eng.activation(w2_hi[:, 4 * quad:4 * quad + 4, :], bank(quad).rearrange("i (e h) -> i e h", e=4),
                               ACT.Copy, scale=(LIMIT + 1.0) / ALPHA).then_inc(prep2_hi, 1)
            eng.wait_ge(prep2_ps, 9)
            eng.activation(b1T[:, :], bank(4)[:, 0:NE], ACT.Copy, scale=ALPHA).then_inc(prep2_sb, 1)
            eng.activation(top_col[:, :], limit_col[:, :], ACT.Silu, scale=ALPHA).then_inc(prep2_sb, 1)

            def split(F, b, e):
                wait(eng, F["s"], NE * b + e + 1)
                wait(eng, F["out"], NE * b + e + 1 - NR)
                wait(eng, F["lo"], NE * b + e + 1 - NR)
                eng.activation(s_hi[:, e % NR, :], s_ring[:, e % 2, :], ACT.Copy).then_inc(F["hi"], 1)

            def ffn(F, b, peeled, tail=False):
                for e in range(NE):
                    if not tail:
                        wait(eng, F["h"], NE * b + e + 1)
                        wait(eng, F["s"], NE * b + e + 1 - 2)
                        eng.activation(act_ring[:, e % 2, :], bank(e % 4), ACT.Silu, bias=b1T[:, e:e + 1],
                                       scale=ALPHA).then_inc(F["act"], 1)
                        if e:
                            split(F, b, e - 1)
                    if e == 0 and (tail or not peeled):
                        split(F, b - 1, NE - 1)
                    if e == 3 and (tail or not peeled):
                        wait(eng, F["out"], NE * b)
                        wait(eng, F["back"], b - 1)
                        eng.activation(acc_sb[:, :], bank(6), ACT.Copy).then_inc(F["acc_sb"], 1)

            eng.wait_ge(prep2_sb, 10)
            ffn(F1, 0, True)
            ffn(F1, 1, False)
            with eng.Fori(2, NB) as b:
                ffn(F1, b, False)
            ffn(F1, NB, False, True)
            for k in range(PH):
                eng.wait_ge(prep3_ps, k + 1)
                eng.activation(tapT[:, k, :, :], bank(k).rearrange("d (w c) -> d w c", w=CONV_W),
                               ACT.Copy).then_inc(prep3_sb, 1)
            eng.wait_ge(prep3_ps, PH + 1)
            eng.activation(bcT[:, :, :], bank(2)[:, 0:2 * P].rearrange("d (j c) -> d j c", j=2),
                           ACT.Copy).then_inc(prep3_sb, 1)
            eng.activation(zT[:, :], bank(2)[:, 2 * P:4 * P], ACT.Copy).then_inc(prep3_sb, 1)
            eng.wait_ge(prep3_ps, PH + 2)
            eng.activation(dtT[:, :], bank(3)[:, 0:NH], ACT.Copy).then_inc(prep3_sb, 1)
            eng.activation(cols[:, :], bank(3)[:, NH:NH + NJ + 2], ACT.Copy).then_inc(prep3_sb, 1)
            eng.wait_ge(prep3_sb, PH + 4)
            for j in range(2):
                eng.activation(outT[:, j, :], bank(3)[:, P * (j + 1):P * (j + 2)], ACT.Copy,
                               scale=norm_col[:, j:j + 1]).then_inc(prep3_sb, 1)
            eng.activation(neg_A[:, :], vecs[:, VA:VA + NH], ACT.Exp).then_inc(prep3_sb, 1)
            eng.wait_ge(prep3_sb, PREP3)

            def u_out(b):
                wait(eng, M["uT_ps"], b + 1)
                wait(eng, M["dt_ps"], b)
                wait(eng, M["z_ps"], 2 * b)
                eng.activation(xnT[:, :].rearrange("d (p r) -> d r p", r=NT),
                               bank(5).rearrange("d (r p) -> d r p", r=NT), ACT.Copy).then_inc(M["uT"], 1)

            def conv_first(b, k):
                j = DVE_TILES[k]
                wait(eng, M["cv_ps"], NJ * b + k + 1)
                wait(eng, M["xs"], NJ * (b - 1) + 3 + k)
                eng.activation(conv_acc[:, k, :], bank(6 + k), ACT.Identity, bias=conv_bias[:, j:j + 1],
                               scale=conv_taps[:, j, CONV_W - 1:CONV_W]).then_inc(M["tap"], 1)

            def conv_silu(b, k, j):
                wait(eng, M["y_ps"], NT * b)
                if k < len(DVE_TILES):
                    wait(eng, M["conv"], 6 * b + 3 * k + 3)
                    eng.activation(xs[:, j, :], conv_acc[:, k, :], ACT.Silu).then_inc(M["xs"], 1)
                else:
                    wait(eng, M["cv_ps"], NJ * b + k + 1)
                    eng.activation(xs[:, j, :], bank(6 + k % 2), ACT.Silu, bias=conv_bias[:, j:j + 1]).then_inc(M["xs"], 1)

            def z_silu(b, k):
                wait(eng, M["z_ps"], 2 * b + k + 1)
                wait(eng, M["g"], NT * (b - 1) + 2 * k + 2)
                eng.activation(zs[:, 2 * k:2 * k + 2, :], bank(6 + k).rearrange("t (c e) -> t c e", c=2),
                               ACT.Silu).then_inc(M["zs"], 1)

            def dt_exp(b):
                wait(eng, M["dt_m"], b + 1)
                eng.activation(dt_tmp[:, 2, :], dt_tmp[:, 1, :], ACT.Exp).then_inc(M["dt_u"], 1)

            def decays(b):
                wait(eng, M["dk_ps"], b + 1)
                wait(eng, M["y_off"], (NT - 1) * b)
                wait(eng, M["state_d"], (NT - 2) * b)
                eng.activation(decay[:, :, :, :], bank(5)[:, 0:2 * NT * NH].rearrange("p (k c h) -> p k c h", k=2, c=NT),
                               ACT.Exp).then_inc(M["decay"], 1)

            def xb_out(b, c):
                n = NT * b + c
                wait(eng, M["xb_ps"], n + 1)
                wait(eng, M["y_ps"], n - 1)
                wait(eng, M["st_ps"], (NT - 1) * b + min(c - 1, NT - 2) if c else (NT - 1) * b)
                wait(eng, M["xw"], (NT - 1) * b + min(c - 1, NT - 2) if c else (NT - 1) * b)
                eng.activation(xb_tok[:, c % 2, :, :], bank(1)[:, 0:3 * P].rearrange("t (j c) -> t j c", j=3),
                               ACT.Copy).then_inc(M["xb"], 1)

            def seg_exp(b, c):
                n = NT * b + c
                wait(eng, M["seg_ps"], n + 1)
                wait(eng, M["gram"], NH * (n - 1))
                wait(eng, M["end"], n - 1)
                eng.activation(segs[:, c % 2, :, :], bank(2).rearrange("s (h t) -> s h t", h=NH),
                               ACT.Exp).then_inc(M["segs"], 1)

            def square(b, c):
                n = NT * b + c
                wait(eng, M["g"], n + 1)
                wait(eng, M["sq"], n)
                eng.activation(g_sq[:, :], g[:, c % 2, :], ACT.Square, scale=float(DI) ** -0.5,
                               accum_out=g_ss[:, c:c + 1]).then_inc(M["sq"], 1)

            def gT_out(b, c):
                n = NT * b + c
                wait(eng, M["gT_ps"], n + 1)
                wait(eng, M["o_ps"], b)
                eng.activation(gT[:, :, c * P:(c + 1) * P], bank(5)[:, 0:2 * P].rearrange("e (j t) -> e j t", j=2),
                               ACT.Copy).then_inc(M["gT"], 1)

            def step(i, first, second, third):
                if second:
                    conv_first(i, 0)
                    conv_first(i, 1)
                    conv_silu(i, 2, PE_TILES[0])
                    conv_silu(i, 3, PE_TILES[1])
                    conv_silu(i, 0, DVE_TILES[0])
                    conv_silu(i, 1, DVE_TILES[1])
                    z_silu(i, 0)
                    z_silu(i, 1)
                if third:
                    router_t(R2, i - 1)
                if second:
                    dt_exp(i)
                if third:
                    router_exp(R2, i - 1)
                if second:
                    decays(i)
                    xb_out(i, 0)
                    seg_exp(i, 0)
                if third:
                    router_out(R2, i - 1, 5)
                if second:
                    for c in range(NT):
                        if c + 1 < NT:
                            xb_out(i, c + 1)
                            seg_exp(i, c + 1)
                        square(i, c)
                        if c:
                            gT_out(i, c - 1)
                    gT_out(i, NT - 1)
                if first:
                    u_out(i + 1)
            skew(eng, step)

            ffn(F2, 0, True)
            ffn(F2, 1, False)
            with eng.Fori(2, NB) as b:
                ffn(F2, b, False)
            ffn(F2, NB, False, True)

        @block.vector
        def _(eng):
            def ln1_stats(b):
                for r in range(NT):
                    eng.bn_stats(ln1_st[:, r, :], X[:, b, r, :]).then_inc(S1["stats"], 1)
                eng.wait_ge(S1["stats"], NT * b + NT).then_inc(gate_dve, 1)
                for r in range(NT):
                    eng.bn_aggr(ln1_mv[:, r, :], ln1_st[:, r, :]).then_inc(S1["aggr"], 1)

            def xn_out(b):
                wait(eng, S1["rstd"], 2 * b + 2)
                wait(eng, S1["xnT_ps"], b)
                for r in range(NT):
                    eng.tensor_scalar(xn[:, r, :], X[:, b, r, :], ln1_mv[:, r, 0:1], ln1_rs[:, r:r + 1],
                                      ALU.subtract, ALU.mult).then_inc(S1["xn"], 1)

            def q_out(b):
                wait(eng, S1["q_ps"], b + 1)
                wait(eng, S1["scores"], NT * b)
                eng.tensor_copy(qT[:, :], bank(5)).then_inc(S1["q"], 1)

            def maxes(b):
                for r in range(NT):
                    wait(eng, S1["scores"], NT * b + r + 1)
                    wait(eng, S1["probs"], NT * (b - 1) + r + 1)
                    eng.tensor_reduce(neg_max[:, r:r + 1], bank(r), AX.X, ALU.max, negate=True).then_inc(S1["max"], 1)

            def recip(b):
                wait(eng, S1["probs"], NT * b + NT)
                eng.reciprocal(row_rec[:, :], row_sum[:, :]).then_inc(S1["rec"], 1)

            def attn_out(b):
                wait(eng, S1["rec"], b + 1)
                wait(eng, S1["o_ps"], b + 1)
                wait(eng, S1["y_ps"], b)
                eng.tensor_tensor(attn[:, :, :], bank(7).rearrange("q (r h) -> q r h", r=NT),
                                  row_rec[:, :].unsqueeze(2).to_broadcast([P, NT, D]), ALU.mult).then_inc(S1["o"], 1)

            def x1_out(b):
                wait(eng, S1["xb"], b + 1)
                wait(eng, S1["y_ps"], b + 1)
                eng.tensor_tensor(X[:, b, :, :], bank(5).rearrange("p (r d) -> p r d", r=NT), X[:, b, :, :],
                                  ALU.add).then_inc(S1["x1"], 1)

            def router_stats(R, b, before):
                wait(eng, before, b + 1)
                for r in range(NT):
                    eng.bn_stats(rt_st[:, r, :], X[:, b, r, :]).then_inc(R["stats"], 1)
                eng.wait_ge(R["stats"], NT * b + NT).then_inc(gate_dve, 1)
                for r in range(NT):
                    eng.bn_aggr(rt_mv[:, r, :], rt_st[:, r, :]).then_inc(R["aggr"], 1)

            def router_norm(R, b):
                wait(eng, R["pool"], 7 * b + 7)
                for r in range(NT):
                    eng.tensor_scalar(n2[:, r, :], X[:, b, r, :], rt_mv[:, r, 0:1], rt_small[:, 1, r:r + 1],
                                      ALU.subtract, ALU.mult).then_inc(R["n2"], 1)
                wait(eng, R["t_ps"], b)
                for r in range(NT):
                    eng.tensor_scalar(t0[:, r, :], X[:, b, r, :], rt_mv[:, r, 0:1], rt_small[:, 6, r:r + 1],
                                      ALU.subtract, ALU.mult).then_inc(R["t0"], 1)

            def router_top(R, b):
                sh, ex, mk, em, rt, rest = (rt_tmp[:, k, :, :] for k in range(6))
                wait(eng, R["lg_ps"], b + 1)
                eng.tensor_tensor(logits[:, :, 0:NE], bank(7)[:, 0:NT * NE].rearrange("p (r e) -> p r e", r=NT),
                                  gate_b_all.unsqueeze(1).to_broadcast([P, NT, NE]), ALU.add).then_inc(R["lg"], 1)
                wait(eng, R["n2"], NT * b + NT)
                eng.tensor_tensor(X[:, b, :, :], X[:, b, :, :], n2[:, :, :], ALU.add).then_inc(R["xn"], 1)
                eng.wait_ge(R["lg"], b + 1).then_inc(gate_dve, 1)
                for r in range(NT):
                    eng.max(top8[:, r, :], logits[:, r, 0:NE]).then_inc(R["max"], 1)
                wait(eng, R["max"], NT * b + NT)
                eng.memset(top8[:, :, TOPK:], LOWEST).then_inc(R["cut"], 1)
                wait(eng, R["exp"], b)
                eng.tensor_tensor(sh, logits[:, :, 0:NE], top8[:, :, 0:1].to_broadcast([P, NT, NE]),
                                  ALU.subtract).then_inc(R["shift"], 1)
                eng.wait_ge(R["cut"], b + 1).then_inc(gate_dve, 1)
                for r in range(NT):
                    eng.match_replace(replaced[:, r, :], top8[:, r, :], logits[:, r, :], LOWEST).then_inc(R["rep"], 1)
                wait(eng, R["rep"], NT * b + NT)
                eng.tensor_tensor(mk, replaced[:, :, 0:NE], logits[:, :, 0:NE], ALU.not_equal).then_inc(R["mask"], 1)

            def router_weights(R, b):
                sh, ex, mk, em, rt, rest = (rt_tmp[:, k, :, :] for k in range(6))
                wait(eng, R["mask"], b + 1)
                wait(eng, R["exp"], b + 1)
                eng.tensor_tensor(em, ex, mk, ALU.mult).then_inc(R["em"], 1)
                wait(eng, R["em"], b + 1)
                n = [0]

                def link(ins):
                    ins.then_inc(R["weights"], 1)
                    n[0] += 1
                    wait(eng, R["weights"], 6 * b + n[0])

                link(eng.tensor_reduce(rt_sum[:, 0, :], em, AX.X, ALU.add))
                link(eng.reciprocal(rt_sum[:, 1, :], rt_sum[:, 0, :]))
                link(eng.tensor_tensor(rt, em, rt_sum[:, 1, :].unsqueeze(2).to_broadcast([P, NT, NE]), ALU.mult))
                hi, mid, lo = (rt_parts[:, :, g, 0:NE] for g in range(PARTS))
                wait(eng, R["rt_ps"], b)
                link(eng.tensor_copy(hi, rt))
                link(eng.tensor_tensor(rest, rt, hi, ALU.subtract))
                link(eng.tensor_copy(mid, rest))
                eng.tensor_tensor(lo, rest, mid, ALU.subtract).then_inc(R["lo"], 1)

            eng.wait_ge(prep_sb, 3)
            eng.wait_ge(consts, N_CONST)
            eng.wait_ge(x_first, 16)

            def step(i, first, second, third):
                if third:
                    router_stats(R1, i - 1, S1["x1"])
                if second:
                    maxes(i)
                if third:
                    router_norm(R1, i - 1)
                if first:
                    if isinstance(i, int) and i == 0:
                        eng.wait_ge(x_rest, 16)
                    ln1_stats(i + 1)
                if second:
                    recip(i)
                if first:
                    xn_out(i + 1)
                if third:
                    router_top(R1, i - 1)
                if second:
                    attn_out(i)
                if first:
                    q_out(i + 1)
                if third:
                    router_weights(R1, i - 1)
                if second:
                    x1_out(i)
            skew(eng, step)

            for quad in range(NE // 4):
                eng.wait_ge(prep2_hi, quad + 1)
                eng.tensor_tensor(w1_lo[:, 4 * quad:4 * quad + 4, :], bank(quad).rearrange("d (e i) -> d e i", e=4),
                                  w1_hi[:, 4 * quad:4 * quad + 4, :].bitcast(F32), ALU.subtract).then_inc(prep2_sb, 1)
            for quad in range(NE // 4):
                eng.wait_ge(prep2_hi, 4 + quad + 1)
                eng.scalar_tensor_tensor(out=w2_lo[:, 4 * quad:4 * quad + 4, :],
                                         in0=bank(quad).rearrange("i (e h) -> i e h", e=4), scalar=(LIMIT + 1.0) / ALPHA,
                                         in1=w2_hi[:, 4 * quad:4 * quad + 4, :].bitcast(F32), op0=ALU.mult,
                                         op1=ALU.subtract).then_inc(prep2_sb, 1)
            eng.wait_ge(w_ffn, 96)
            eng.tensor_copy(b2_parts[:, 0, :], b2_rows[:, :]).then_inc(b2_split, 1)
            eng.wait_ge(b2_split, 1)
            eng.tensor_tensor(b2_rest[:, 0, :], b2_rows[:, :], b2_parts[:, 0, :], ALU.subtract).then_inc(b2_split, 1)
            eng.wait_ge(b2_split, 2)
            eng.tensor_copy(b2_parts[:, 1, :], b2_rest[:, 0, :]).then_inc(b2_split, 1)
            eng.wait_ge(b2_split, 3)
            eng.tensor_tensor(b2_parts[:, 2, :], b2_rest[:, 0, :], b2_parts[:, 1, :], ALU.subtract).then_inc(b2_split, 1)

            def split(F, b, e):
                wait(eng, F["hi"], NE * b + e + 1)
                wait(eng, F["out"], NE * b + e + 1 - NR)
                eng.tensor_tensor(s_lo[:, e % NR, :], s_ring[:, e % 2, :], s_hi[:, e % NR, :].bitcast(F32),
                                  ALU.subtract).then_inc(F["lo"], 1)

            def ffn(F, b, peeled, tail=False):
                for e in range(NE):
                    if e == 9 and (tail or not peeled):
                        wait(eng, F["back"], b)
                        eng.tensor_tensor(X[:, b - 1, :, :], bank(7).rearrange("p (r d) -> p r d", r=NT),
                                          X[:, b - 1, :, :], ALU.add).then_inc(F["x"], 1)
                    if not tail:
                        wait(eng, F["lo"], NE * b + e + 1 - 2)
                        wait(eng, F["act"], NE * b + e + 1)
                        wait(eng, F["rb"], NE * b + e + 1)
                        eng.scalar_tensor_tensor(out=s_ring[:, e % 2, :], in0=act_ring[:, e % 2, :],
                                                 scalar=top_col[:, 0:1], in1=bank(4 + e % 2), op0=ALU.min,
                                                 op1=ALU.mult).then_inc(F["s"], 1)
                        if e:
                            split(F, b, e - 1)
                    if e == 0 and (tail or not peeled):
                        split(F, b - 1, NE - 1)

            eng.wait_ge(prep2_sb, 10)
            ffn(F1, 0, True)
            ffn(F1, 1, False)
            with eng.Fori(2, NB) as b:
                ffn(F1, b, False)
            ffn(F1, NB, False, True)
            eng.wait_ge(w_ssm, 96)
            for k, j in enumerate(PE_TILES):
                for w in range(CONV_W):
                    eng.tensor_scalar(tap_rows[:, k, w, :], in_rows[:, 2 + j, :], conv_taps[:, j, w:w + 1], None,
                                      ALU.mult).then_inc(taps_ready, 1)
            for j in range(2):
                eng.tensor_tensor(skip_diag[:, j, :].rearrange("c (h p) -> c h p", h=2),
                                  ident[:, :].rearrange("c (h p) -> c h p", h=2),
                                  vecs[:, VD + 2 * j:VD + 2 * j + 2].unsqueeze(2).to_broadcast([P, 2, HD]),
                                  ALU.mult).then_inc(taps_ready, 1)
            eng.wait_ge(prep3_sb, PREP3)
            eng.tensor_scalar(neg_A[:, :], neg_A[:, :], -1.0, None, ALU.mult).then_inc(taps_ready, 1)

            eng.wait_ge(F1["x"], NB)

            def ssm_stats(b):
                wait(eng, M["aggr"], NT * b)
                for r in range(NT):
                    eng.bn_stats(ln1_st[:, r, :], X[:, b, r, :]).then_inc(M["stats"], 1)
                eng.wait_ge(M["stats"], NT * b + NT).then_inc(gate_dve, 1)
                for r in range(NT):
                    eng.bn_aggr(ln1_mv[:, r, :], ln1_st[:, r, :]).then_inc(M["aggr"], 1)

            def ssm_xn(b):
                wait(eng, M["rstd"], 2 * b + 2)
                wait(eng, M["uT_ps"], b)
                for r in range(NT):
                    eng.tensor_scalar(xn[:, r, :], X[:, b, r, :], ln1_mv[:, r, 0:1], ln1_rs[:, r:r + 1],
                                      ALU.subtract, ALU.mult).then_inc(M["xn"], 1)

            def conv_taps_of(b, k):
                j = DVE_TILES[k]
                wait(eng, M["tap"], 2 * b + k + 1)
                for s in range(1, CONV_W):
                    eng.scalar_tensor_tensor(out=conv_acc[:, k, s:], in0=bank(6 + k)[:, 0:SEQ - s],
                                             scalar=conv_taps[:, j, CONV_W - 1 - s:CONV_W - s], in1=conv_acc[:, k, s:],
                                             op0=ALU.mult, op1=ALU.add).then_inc(M["conv"], 1)
                    if s < CONV_W - 1:
                        wait(eng, M["conv"], 6 * b + 3 * k + s)

            def dt_arg(b):
                wait(eng, M["dt_ps"], b + 1)
                eng.tensor_tensor(dt_tmp[:, 0, :].rearrange("p (c h) -> p c h", h=NH),
                                  bank(4)[:, 0:NT * NH].rearrange("p (c h) -> p c h", h=NH),
                                  vecs[:, VDT:VDT + NH].unsqueeze(1).to_broadcast([P, NT, NH]), ALU.add).then_inc(M["dt_x"], 1)
                wait(eng, M["dt_x"], b + 1)
                eng.scalar_tensor_tensor(out=dt_tmp[:, 1, :], in0=dt_tmp[:, 0, :], scalar=-1.0, in1=dt_tmp[:, 0, :],
                                         op0=ALU.mult, op1=ALU.min).then_inc(M["dt_m"], 1)

            def softplus(b):
                x_, m_, u_, w_, z_, z2, q_ = (dt_tmp[:, k, :] for k in range(7))
                n = [0]

                def link(ins):
                    ins.then_inc(M["log"], 1)
                    n[0] += 1
                    wait(eng, M["log"], 13 * b + n[0])

                wait(eng, M["dt_u"], b + 1)
                link(eng.tensor_scalar(w_, u_, 2.0, None, ALU.add))
                link(eng.reciprocal(w_, w_))
                link(eng.tensor_tensor(z_, u_, w_, ALU.mult))
                link(eng.tensor_tensor(z2, z_, z_, ALU.mult))
                link(eng.tensor_scalar(q_, z2, 1.0 / 15, None, ALU.mult))
                for k in (13, 11, 9, 7, 5, 3):
                    link(eng.scalar_tensor_tensor(out=q_, in0=q_, scalar=1.0 / k, in1=z2, op0=ALU.add, op1=ALU.mult))
                link(eng.scalar_tensor_tensor(out=q_, in0=q_, scalar=1.0, in1=z_, op0=ALU.add, op1=ALU.mult))
                link(eng.tensor_scalar(x_, x_, 0.0, None, ALU.max))
                wait(eng, M["gram"], NH * NT * b)
                eng.scalar_tensor_tensor(out=dt_a[:, 0, :, :].rearrange("p c h -> p (c h)"), in0=q_, scalar=2.0, in1=x_,
                                         op0=ALU.mult, op1=ALU.add).then_inc(M["dt"], 1)
                wait(eng, M["dt"], b + 1)
                eng.tensor_tensor(dt_a[:, 1, :, :], dt_a[:, 0, :, :],
                                  neg_A[:, :].unsqueeze(1).to_broadcast([P, NT, NH]), ALU.mult).then_inc(M["a"], 1)

            def grams(b, c):
                n = NT * b + c
                wait(eng, M["cb_ps"], n + 1)
                eng.tensor_tensor(cb[:, c % 2, :], bank(0)[:, 0:P], upto[:, :], ALU.mult).then_inc(M["cb"], 1)
                wait(eng, M["segs"], n + 1)
                wait(eng, M["xw"], (NT - 1) * b + min(c - 1, NT - 1) if c else (NT - 1) * b)
                eng.tensor_tensor(to_end[:, c % 2, :], segs[:, c % 2, :, P - 1], dt_a[:, 0, c, :], ALU.mult).then_inc(M["end"], 1)
                wait(eng, M["cb"], n + 1)
                wait(eng, M["y_ps"], n - 1)
                for h in range(NH):
                    eng.scalar_tensor_tensor(out=gram[:, c % 2, h, :], in0=segs[:, c % 2, h, :], scalar=dt_a[:, 0, c, h:h + 1],
                                             in1=cb[:, c % 2, :], op0=ALU.mult, op1=ALU.mult).then_inc(M["gram"], 1)

            def states(b, c):
                if c == NT - 1:
                    return
                k = (NT - 1) * b + c
                wait(eng, M["st_ps"], k + 1)
                if c == 0:
                    wait(eng, M["y_ps"], NT * b)
                    eng.tensor_copy(state[:, 0, :], bank(4)[:, 0:DI]).then_inc(M["state"], 1)
                else:
                    wait(eng, M["state_d"], (NT - 2) * b + c)
                    eng.tensor_tensor(state[:, c % 2, :], bank(4)[:, 0:DI], state_d[:, :], ALU.add).then_inc(M["state"], 1)

            def ys(b, c):
                n = NT * b + c
                wait(eng, M["y_ps"], n + 1)
                if c == 0:
                    wait(eng, M["g"], n - 1)
                    eng.tensor_copy(y[:, c % 2, :], bank(3)[:, 0:DI]).then_inc(M["y"], 1)
                    return
                k = (NT - 1) * b + c
                eng.tensor_tensor(y_off[:, :].rearrange("t (h p) -> t h p", h=NH),
                                  bank(3)[:, DI:2 * DI].rearrange("t (h p) -> t h p", h=NH),
                                  decay[:, 0, c, :].unsqueeze(2).to_broadcast([P, NH, HD]), ALU.mult).then_inc(M["y_off"], 1)
                wait(eng, M["y_off"], k)
                wait(eng, M["g"], n - 1)
                eng.tensor_tensor(y[:, c % 2, :], bank(3)[:, 0:DI], y_off[:, :], ALU.add).then_inc(M["y"], 1)

            def norms(b, c):
                n = NT * b + c
                wait(eng, M["rms"], 2 * n + 2)
                wait(eng, M["gT_ps"], n - 1)
                eng.tensor_scalar(gn[:, c % 2, :], g[:, c % 2, :], g_rs[:, 1, c:c + 1], None, ALU.mult).then_inc(M["gn"], 1)

            def x3_out(b):
                wait(eng, M["o_ps"], b + 1)
                eng.tensor_tensor(X[:, b, :, :], bank(4).rearrange("p (r d) -> p r d", r=NT), X[:, b, :, :],
                                  ALU.add).then_inc(M["x"], 1)

            def step(i, first, second, third):
                if third:
                    router_stats(R2, i - 1, M["x"])
                if second:
                    conv_taps_of(i, 0)
                    conv_taps_of(i, 1)
                if third:
                    router_norm(R2, i - 1)
                if second:
                    dt_arg(i)
                if third:
                    router_top(R2, i - 1)
                if second:
                    softplus(i)
                if third:
                    router_weights(R2, i - 1)
                if second:
                    for c in range(NT):
                        grams(i, c)
                        states(i, c)
                        if c:
                            norms(i, c - 1)
                        ys(i, c)
                if first:
                    ssm_stats(i + 1)
                if second:
                    norms(i, NT - 1)
                if first:
                    ssm_xn(i + 1)
                if second:
                    x3_out(i)
            skew(eng, step)

            ffn(F2, 0, True)
            ffn(F2, 1, False)
            with eng.Fori(2, NB) as b:
                ffn(F2, b, False)
            ffn(F2, NB, False, True)

        @block.tensor
        def _(eng):
            eng.wait_ge(consts, N_CONST + 1)
            eng.wait_ge(w_attn, 9 * 16)
            eng.matmul(bank(0)[:, 0:D], qkv_rows[:, 0, :], qkv_rows[:, 1, :], start=True, stop=True).then_inc(prep_ps, 1)
            eng.transpose(bank(1)[:, 0:D], qkv_rows[:, 2, :], ident[:, :])
            eng.transpose(bank(1)[:, D:2 * D], proj_rows[:, :], ident[:, :])
            eng.transpose(bank(1)[:, 2 * D:2 * D + NE], gate_rows[:, :], ident[0:NE, 0:NE]).then_inc(prep_ps, 1)
            eng.matmul(bank(2)[:, 0:VEND], ones[0:1, :], vec_row[0:1, 0:VEND], start=True, stop=True).then_inc(prep_ps, 1)
            eng.wait_ge(prep_sb, 3)

            def scores(b):
                wait(eng, S1["q"], b + 1)
                wait(eng, S1["pT"], NT * b)
                for r in range(NT):
                    eng.matmul(bank(r), qT[:, r * P:(r + 1) * P], xnT[:, :], start=True,
                               stop=True).then_inc(S1["scores"], 1)

            def xn_turn(b):
                wait(eng, S1["xn"], NT * b + NT)
                wait(eng, R1["route"], b - 2)
                for r in range(NT):
                    mm = eng.transpose(bank(4)[:, r * P:(r + 1) * P], xn[:, r, :], ident[:, :])
                mm.then_inc(S1["xnT_ps"], 1)

            def qv(b):
                wait(eng, S1["xnT"], b + 1)
                wait(eng, S1["x1"], b - 1)
                eng.matmul(bank(5), a_qk[:, :], xnT[:, :], start=True, stop=True).then_inc(S1["q_ps"], 1)
                wait(eng, R1["t"], b - 1)
                for t in range(NT):
                    mm = eng.matmul(bank(6)[:, t * D:(t + 1) * D], xnT[:, t * P:(t + 1) * P], wvT, start=True, stop=True)
                mm.then_inc(S1["v_ps"], 1)

            def p_turn(b):
                for r in range(NT):
                    wait(eng, S1["probs"], NT * b + r + 1)
                    for t in range(NT):
                        mm = eng.transpose(bank(r)[:, t * P:(t + 1) * P], probs[:, r, t * P:(t + 1) * P], ident[:, :])
                    mm.then_inc(S1["pT_ps"], 1)

            def pv(b):
                wait(eng, S1["v"], b + 1)
                wait(eng, R1["lg"], b)
                for r in range(NT):
                    wait(eng, S1["pT"], NT * b + r + 1)
                    for t in range(NT):
                        mm = eng.matmul(bank(7)[:, r * D:(r + 1) * D], probsT[:, r, t, :], v[:, t, :],
                                        start=(t == 0), stop=(t == NT - 1))
                mm.then_inc(S1["o_ps"], 1)

            def project(b):
                wait(eng, S1["o"], b + 1)
                wait(eng, S1["q"], least(b + 2, NB))
                for r in range(NT):
                    mm = eng.matmul(bank(5)[:, r * D:(r + 1) * D], attn[:, r, :], wpT, start=True, stop=True)
                mm.then_inc(S1["y_ps"], 1)

            def router_turn(R, b, bank_free):
                wait(eng, R["t0"], NT * b + NT)
                bank_free()
                for r in range(NT):
                    mm = eng.transpose(bank(6)[:, r * P:(r + 1) * P], t0[:, r, :], ident[:, :])
                mm.then_inc(R["t_ps"], 1)

            def router_logits(R, b, bank_free):
                wait(eng, R["t"], b + 1)
                bank_free()
                for r in range(NT):
                    mm = eng.matmul(bank(7)[:, r * NE:(r + 1) * NE], tT[:, r * P:(r + 1) * P], gateT, start=True, stop=True)
                mm.then_inc(R["lg_ps"], 1)

            def router_parts(R, b, at, bank_free):
                wait(eng, R["lo"], b + 1)
                bank_free()
                for r in range(NT):
                    mm = eng.transpose(bank(at).bitcast(BF16)[0:PARTS * PSTEP, r * P:(r + 1) * P],
                                       rt_parts[:, r, :, :].rearrange("p g e -> p (g e)"), ident_b[:, :])
                mm.then_inc(R["rt_ps"], 1)

            def step(i, first, second, third):
                if second:
                    scores(i)
                if third:
                    router_turn(R1, i - 1, lambda: wait(eng, S1["v"], least(i + 1, NB)))
                if second:
                    p_turn(i)
                if first:
                    xn_turn(i + 1)
                if third:
                    router_logits(R1, i - 1, lambda: wait(eng, S1["o"], i))
                if second:
                    pv(i)
                if first:
                    qv(i + 1)
                if second:
                    project(i)
                if third:
                    router_parts(R1, i - 1, 4, lambda: wait(eng, S1["xnT"], least(i + 2, NB)))
            skew(eng, step)

            eng.wait_ge(w_ffn, 96)
            eng.wait_ge(S1["pT"], NT * NB)
            for quad in range(NE // 4):
                for k in range(4):
                    mm = eng.transpose(bank(quad)[:, k * P:(k + 1) * P], w1_rows[:, 4 * quad + k, :], ident[:, :])
                mm.then_inc(prep2_ps, 1)
            for quad in range(NE // 4):
                eng.wait_ge(prep2_sb, quad + 1)
                for k in range(4):
                    mm = eng.transpose(bank(quad)[:, k * P:(k + 1) * P], w2_rows[:, 4 * quad + k, :], ident[:, :])
                mm.then_inc(prep2_ps, 1)
            eng.wait_ge(R1["route"], NB)
            eng.transpose(bank(4)[:, 0:NE], b1_rows[:, 0:2 * I:2], ident[0:NE, 0:NE]).then_inc(prep2_ps, 1)

            def ffn_out(F, b, e):
                wait(eng, F["lo"], NE * b + e + 1)
                if e == 0:
                    wait(eng, F["acc_sb"], b)
                    for g in range(PARTS):
                        eng.matmul(bank(6), b2_parts[:, g, :], route[:, b, :], start=(g == 0), stop=False)
                eng.matmul(bank(6), w2_hi[:, e, :], s_hi[:, e % NR, :], start=False, stop=False)
                eng.matmul(bank(6), w2_hi[:, e, :], s_lo[:, e % NR, :], start=False, stop=False)
                eng.matmul(bank(6), w2_lo[:, e, :], s_hi[:, e % NR, :], start=False, stop=(e == NE - 1)).then_inc(F["out"], 1)

            LAG = 3

            def ffn(F, b, peeled, tail=False):
                for e in range(NE):
                    if not tail:
                        wait(eng, F["act"], NE * b + e + 1 - 4)
                        eng.matmul(bank(e % 4), w1_hi[:, e, :], ffn_hi[:, b, :], start=True, stop=False)
                        eng.matmul(bank(e % 4), w1_hi[:, e, :], ffn_lo[:, b, :], start=False, stop=False)
                        eng.matmul(bank(e % 4), w1_lo[:, e, :], ffn_hi[:, b, :], start=False, stop=True).then_inc(F["h"], 1)
                        wait(eng, F["s"], NE * b + e + 1 - 2)
                        eng.matmul(bank(4 + e % 2), pick[:, e, :], route[:, b, :], start=True,
                                   stop=True).then_inc(F["rb"], 1)
                    if e >= LAG:
                        if not tail:
                            ffn_out(F, b, e - LAG)
                    elif tail or not peeled:
                        ffn_out(F, b - 1, NE - LAG + e)
                    if e == 6 and (tail or not peeled):
                        wait(eng, F["acc_sb"], b)
                        wait(eng, F["x"], b - 1)
                        for r in range(NT):
                            mm = eng.transpose(bank(7)[:, r * P:(r + 1) * P], acc_sb[:, r * P:(r + 1) * P], ident[:, :])
                        mm.then_inc(F["back"], 1)

            eng.wait_ge(prep2_sb, 10)
            eng.wait_ge(b2_split, 4)
            eng.wait_ge(R1["stash"], NB)
            ffn(F1, 0, True)
            ffn(F1, 1, False)
            with eng.Fori(2, NB) as b:
                ffn(F1, b, False)
            ffn(F1, NB, False, True)
            eng.wait_ge(taps_ready, PH * CONV_W)
            eng.wait_ge(F1["act"], NE * NB)
            eng.wait_ge(F1["s"], NE * NB)
            eng.wait_ge(F1["acc_sb"], NB)
            eng.wait_ge(F1["x"], NB)
            for k in range(PH):
                for w in range(CONV_W):
                    mm = eng.transpose(bank(k)[:, w * P:(w + 1) * P], tap_rows[:, k, w, :], ident[:, :])
                mm.then_inc(prep3_ps, 1)
            for k, j in enumerate((2 + DVE_TILES[0], 2 + DVE_TILES[1], 0, 1)):
                mm = eng.transpose(bank(2)[:, k * P:(k + 1) * P], in_rows[:, j, :], ident[:, :])
            mm.then_inc(prep3_ps, 1)
            eng.transpose(bank(3)[:, 0:NH], dt_rows[:, :], ident[0:NH, 0:NH])
            eng.transpose(bank(3)[:, NH:NH + NJ + 2], col_rows[:, :], ident[0:NJ + 2, 0:NJ + 2])
            for j in range(2):
                mm = eng.transpose(bank(3)[:, (j + 1) * P:(j + 2) * P], out_rows[:, j * P:(j + 1) * P], ident[:, :])
            mm.then_inc(prep3_ps, 1)
            eng.wait_ge(prep3_sb, PREP3)

            def u_turn(b):
                wait(eng, M["xn"], NT * b + NT)
                wait(eng, M["gT"], NT * b)
                for r in range(NT):
                    mm = eng.transpose(bank(5)[:, r * P:(r + 1) * P], xn[:, r, :], ident[:, :])
                mm.then_inc(M["uT_ps"], 1)

            def conv(b, k):
                n = NJ * b + k
                if k == 0:
                    wait(eng, M["uT"], b + 1)
                if k < 2:
                    wait(eng, M["zs"], 2 * (b - 1) + k + 1)
                    wait(eng, R2["lg" if k else "t"], b - 1)
                    eng.matmul(bank(6 + k), bcT[:, k, :], xnT[:, :], start=True, stop=True).then_inc(M["cv_ps"], 1)
                    return
                wait(eng, M["conv"], 6 * b + 3 * (k - 1))
                for s in range(CONV_W):
                    mm = eng.matmul(bank(6 + k % 2)[:, s:], tapT[:, k - 2, CONV_W - 1 - s, :], xnT[:, 0:SEQ - s],
                                    start=(s == 0), stop=(s == CONV_W - 1), skip_group_check=True)
                mm.then_inc(M["cv_ps"], 1)

            def z_proj(b, k):
                wait(eng, M["xs"], NJ * b + k + 1)
                for c in range(2):
                    mm = eng.matmul(bank(6 + k)[:, c * DI:(c + 1) * DI], xnT[:, (2 * k + c) * P:(2 * k + c + 1) * P], zT[:, :],
                                    start=True, stop=True)
                mm.then_inc(M["z_ps"], 1)

            def dt_proj(b):
                wait(eng, M["x"], b)
                for c in range(NT):
                    mm = eng.matmul(bank(4)[:, c * NH:(c + 1) * NH], xnT[:, c * P:(c + 1) * P], dtT[:, :], start=True, stop=True)
                mm.then_inc(M["dt_ps"], 1)

            def decay_sums(b):
                wait(eng, M["a"], b + 1)
                a_all = dt_a[:, 1, :, :].rearrange("p c h -> p (c h)")
                eng.matmul(bank(5)[:, 0:NT * NH], upto[:, :], a_all, start=True, stop=True)
                eng.matmul(bank(5)[:, NT * NH:2 * NT * NH], ones[:, :], a_all, start=True, stop=True).then_inc(M["dk_ps"], 1)

            def front(b, c):
                n = NT * b + c
                at = slice(c * P, (c + 1) * P)
                if c == 0:
                    wait(eng, M["xs"], NJ * b + NJ)
                wait(eng, M["cb"], n)
                eng.matmul(bank(0)[:, 0:P], xs[:, 2, at], xs[:, 3, at], start=True, stop=True).then_inc(M["cb_ps"], 1)
                wait(eng, M["xb"], n)
                for j in range(3):
                    mm = eng.transpose(bank(1)[:, j * P:(j + 1) * P], xs[:, j, at], ident[:, :])
                mm.then_inc(M["xb_ps"], 1)
                wait(eng, M["segs"], n)
                wait(eng, M["ramp"], n + 1)
                eng.matmul(bank(2), after[:, :], ramp[:, c % 2, :, :].rearrange("k h t -> k (h t)"), start=True,
                           stop=True).then_inc(M["seg_ps"], 1)

            def back(b, c):
                n = NT * b + c
                at = slice(c * P, (c + 1) * P)
                if c < NT - 1:
                    wait(eng, M["xw"], (NT - 1) * b + c + 1)
                    if c:
                        wait(eng, M["state"], (NT - 1) * b + c)
                    else:
                        wait(eng, M["dt_x"], b + 1)
                    eng.matmul(bank(4)[:, 0:DI], xb_tok[:, c % 2, 2, :], xw[:, c % 2, :], start=True, stop=True).then_inc(M["st_ps"], 1)
                wait(eng, M["y"], n)
                for j in range(2):
                    eng.matmul(bank(3)[:, j * P:(j + 1) * P], xs[:, j, at], skip_diag[:, j, :], start=(j == 0), stop=False,
                               skip_group_check=True)
                if c:
                    wait(eng, M["state"], (NT - 1) * b + c)
                    eng.matmul(bank(3)[:, DI:2 * DI], xs[:, 3, at], state[:, (c - 1) % 2, :], start=False, stop=True,
                               skip_group_check=True)
                wait(eng, M["gram"], NH * (n + 1))
                for h in range(NH):
                    mm = eng.matmul(bank(3)[:, h * HD:(h + 1) * HD], gram[:, c % 2, h, :],
                                    xb_tok[:, c % 2, h // 2, (h % 2) * HD:(h % 2 + 1) * HD], start=False, stop=(h == NH - 1),
                                    skip_group_check=True)
                mm.then_inc(M["y_ps"], 1)

            def g_turn(b, c):
                n = NT * b + c
                wait(eng, M["gn"], n + 1)
                if c == 0:
                    wait(eng, M["decay"], b + 1)
                    wait(eng, R2["route"], b)
                wait(eng, M["gT"], n)
                for j in range(2):
                    mm = eng.transpose(bank(5)[:, j * P:(j + 1) * P], gn[:, c % 2, j * P:(j + 1) * P], ident[:, :])
                mm.then_inc(M["gT_ps"], 1)

            def out_proj(b):
                wait(eng, M["gT"], NT * b + NT)
                wait(eng, M["state"], (NT - 1) * (b + 1))
                for r in range(NT):
                    for j in range(2):
                        mm = eng.matmul(bank(4)[:, r * D:(r + 1) * D], gT[:, j, r:SEQ:NT], outT[:, j, :], start=(j == 0),
                                        stop=(j == 1))
                mm.then_inc(M["o_ps"], 1)

            def step(i, first, second, third):
                if second:
                    conv(i, 0)
                    conv(i, 1)
                    dt_proj(i)
                    conv(i, 2)
                    conv(i, 3)
                    z_proj(i, 0)
                    z_proj(i, 1)
                if third:
                    router_turn(R2, i - 1, lambda: wait(eng, M["zs"], least(2 * i + 1, 2 * NB)))
                    router_logits(R2, i - 1, lambda: wait(eng, M["zs"], least(2 * i + 2, 2 * NB)))
                if second:
                    decay_sums(i)
                    front(i, 0)
                if third:
                    router_parts(R2, i - 1, 5, lambda: wait(eng, M["decay"] if second else M["gT"],
                                                            i + 1 if second else NT * NB))
                if second:
                    for c in range(NT):
                        if c + 1 < NT:
                            front(i, c + 1)
                        back(i, c)
                        if c:
                            g_turn(i, c - 1)
                    g_turn(i, NT - 1)
                if first:
                    u_turn(i + 1)
                if second:
                    out_proj(i)
            skew(eng, step)

            eng.wait_ge(R2["stash"], NB)
            eng.wait_ge(R2["route"], NB)
            eng.wait_ge(R2["xn"], NB)
            eng.wait_ge(M["x"], NB)
            eng.wait_ge(M["y"], NB * NT)
            ffn(F2, 0, True)
            ffn(F2, 1, False)
            with eng.Fori(2, NB) as b:
                ffn(F2, b, False)
            ffn(F2, NB, False, True)


_INS = ['L0_attn_a_x', 'L0_attn_a_w_qkv', 'L0_attn_a_w_proj', 'L0_attn_a_b_proj', 'L0_attn_b_W_in', 'L0_attn_b_conv_w',
        'L0_attn_b_conv_b', 'L0_attn_b_dt_bias', 'L0_attn_b_A_log', 'L0_attn_b_D', 'L0_attn_b_norm_w', 'L0_attn_b_W_out',
        'L0_ffn_scale', 'L0_ffn_gate_w', 'L0_ffn_gate_b', 'L0_ffn_mlp1_w', 'L0_ffn_mlp1_b', 'L0_ffn_mlp2_w', 'L0_ffn_mlp2_b']


def kernel(**inputs):
    import concourse.bacc as bacc
    from concourse.bass_utils import run_bass_kernel_spmd
    nc = bacc.Bacc("TRN2", target_bir_lowering=False, num_devices=1)
    ins = {name: np.ascontiguousarray(np.asarray(inputs[name])) for name in _INS}
    drams = [nc.dram_tensor(f"in_{name}_dram", ins[name].shape, F32, kind="ExternalInput").ap() for name in _INS]
    out = nc.dram_tensor("out_dram", (NB, SEQ, D), F32, kind="ExternalOutput").ap()
    build(nc, *drams, out)
    arrays = {f"in_{name}_dram": ins[name] for name in _INS}
    return run_bass_kernel_spmd(nc, [arrays], core_ids=[0]).results[0]["out_dram"]
```

```python
from contextlib import ExitStack

import numpy as np
import concourse.bass as bass
from concourse import mybir

F32 = mybir.dt.float32
F32R = mybir.dt.float32r
BF16 = mybir.dt.bfloat16
ALU = mybir.AluOpType
ACT = mybir.ActivationFunctionType
AX = mybir.AxisListType

P = 128
NB = 8
SEQ = 512
NT = SEQ // P
D = 128
NE = 16
TOPK = 4
I = 128
HEAD = 8
LN_EPS = 1e-5
ALPHA = 1.702
LIMIT = 7.0
CONV_W = 4
NH = 4
HD = 64
DI = NH * HD
NJ = 4
PARTS = 3
PSTEP = 32
LOWEST = -3.0e38
PE_TILES = (0, 1)
DVE_TILES = (2, 3)


def build(nc, x, w_qkv, w_proj, b_proj, W_in, conv_w, conv_b, dt_bias, A_log, Dskip, norm_w, W_out,
          ffn_scale, gate_w, gate_b, mlp1_w, mlp1_b, mlp2_w, mlp2_b, out):
    with ExitStack() as ctx:
        def sb(name, shape, dt=F32):
            return ctx.enter_context(nc.sbuf_tensor(name, shape, dt))

        def sem(name):
            return ctx.enter_context(nc.semaphore(name))

        X = sb("X", [P, NB, NT, D])
        ffn_hi = sb("ffn_hi", [P, NB, SEQ], F32R)
        ffn_lo = sb("ffn_lo", [P, NB, SEQ], F32R)
        route = sb("route", [PARTS * PSTEP, NB, SEQ], BF16)
        ident = sb("ident", [P, P])
        ident_b = sb("ident_b", [P, P], BF16)
        ones = sb("ones", [P, P])
        upto = sb("upto", [P, P])
        after = sb("after", [P, P])
        pick = sb("pick", [PARTS * PSTEP, NE, P], BF16)
        eps4 = sb("eps4", [P, NT])
        mhalf4 = sb("mhalf4", [P, NT])
        limit_col = sb("limit_col", [P, 1])
        top_col = sb("top_col", [P, 1])
        gate_rows = sb("gate_rows", [NE, D])
        vec_row = sb("vec_row", [1, 160])
        scale_col = sb("scale_col", [P, 1])
        w1_rows = sb("w1_rows", [P, NE, D])
        w2_rows = sb("w2_rows", [P, NE, I])
        b1_rows = sb("b1_rows", [NE, 2 * I])
        b2_rows = sb("b2_rows", [PARTS * PSTEP, D])
        a_qk = sb("a_qk", [P, D])
        vpg = sb("vpg", [P, 2 * D + NE])
        wvT, wpT, gateT = vpg[:, 0:D], vpg[:, D:2 * D], vpg[:, 2 * D:]
        vecs = sb("vecs", [P, 160])
        w1_hi = sb("w1_hi", [P, NE, I], F32R)
        w1_lo = sb("w1_lo", [P, NE, I], F32R)
        w2_hi = sb("w2_hi", [P, NE, D], F32R)
        w2_lo = sb("w2_lo", [P, NE, D], F32R)
        b1T = sb("b1T", [P, NE])
        b2_parts = sb("b2_parts", [PARTS * PSTEP, PARTS, D], BF16)
        ln1_st = sb("ln1_st", [P, NT, 6])
        ln1_mv = sb("ln1_mv", [P, NT, 2])
        ln1_ve = sb("ln1_ve", [P, NT])
        ln1_rs = sb("ln1_rs", [P, NT])
        xn = sb("xn", [P, NT, D])
        rt_st = sb("rt_st", [P, NT, 6])
        rt_mv = sb("rt_mv", [P, NT, 2])
        rt_small = sb("rt_small", [P, 9, NT])
        t0 = sb("t0", [P, NT, D])
        tT = sb("tT", [P, SEQ])
        logits = sb("logits", [P, NT, NE + TOPK])
        replaced = sb("replaced", [P, NT, NE + TOPK])
        top8 = sb("top8", [P, NT, 8])
        rt_tmp = sb("rt_tmp", [P, 6, NT, NE])
        rt_sum = sb("rt_sum", [P, 2, NT])
        rt_parts = sb("rt_parts", [P, NT, PARTS, PSTEP], BF16)
        in_rows = sb("in_rows", [P, 6, D])
        dt_rows = sb("dt_rows", [NH, D])
        out_rows = sb("out_rows", [P, DI])
        conv_taps = sb("conv_taps", [P, NJ, CONV_W])
        col_rows = sb("col_rows", [NJ + 2, P])
        cols = sb("cols", [P, NJ + 2])
        conv_bias, norm_col = cols[:, 0:NJ], cols[:, NJ:]
        tapT = sb("tapT", [P, len(PE_TILES), CONV_W, P])
        bcT = sb("bcT", [P, len(DVE_TILES), P])
        zT = sb("zT", [P, DI])
        dtT = sb("dtT", [P, NH])
        outT = sb("outT", [P, 2, D])
        skip_diag = sb("skip_diag", [P, 2, P])
        neg_A = sb("neg_A", [P, NH])

        with ExitStack() as stage:
            def own(name, shape, dt=F32):
                return stage.enter_context(nc.sbuf_tensor(name, shape, dt))

            proj_rows = own("proj_rows", [P, D])
            qkv_rows = own("qkv_rows", [P, 3, D])
            xnT = own("xnT", [P, 2, SEQ])
            qT = own("qT", [P, 2, SEQ])
            v = own("v", [P, 2, NT, D])
            probs = own("probs", [P, NT, SEQ])
            probsT = own("probsT", [P, NT, NT, P])
            attn = own("attn", [P, NT, D])
            neg_max = own("neg_max", [P, NT])
            row_sum = own("row_sum", [P, NT])
            row_rec = own("row_rec", [P, NT])
        with ExitStack() as stage:
            NR = 4
            act_ring = own("act_ring", [P, 2, SEQ])
            s_ring = own("s_ring", [P, 2, SEQ])
            s_hi = own("s_hi", [P, NR, SEQ], F32R)
            s_lo = own("s_lo", [P, NR, SEQ], F32R)
            acc_sb = own("acc_sb", [P, SEQ])
            b2_rest = own("b2_rest", [PARTS * PSTEP, 2, D])
        with ExitStack() as stage:
            uT = own("uT", [P, SEQ])
            conv_acc = own("conv_acc", [P, NJ, SEQ])
            xs = own("xs", [P, 2, NJ, SEQ])
            zs = own("zs", [P, 2, NT, DI])
            dt_tmp = own("dt_tmp", [P, 7, NT * NH])
            dt_a = own("dt_a", [P, 2, 2, NT, NH])
            decay = own("decay", [P, 2, 2, NT, NH])
            ramp = own("ramp", [P, 2, NH, P])
            segs = own("segs", [P, 2, NH, P])
            tap_rows = segs
            cb = own("cb", [P, 2, P])
            gram = own("gram", [P, 2, NH, P])
            xb_tok = own("xb_tok", [P, 2, 3, P])
            to_end = own("to_end", [P, 2, NH])
            xw = own("xw", [P, 2, DI])
            state = own("state", [P, 2, DI])
            state_d = own("state_d", [P, DI])
            y_off = own("y_off", [P, DI])
            y = own("y", [P, 2, DI])
            g = own("g", [P, 2, DI])
            g_sq = own("g_sq", [P, DI])
            table_col = own("table_col", [P, 1])
            g_ss = own("g_ss", [P, NT])
            g_rs = own("g_rs", [P, 2, NT])
            gn = own("gn", [P, 2, DI])
            gT = own("gT", [P, 2, SEQ])

        ps = ctx.enter_context(nc.psum_tensor("ps", [P, 8, 512], F32))

        def bank(i):
            return ps[:, i, :]

        x_first = sem("x_first")
        x_rest = sem("x_rest")
        w_attn = sem("w_attn")
        w_vecs = sem("w_vecs")
        w_ffn = sem("w_ffn")
        consts = sem("consts")
        prep_ps = sem("prep_ps")
        prep_sb = sem("prep_sb")
        prep2_ps = sem("prep2_ps")
        prep2_sb = sem("prep2_sb")
        prep2_hi = sem("prep2_hi")
        b2_split = sem("b2_split")
        stored = sem("stored")
        gate_pool = sem("gate_pool")
        gate_dve = sem("gate_dve")
        gate_act = sem("gate_act")
        table = sem("table")
        N_CONST = 16

        VB, VG, VDT, VA, VD = 0, D, D + NE, D + NE + NH, D + NE + 2 * NH
        VEND = VD + NH
        b_proj_all = vecs[:, VB:VB + D]
        gate_b_all = vecs[:, VG:VG + NE]

        S1 = {n: sem("attn_" + n) for n in (
            "stats", "aggr", "rstd", "xn", "xnT_ps", "xnT", "q_ps", "q", "v_ps", "v", "scores", "max", "probs",
            "pT_ps", "pT", "o_ps", "rec", "o", "y_ps", "xb", "x1")}

        def router_sems(tag):
            return {n: sem(tag + n) for n in (
                "stats", "aggr", "pool", "t0", "xn", "t_ps", "t", "t_hi", "stash", "lg_ps", "lg", "max", "cut", "shift",
                "rep", "mask", "exp", "em", "weights", "lo", "rt_ps", "route")}

        R1 = router_sems("router1_")

        def ffn_sems(tag):
            return {n: sem(tag + n) for n in ("h", "rb", "act", "s", "hi", "lo", "out", "acc_sb", "back", "x")}

        F1 = ffn_sems("ffn1_")

        R2 = router_sems("router2_")
        F2 = ffn_sems("ffn2_")
        M = {n: sem("ssm_" + n) for n in (
            "stats", "aggr", "rstd", "xn", "uT_ps", "uT", "cv_ps", "tap", "conv", "raw", "xs", "z_ps", "z_raw", "zs", "dt_ps", "dt_x",
            "dt_m", "dt_u", "log", "dt", "a", "dk_ps", "decay", "ramp", "cb_ps", "cb", "xb_ps", "xb", "seg_ps", "segs",
            "gram", "end", "xw", "st_ps", "state_d", "state", "y_ps", "y_off", "y", "g", "sq", "rms", "gn", "gT_ps",
            "gT", "o_ps", "x")}
        w_ssm = sem("w_ssm")
        taps_ready = sem("taps_ready")
        prep3_ps = sem("prep3_ps")
        prep3_sb = sem("prep3_sb")

        block = ctx.enter_context(nc.Block())

        PREP3 = 9
        PH = len(PE_TILES)

        def wait(eng, s, value):
            if isinstance(value, int) and value <= 0:
                return
            eng.wait_ge(s, value)

        def skew_pairs(eng, step, count=NB, tail=()):
            for i in range(-1, 3):
                step(i, i % 2, True, i >= 0, i >= 1, i >= 2)
            with eng.Fori(3, count - 2, 2) as i:
                step(i, 1, True, True, True, True)
                step(i + 1, 0, True, True, True, True)
            for i in range(count - 1, count + 2):
                if tail and i >= count:
                    tail[i - count]()
                step(i, i % 2, False, i < count, i <= count, True)

        def least(a, cap):
            return min(a, cap) if isinstance(a, int) else a

        @block.sync
        def _(eng):
            eng.dma_start(X[:, 0, :, :], x[0].rearrange("(p r) d -> p r d", r=NT)).then_inc(x_first, 16)
            eng.dma_start(qkv_rows[:, :, :], w_qkv.rearrange("(m p) d -> p m d", p=P)).then_inc(w_attn, 16)
            eng.dma_start(proj_rows[:, :], w_proj).then_inc(w_attn, 16)
            eng.dma_start(gate_rows[:, :], gate_w).then_inc(w_attn, 16)
            eng.dma_start(X[:, 1:NB, :, :], x[1:NB].rearrange("b (p r) d -> p b r d", r=NT)).then_inc(x_rest, 16)
            eng.dma_start(w1_rows[:, :, :], mlp1_w.rearrange("e (i two) d -> i two e d", two=2)[:, 0]).then_inc(w_ffn, 16)
            eng.dma_start(w2_rows[:, :, :], mlp2_w.rearrange("e h i -> h e i")).then_inc(w_ffn, 16)
            eng.dma_start(b1_rows[:, :], mlp1_b).then_inc(w_ffn, 16)
            eng.dma_start(in_rows[:, :, :], W_in[0:6 * P].rearrange("(m p) d -> p m d", p=P)).then_inc(w_ssm, 16)
            eng.dma_start(dt_rows[:, :], W_in[6 * P:]).then_inc(w_ssm, 16)
            eng.dma_start(out_rows[:, :], W_out).then_inc(w_ssm, 16)
            eng.dma_start(conv_taps[:, :, :], conv_w.rearrange("(j p) w -> p j w", p=P)).then_inc(w_ssm, 16)
            eng.dma_start(col_rows[0:NJ, :], conv_b.rearrange("(j p) -> j p", p=P)).then_inc(w_ssm, 16)
            eng.dma_start(col_rows[NJ:NJ + 2, :], norm_w.rearrange("(j p) -> j p", p=P)).then_inc(w_ssm, 16)
            eng.wait_ge(consts, N_CONST)
            for g in range(PARTS):
                eng.dma_start(b2_rows[g * PSTEP:g * PSTEP + NE, :], mlp2_b).then_inc(w_ffn, 16)
            with eng.Fori(0, NB) as b:
                eng.wait_ge(F2["x"], b + 1)
                eng.dma_start(out[b].rearrange("(p r) d -> p r d", r=NT), X[:, b, :, :]).then_inc(stored, 16)
            eng.wait_ge(stored, 16 * NB)

        @block.gpsimd
        def _(eng):
            c = [0]

            def const(ins):
                ins.then_inc(consts, 1)
                c[0] += 1

            const(eng.memset(ident[:, :], 0.0))
            const(eng.memset(ident_b[:, :], 0.0))
            const(eng.memset(ones[:, :], 1.0))
            const(eng.memset(pick[:, :, :], 0.0))
            const(eng.memset(eps4[:, :], LN_EPS))
            const(eng.memset(mhalf4[:, :], -0.5))
            const(eng.memset(limit_col[:, :], LIMIT))
            const(eng.memset(logits[:, :, NE:], LOWEST))
            const(eng.memset(rt_parts[:, :, :, :], 0.0))
            const(eng.memset(b2_rows[:, :], 0.0))
            eng.wait_ge(consts, c[0])
            for m in (ident, ident_b):
                const(eng.affine_select(out=m[:, :], in_=m[:, :], compare_op=ALU.not_equal, fill=1.0, base=0,
                                        pattern=[[-1, P]], channel_multiplier=1))
            const(eng.affine_select(out=upto[:, :], in_=ones[:, :], compare_op=ALU.is_ge, fill=0.0, base=0,
                                    pattern=[[1, P]], channel_multiplier=-1))
            const(eng.affine_select(out=after[:, :], in_=ones[:, :], compare_op=ALU.is_gt, fill=0.0, base=0,
                                    pattern=[[-1, P]], channel_multiplier=1))
            for part in range(PARTS):
                eng.wait_ge(consts, c[0])
                ins = eng.affine_select(out=pick[:, :, :], in_=pick[:, :, :], compare_op=ALU.not_equal, fill=1.0,
                                        base=-part * PSTEP, pattern=[[-1, NE], [0, P]], channel_multiplier=1)
                if part < PARTS - 1:
                    const(ins)
            ins.then_inc(consts, 1)
            assert c[0] + 1 == N_CONST + 1 or True

            def router_chain(R, b):
                n = [0]

                def tt(o, a, bb, op):
                    eng.tensor_tensor(o, a, bb, op).then_inc(R["pool"], 1)
                    n[0] += 1
                    wait(eng, R["pool"], 9 * b + n[0])

                var = rt_mv[:, :, 1]
                wait(eng, R["aggr"], NT * b + NT)
                wait(eng, R["xn"], NT * b)
                tt(rt_small[:, 0, :], var, eps4[:, :], ALU.add)
                tt(rt_small[:, 1, :], rt_small[:, 0, :], mhalf4[:, :], ALU.pow)
                tt(rt_small[:, 2, :], rt_small[:, 1, :], rt_small[:, 1, :], ALU.mult)
                tt(rt_small[:, 3, :], rt_small[:, 2, :], var, ALU.mult)
                tt(rt_small[:, 4, :], rt_small[:, 3, :], eps4[:, :], ALU.add)
                tt(rt_small[:, 5, :], rt_small[:, 4, :], mhalf4[:, :], ALU.pow)
                tt(rt_small[:, 6, :], rt_small[:, 5, :], rt_small[:, 1, :], ALU.mult)
                tt(rt_small[:, 7, :], rt_small[:, 1, :], ones[:, 0:NT], ALU.add)
                eng.tensor_tensor(rt_small[:, 8, :], rt_small[:, 1, :], rt_mv[:, :, 0], ALU.mult).then_inc(R["pool"], 1)

            def router_stash(R, b):
                eng.wait_ge(R["t"], b + 1).then_inc(gate_pool, 1)
                eng.wait_ge(R["t_hi"], b + 1).then_inc(gate_pool, 1)
                eng.tensor_tensor(ffn_lo[:, b, :], tT[:, :], ffn_hi[:, b, :].bitcast(F32),
                                  ALU.subtract).then_inc(R["stash"], 1)

            def ln1_chain(b):
                wait(eng, S1["aggr"], NT * b + NT)
                wait(eng, S1["xn"], NT * b)
                eng.tensor_tensor(ln1_ve[:, :], ln1_mv[:, :, 1], eps4[:, :], ALU.add).then_inc(S1["rstd"], 1)
                wait(eng, S1["rstd"], 2 * b + 1)
                eng.tensor_tensor(ln1_rs[:, :], ln1_ve[:, :], mhalf4[:, :], ALU.pow).then_inc(S1["rstd"], 1)

            def add_bias(b):
                eng.wait_ge(S1["xn"], NT * b + NT).then_inc(gate_pool, 1)
                if isinstance(b, int) and b == 0:
                    eng.wait_ge(prep_sb, 3)
                eng.tensor_tensor(X[:, b, :, :], X[:, b, :, :],
                                  b_proj_all.unsqueeze(1).to_broadcast([P, NT, D]), ALU.add).then_inc(S1["xb"], 1)

            eng.wait_ge(consts, N_CONST)

            def step(i, odd, first, second, third, fourth):
                if first:
                    ln1_chain(i + 1)
                if fourth:
                    router_stash(R1, i - 2)
                if third:
                    router_chain(R1, i - 1)
                if first:
                    add_bias(i + 1)
            skew_pairs(eng, step)

            def ssm_norm(b):
                wait(eng, M["aggr"], NT * b + NT)
                wait(eng, M["xn"], NT * b)
                eng.tensor_tensor(ln1_ve[:, :], ln1_mv[:, :, 1], eps4[:, :], ALU.add).then_inc(M["rstd"], 1)
                wait(eng, M["rstd"], 2 * b + 1)
                eng.tensor_tensor(ln1_rs[:, :], ln1_ve[:, :], mhalf4[:, :], ALU.pow).then_inc(M["rstd"], 1)

            def ramps(b, par, c):
                n = NT * b + c
                wait(eng, M["seg_ps"], n - 1)
                wait(eng, M["a"], b + 1)
                eng.tensor_tensor(ramp[:, c % 2, :, :], upto[:, :].unsqueeze(1).to_broadcast([P, NH, P]),
                                  dt_a[:, par, 1, c, :].unsqueeze(2).to_broadcast([P, NH, P]),
                                  ALU.mult).then_inc(M["ramp"], 1)

            def weigh(b, par, c):
                n = NT * b + c
                k = (NT - 1) * b + c
                wait(eng, M["xb"], n + 1)
                wait(eng, M["st_ps"], k - 1)
                wait(eng, M["end"], n + 1)
                eng.tensor_tensor(xw[:, c % 2, :].rearrange("s (h p) -> s h p", h=NH),
                                  xb_tok[:, c % 2, 0:2, :].rearrange("s j (h p) -> s (j h) p", p=HD),
                                  to_end[:, c % 2, :].unsqueeze(2).to_broadcast([P, NH, HD]),
                                  ALU.mult).then_inc(M["xw"], 1)
                if c:
                    wait(eng, M["state"], k)
                    eng.tensor_tensor(state_d[:, :].rearrange("n (h p) -> n h p", h=NH),
                                      state[:, (c - 1) % 2, :].rearrange("n (h p) -> n h p", h=NH),
                                      decay[:, par, 1, c, :].unsqueeze(2).to_broadcast([P, NH, HD]),
                                      ALU.mult).then_inc(M["state_d"], 1)

            def gate(b, par, c):
                n = NT * b + c
                wait(eng, M["y"], n + 1)
                wait(eng, M["gn"], n - 1)
                wait(eng, M["zs"], b + 1)
                eng.tensor_tensor(g[:, c % 2, :], y[:, c % 2, :], zs[:, par, c, :], ALU.mult).then_inc(M["g"], 1)

            def rms(b, c):
                n = NT * b + c
                wait(eng, M["sq"], n + 1)
                eng.tensor_tensor(g_rs[:, 0, c:c + 1], g_ss[:, c:c + 1], eps4[:, 0:1], ALU.add).then_inc(M["rms"], 1)
                wait(eng, M["rms"], 2 * n + 1)
                wait(eng, M["gn"], n - 3)
                eng.tensor_tensor(g_rs[:, 1, c:c + 1], g_rs[:, 0, c:c + 1], mhalf4[:, 0:1], ALU.pow).then_inc(M["rms"], 1)

            eng.wait_ge(prep3_sb, PREP3)

            def step(i, odd, first, second, third, fourth):
                if first:
                    ssm_norm(i + 1)
                if second:
                    weigh(i, odd, 0)
                    ramps(i, odd, 2)
                    gate(i, odd, 0)
                    rms(i, 0)
                    weigh(i, odd, 1)
                if fourth:
                    router_stash(R2, i - 2)
                if second:
                    ramps(i, odd, 3)
                    gate(i, odd, 1)
                    rms(i, 1)
                    weigh(i, odd, 2)
                if third:
                    router_chain(R2, i - 1)
                if second:
                    gate(i, odd, 2)
                    rms(i, 2)
                if first:
                    ramps(i + 1, 1 - odd, 0)
                    ramps(i + 1, 1 - odd, 1)
                if second:
                    gate(i, odd, 3)
                    rms(i, 3)
            skew_pairs(eng, step)

        @block.scalar
        def _(eng):
            for at, src in ((VB, b_proj), (VG, gate_b), (VDT, dt_bias), (VA, A_log), (VD, Dskip)):
                eng.dma_start(vec_row[0:1, at:at + src.shape[0]], src.rearrange("(a n) -> a n", a=1)).then_inc(w_vecs, 16)
            eng.dma_start(scale_col[:, :], ffn_scale.rearrange("(p a) -> p a", a=1)).then_inc(w_vecs, 16)
            eng.wait_ge(prep_ps, 1)
            eng.activation(a_qk[:, :], bank(0)[:, 0:D], ACT.Copy, scale=float(HEAD) ** -0.5).then_inc(prep_sb, 1)
            eng.wait_ge(prep_ps, 2)
            eng.activation(vpg[:, :], bank(1)[:, 0:2 * D + NE], ACT.Copy).then_inc(prep_sb, 1)
            eng.wait_ge(prep_ps, 3)
            eng.activation(vecs[:, 0:VEND], bank(2)[:, 0:VEND], ACT.Copy).then_inc(prep_sb, 1)

            def exps(b, rs):
                for r in rs:
                    wait(eng, S1["max"], NT * b + r + 1)
                    if r == 0:
                        wait(eng, S1["rec"], b)
                    wait(eng, S1["pT_ps"], NT * (b - 1) + r + 1)
                    eng.activation(probs[:, r, :], bank(r), ACT.Exp, bias=neg_max[:, r:r + 1],
                                   accum_out=row_sum[:, r:r + 1]).then_inc(S1["probs"], 1)

            def pT(b, rs):
                for r in rs:
                    wait(eng, S1["pT_ps"], NT * b + r + 1)
                    wait(eng, S1["o_ps"], b)
                    eng.activation(probsT[:, r, :, :], bank(r).rearrange("k (t q) -> k t q", t=NT),
                                   ACT.Copy).then_inc(S1["pT"], 1)

            def xnT_out(b, par):
                wait(eng, S1["xnT_ps"], b + 1)
                wait(eng, S1["v_ps"], b - 1)
                wait(eng, S1["scores"], NT * (b - 1))
                eng.activation(xnT[:, par, :].rearrange("d (p r) -> d r p", r=NT),
                               bank(4).rearrange("d (r p) -> d r p", r=NT), ACT.Copy).then_inc(S1["xnT"], 1)

            def q_out(b, par):
                wait(eng, S1["q_ps"], b + 1)
                wait(eng, S1["scores"], NT * (b - 1))
                eng.activation(qT[:, par, :], bank(4), ACT.Copy).then_inc(S1["q"], 1)

            def v_out(b, par):
                wait(eng, S1["v_ps"], b + 1)
                wait(eng, S1["o_ps"], b - 1)
                eng.activation(v[:, par, :, :], bank(6).rearrange("k (t h) -> k t h", t=NT), ACT.Copy).then_inc(S1["v"], 1)

            def attn_out(b):
                wait(eng, S1["rec"], b + 1)
                wait(eng, S1["o_ps"], b + 1)
                wait(eng, S1["y_ps"], b)
                for r in range(NT):
                    eng.activation(attn[:, r, :], bank(5)[:, r * D:(r + 1) * D], ACT.Copy,
                                   scale=row_rec[:, r:r + 1]).then_inc(S1["o"], 1)

            def router_t(R, b, at):
                wait(eng, R["t_ps"], b + 1)
                wait(eng, R["lg_ps"], b)
                wait(eng, R["stash"], b)
                eng.activation(tT[:, :], bank(at), ACT.Copy, scale=scale_col[:, 0:1]).then_inc(R["t"], 1)
                eng.wait_ge(R["t"], b + 1).then_inc(gate_act, 1)
                eng.activation(ffn_hi[:, b, :], tT[:, :], ACT.Copy).then_inc(R["t_hi"], 1)

            def router_exp(R, b):
                wait(eng, R["shift"], b + 1)
                wait(eng, R["em"], b)
                eng.activation(rt_tmp[:, 1, :, :], rt_tmp[:, 0, :, :], ACT.Exp).then_inc(R["exp"], 1)

            def router_out(R, b, rt_bank):
                eng.wait_ge(R["rt_ps"], b + 1).then_inc(gate_act, 1)
                eng.activation(route[:, b, :], rt_bank.bitcast(BF16)[0:PARTS * PSTEP, 0:SEQ],
                               ACT.Copy).then_inc(R["route"], 1)

            def step(i, odd, first, second, third, fourth):
                if second:
                    exps(i, (0, 1))
                if fourth:
                    router_t(R1, i - 2, 7)
                if second:
                    exps(i, (2, 3))
                    pT(i, range(NT))
                if first:
                    xnT_out(i + 1, 1 - odd)
                if fourth:
                    router_exp(R1, i - 2)
                if first:
                    q_out(i + 1, 1 - odd)
                    v_out(i + 1, 1 - odd)
                if second:
                    attn_out(i)
                if fourth:
                    router_out(R1, i - 2, bank(7))

            def expert_weights_1():
                for quad in range(NE // 4):
                    eng.wait_ge(prep2_ps, quad + 1)
                    eng.activation(w1_hi[:, 4 * quad:4 * quad + 4, :], bank(quad).rearrange("d (e i) -> d e i", e=4),
                                   ACT.Copy).then_inc(prep2_hi, 1)

            def expert_weights_2():
                for quad in range(NE // 4):
                    eng.wait_ge(prep2_ps, 4 + quad + 1)
                    eng.activation(w2_hi[:, 4 * quad:4 * quad + 4, :], bank(quad).rearrange("i (e h) -> i e h", e=4),
                                   ACT.Copy, scale=(LIMIT + 1.0) / ALPHA).then_inc(prep2_hi, 1)

                for k in range(PH):
                    eng.wait_ge(prep3_ps, k + 1)
                    eng.activation(tapT[:, k, :, :], bank(k).rearrange("d (w c) -> d w c", w=CONV_W),
                                   ACT.Copy).then_inc(prep3_sb, 1)
                eng.wait_ge(prep3_ps, PH + 1)
                eng.activation(bcT[:, :, :], bank(2)[:, 0:2 * P].rearrange("d (j c) -> d j c", j=2),
                               ACT.Copy).then_inc(prep3_sb, 1)
                eng.activation(zT[:, :], bank(2)[:, 2 * P:4 * P], ACT.Copy).then_inc(prep3_sb, 1)
                eng.wait_ge(prep3_ps, PH + 2)
                eng.activation(dtT[:, :], bank(3)[:, 0:NH], ACT.Copy).then_inc(prep3_sb, 1)
                eng.activation(cols[:, :], bank(3)[:, NH:NH + NJ + 2], ACT.Copy).then_inc(prep3_sb, 1)
                eng.wait_ge(prep3_sb, PH + 4)
                for j in range(2):
                    eng.activation(outT[:, j, :], bank(3)[:, P * (j + 1):P * (j + 2)], ACT.Copy,
                                   scale=norm_col[:, j:j + 1]).then_inc(prep3_sb, 1)
                eng.activation(neg_A[:, :], vecs[:, VA:VA + NH], ACT.Exp).then_inc(prep3_sb, 1)

            skew_pairs(eng, step, tail=(expert_weights_1, expert_weights_2))

            eng.wait_ge(prep2_ps, 9)
            eng.activation(b1T[:, :], bank(4)[:, 0:NE], ACT.Copy, scale=ALPHA).then_inc(prep2_sb, 1)
            eng.activation(top_col[:, :], limit_col[:, :], ACT.Silu, scale=ALPHA).then_inc(prep2_sb, 1)

            def split(F, b, e):
                wait(eng, F["s"], NE * b + e + 1)
                wait(eng, F["out"], NE * b + e + 1 - NR)
                wait(eng, F["lo"], NE * b + e + 1 - NR)
                eng.activation(s_hi[:, e % NR, :], s_ring[:, e % 2, :], ACT.Copy).then_inc(F["hi"], 1)

            def ffn(F, b, peeled, tail=False):
                for e in range(NE):
                    if e == 3 and (tail or not peeled):
                        wait(eng, F["out"], NE * b)
                        wait(eng, F["back"], b - 1)
                        eng.activation(acc_sb[:, :], bank(6), ACT.Copy).then_inc(F["acc_sb"], 1)
                    if not tail:
                        wait(eng, F["h"], NE * b + e + 1)
                        wait(eng, F["s"], NE * b + e + 1 - 2)
                        eng.activation(act_ring[:, e % 2, :], bank(e % 4), ACT.Silu, bias=b1T[:, e:e + 1],
                                       scale=ALPHA).then_inc(F["act"], 1)
                        if e:
                            split(F, b, e - 1)
                    if e == 0 and (tail or not peeled):
                        split(F, b - 1, NE - 1)

            eng.wait_ge(prep2_sb, 10)
            ffn(F1, 0, True)
            ffn(F1, 1, False)
            with eng.Fori(2, NB) as b:
                ffn(F1, b, False)
            ffn(F1, NB, False, True)
            eng.wait_ge(prep3_sb, PREP3)

            def u_out(b):
                wait(eng, M["uT_ps"], b + 1)
                wait(eng, M["cv_ps"], NJ * b)
                wait(eng, M["dt_ps"], b)
                wait(eng, M["z_ps"], 2 * b)
                eng.activation(uT[:, :].rearrange("d (p r) -> d r p", r=NT),
                               bank(7).rearrange("d (r p) -> d r p", r=NT), ACT.Copy).then_inc(M["uT"], 1)

            def conv_first(b, k):
                j = DVE_TILES[k]
                wait(eng, M["cv_ps"], NJ * b + k + 1)
                wait(eng, M["xs"], b)
                eng.activation(conv_acc[:, j, :], bank(6 + k), ACT.Identity, bias=conv_bias[:, j:j + 1],
                               scale=conv_taps[:, j, CONV_W - 1:CONV_W]).then_inc(M["tap"], 1)

            def conv_out(b, k):
                j = PE_TILES[k]
                wait(eng, M["cv_ps"], NJ * b + 2 + k + 1)
                wait(eng, M["xs"], b)
                eng.activation(conv_acc[:, j, :], bank(6 + k), ACT.Identity, bias=conv_bias[:, j:j + 1]).then_inc(M["raw"], 1)

            def xs_silu(b, par):
                wait(eng, M["conv"], 6 * b + 6)
                wait(eng, M["raw"], 2 * b + 2)
                wait(eng, M["y_ps"], NT * (b - 1))
                eng.activation(xs[:, par, :, :], conv_acc[:, :, :], ACT.Silu).then_inc(M["xs"], 1)

            def z_out(b, par, k):
                wait(eng, M["z_ps"], 2 * b + k + 1)
                wait(eng, M["g"], NT * (b - 1))
                eng.activation(zs[:, par, 2 * k:2 * k + 2, :], bank(6 + k).rearrange("t (c e) -> t c e", c=2),
                               ACT.Copy).then_inc(M["z_raw"], 1)

            def z_silu(b, par):
                wait(eng, M["z_raw"], 2 * b + 2)
                eng.activation(zs[:, par, :, :], zs[:, par, :, :], ACT.Silu).then_inc(M["zs"], 1)

            def table_of(func):
                eng.activation(table_col[:, :], ones[:, 0:1], func).then_inc(table, 1)

            def dt_exp(b):
                wait(eng, M["dt_m"], b + 1)
                wait(eng, M["a"], b)
                eng.activation(dt_tmp[:, 2, :], dt_tmp[:, 1, :], ACT.Exp).then_inc(M["dt_u"], 1)

            def decays(b, par):
                wait(eng, M["dk_ps"], b + 1)
                wait(eng, M["y_off"], (NT - 1) * (b - 1))
                wait(eng, M["state_d"], (NT - 2) * (b - 1))
                eng.activation(decay[:, par, :, :, :],
                               bank(4)[:, 0:2 * NT * NH].rearrange("p (k c h) -> p k c h", k=2, c=NT),
                               ACT.Exp).then_inc(M["decay"], 1)

            def xb_out(b, c):
                n = NT * b + c
                k = (NT - 1) * b + max(c - 1, 0)
                wait(eng, M["xb_ps"], n + 1)
                wait(eng, M["y_ps"], n - 1)
                wait(eng, M["st_ps"], k)
                wait(eng, M["xw"], k)
                eng.activation(xb_tok[:, c % 2, :, :], bank(1)[:, 0:3 * P].rearrange("t (j c) -> t j c", j=3),
                               ACT.Copy).then_inc(M["xb"], 1)

            def seg_exp(b, c):
                n = NT * b + c
                wait(eng, M["seg_ps"], n + 1)
                wait(eng, M["gram"], NH * (n - 1))
                wait(eng, M["end"], n - 1)
                eng.activation(segs[:, c % 2, :, :], bank(2).rearrange("s (h t) -> s h t", h=NH),
                               ACT.Exp).then_inc(M["segs"], 1)

            def square(b, c):
                n = NT * b + c
                wait(eng, M["g"], n + 1)
                wait(eng, M["sq"], n)
                wait(eng, M["rms"], 2 * (n - 3))
                eng.activation(g_sq[:, :], g[:, c % 2, :], ACT.Square, scale=float(DI) ** -0.5,
                               accum_out=g_ss[:, c:c + 1]).then_inc(M["sq"], 1)

            def gT_out(b, c):
                n = NT * b + c
                wait(eng, M["gT_ps"], n + 1)
                wait(eng, M["o_ps"], b)
                eng.activation(gT[:, :, c * P:(c + 1) * P], bank(5)[:, 0:2 * P].rearrange("e (j t) -> e j t", j=2),
                               ACT.Copy).then_inc(M["gT"], 1)

            def step(i, odd, first, second, third, fourth):
                if second:
                    xb_out(i, 0)
                    seg_exp(i, 0)
                if third:
                    gT_out(i - 1, 3)
                if first:
                    u_out(i + 1)
                if second:
                    xb_out(i, 1)
                    seg_exp(i, 1)
                if fourth:
                    router_t(R2, i - 2, 6)
                if first:
                    conv_first(i + 1, 0)
                if second:
                    square(i, 0)
                if first:
                    conv_first(i + 1, 1)
                if second:
                    xb_out(i, 2)
                    seg_exp(i, 2)
                if first:
                    dt_exp(i + 1)
                if second:
                    gT_out(i, 0)
                    square(i, 1)
                if first:
                    conv_out(i + 1, 0)
                if second:
                    xb_out(i, 3)
                    seg_exp(i, 3)
                if fourth:
                    router_exp(R2, i - 2)
                if second:
                    gT_out(i, 1)
                    square(i, 2)
                if first:
                    z_out(i + 1, 1 - odd, 0)
                    decays(i + 1, 1 - odd)
                    table_of(ACT.Silu)
                    conv_out(i + 1, 1)
                    xs_silu(i + 1, 1 - odd)
                    z_out(i + 1, 1 - odd, 1)
                if second:
                    gT_out(i, 2)
                if first:
                    z_silu(i + 1, 1 - odd)
                    table_of(ACT.Exp)
                if second:
                    square(i, 3)
                if fourth:
                    router_out(R2, i - 2, bank(5))
            skew_pairs(eng, step)

            ffn(F2, 0, True)
            ffn(F2, 1, False)
            with eng.Fori(2, NB) as b:
                ffn(F2, b, False)
            ffn(F2, NB, False, True)

        @block.vector
        def _(eng):
            def ln1_stats(b):
                if isinstance(b, int) and b == 1:
                    eng.wait_ge(x_rest, 16)
                for r in range(NT):
                    eng.bn_stats(ln1_st[:, r, :], X[:, b, r, :]).then_inc(S1["stats"], 1)
                eng.wait_ge(S1["stats"], NT * b + NT).then_inc(gate_dve, 1)
                for r in range(NT):
                    eng.bn_aggr(ln1_mv[:, r, :], ln1_st[:, r, :]).then_inc(S1["aggr"], 1)

            def xn_out(b):
                wait(eng, S1["rstd"], 2 * b + 2)
                wait(eng, S1["xnT_ps"], b)
                for r in range(NT):
                    eng.tensor_scalar(xn[:, r, :], X[:, b, r, :], ln1_mv[:, r, 0:1], ln1_rs[:, r:r + 1],
                                      ALU.subtract, ALU.mult).then_inc(S1["xn"], 1)

            def maxes(b):
                for r in range(NT):
                    wait(eng, S1["scores"], NT * b + r + 1)
                    wait(eng, S1["probs"], NT * (b - 1) + r + 1)
                    eng.tensor_reduce(neg_max[:, r:r + 1], bank(r), AX.X, ALU.max, negate=True).then_inc(S1["max"], 1)

            def recip(b):
                wait(eng, S1["probs"], NT * b + NT)
                wait(eng, S1["o"], NT * b)
                eng.reciprocal(row_rec[:, :], row_sum[:, :]).then_inc(S1["rec"], 1)

            def x1_out(b):
                wait(eng, S1["xb"], b + 1)
                wait(eng, S1["y_ps"], b + 1)
                eng.tensor_tensor(X[:, b, :, :], bank(6).rearrange("p (r d) -> p r d", r=NT), X[:, b, :, :],
                                  ALU.add).then_inc(S1["x1"], 1)

            def router_stats(R, b, before):
                eng.wait_ge(before, b + 1).then_inc(gate_dve, 1)
                for r in range(NT):
                    eng.bn_stats(rt_st[:, r, :], X[:, b, r, :]).then_inc(R["stats"], 1)
                eng.wait_ge(R["stats"], NT * b + NT).then_inc(gate_dve, 1)
                for r in range(NT):
                    eng.bn_aggr(rt_mv[:, r, :], rt_st[:, r, :]).then_inc(R["aggr"], 1)

            def router_norm(R, b):
                wait(eng, R["pool"], 9 * b + 9)
                wait(eng, R["t_ps"], b)
                for r in range(NT):
                    eng.tensor_scalar(t0[:, r, :], X[:, b, r, :], rt_mv[:, r, 0:1], rt_small[:, 6, r:r + 1],
                                      ALU.subtract, ALU.mult).then_inc(R["t0"], 1)
                eng.wait_ge(R["t0"], NT * b + NT).then_inc(gate_dve, 1)
                for r in range(NT):
                    eng.tensor_scalar(X[:, b, r, :], X[:, b, r, :], rt_small[:, 7, r:r + 1], rt_small[:, 8, r:r + 1],
                                      ALU.mult, ALU.subtract).then_inc(R["xn"], 1)

            def router_lg(R, b, lg_bank):
                if isinstance(b, int) and b == 0:
                    eng.wait_ge(prep_sb, 3)
                wait(eng, R["lg_ps"], b + 1)
                eng.tensor_tensor(logits[:, :, 0:NE], lg_bank.rearrange("p (r e) -> p r e", r=NT),
                                  gate_b_all.unsqueeze(1).to_broadcast([P, NT, NE]), ALU.add).then_inc(R["lg"], 1)

            def router_top(R, b):
                sh, ex, mk, em, rt, rest = (rt_tmp[:, k, :, :] for k in range(6))
                eng.wait_ge(R["lg"], b + 1).then_inc(gate_dve, 1)
                for r in range(NT):
                    eng.max(top8[:, r, :], logits[:, r, 0:NE]).then_inc(R["max"], 1)
                wait(eng, R["max"], NT * b + NT)
                eng.memset(top8[:, :, TOPK:], LOWEST).then_inc(R["cut"], 1)
                wait(eng, R["exp"], b)
                eng.tensor_tensor(sh, logits[:, :, 0:NE], top8[:, :, 0:1].to_broadcast([P, NT, NE]),
                                  ALU.subtract).then_inc(R["shift"], 1)
                eng.wait_ge(R["cut"], b + 1).then_inc(gate_dve, 1)
                for r in range(NT):
                    eng.match_replace(replaced[:, r, :], top8[:, r, :], logits[:, r, :], LOWEST).then_inc(R["rep"], 1)
                wait(eng, R["rep"], NT * b + NT)
                eng.tensor_tensor(mk, replaced[:, :, 0:NE], logits[:, :, 0:NE], ALU.not_equal).then_inc(R["mask"], 1)

            def router_weights(R, b):
                sh, ex, mk, em, rt, rest = (rt_tmp[:, k, :, :] for k in range(6))
                wait(eng, R["mask"], b + 1)
                wait(eng, R["exp"], b + 1)
                eng.tensor_tensor(em, ex, mk, ALU.mult).then_inc(R["em"], 1)
                wait(eng, R["em"], b + 1)
                n = [0]

                def link(ins):
                    ins.then_inc(R["weights"], 1)
                    n[0] += 1
                    wait(eng, R["weights"], 6 * b + n[0])

                link(eng.tensor_reduce(rt_sum[:, 0, :], em, AX.X, ALU.add))
                link(eng.reciprocal(rt_sum[:, 1, :], rt_sum[:, 0, :]))
                link(eng.tensor_tensor(rt, em, rt_sum[:, 1, :].unsqueeze(2).to_broadcast([P, NT, NE]), ALU.mult))
                hi, mid, lo = (rt_parts[:, :, g, 0:NE] for g in range(PARTS))
                wait(eng, R["rt_ps"], b)
                link(eng.tensor_copy(hi, rt))
                link(eng.tensor_tensor(rest, rt, hi, ALU.subtract))
                link(eng.tensor_copy(mid, rest))
                eng.tensor_tensor(lo, rest, mid, ALU.subtract).then_inc(R["lo"], 1)

            eng.wait_ge(consts, N_CONST)
            eng.wait_ge(x_first, 16)

            def step(i, odd, first, second, third, fourth):
                if first:
                    ln1_stats(i + 1)
                if second:
                    maxes(i)
                if first:
                    xn_out(i + 1)
                if third:
                    x1_out(i - 1)
                    router_stats(R1, i - 1, S1["x1"])
                if second:
                    recip(i)
                if fourth:
                    router_lg(R1, i - 2, bank(7)[:, 0:NT * NE])
                    router_top(R1, i - 2)
                    router_weights(R1, i - 2)
                if third:
                    router_norm(R1, i - 1)

            def expert_weights_1():
                for quad in range(NE // 4):
                    eng.wait_ge(prep2_hi, quad + 1)
                    eng.tensor_tensor(w1_lo[:, 4 * quad:4 * quad + 4, :], bank(quad).rearrange("d (e i) -> d e i", e=4),
                                      w1_hi[:, 4 * quad:4 * quad + 4, :].bitcast(F32), ALU.subtract).then_inc(prep2_sb, 1)

            def expert_weights_2():
                for quad in range(NE // 4):
                    eng.wait_ge(prep2_hi, 4 + quad + 1)
                    eng.scalar_tensor_tensor(out=w2_lo[:, 4 * quad:4 * quad + 4, :],
                                             in0=bank(quad).rearrange("i (e h) -> i e h", e=4), scalar=(LIMIT + 1.0) / ALPHA,
                                             in1=w2_hi[:, 4 * quad:4 * quad + 4, :].bitcast(F32), op0=ALU.mult,
                                             op1=ALU.subtract).then_inc(prep2_sb, 1)
                eng.wait_ge(w_ffn, 96)
                eng.tensor_copy(b2_parts[:, 0, :], b2_rows[:, :]).then_inc(b2_split, 1)
                eng.wait_ge(b2_split, 1)
                eng.tensor_tensor(b2_rest[:, 0, :], b2_rows[:, :], b2_parts[:, 0, :], ALU.subtract).then_inc(b2_split, 1)
                eng.wait_ge(b2_split, 2)
                eng.tensor_copy(b2_parts[:, 1, :], b2_rest[:, 0, :]).then_inc(b2_split, 1)
                eng.wait_ge(b2_split, 3)
                eng.tensor_tensor(b2_parts[:, 2, :], b2_rest[:, 0, :], b2_parts[:, 1, :], ALU.subtract).then_inc(b2_split, 1)
                eng.wait_ge(w_ssm, 96)
                for k, j in enumerate(PE_TILES):
                    for w in range(CONV_W):
                        eng.tensor_scalar(tap_rows[:, k, w, :], in_rows[:, 2 + j, :], conv_taps[:, j, w:w + 1], None,
                                          ALU.mult).then_inc(taps_ready, 1)
                for j in range(2):
                    eng.tensor_tensor(skip_diag[:, j, :].rearrange("c (h p) -> c h p", h=2),
                                      ident[:, :].rearrange("c (h p) -> c h p", h=2),
                                      vecs[:, VD + 2 * j:VD + 2 * j + 2].unsqueeze(2).to_broadcast([P, 2, HD]),
                                      ALU.mult).then_inc(taps_ready, 1)

            skew_pairs(eng, step, tail=(expert_weights_1, expert_weights_2))

            def split(F, b, e):
                wait(eng, F["hi"], NE * b + e + 1)
                wait(eng, F["out"], NE * b + e + 1 - NR)
                eng.tensor_tensor(s_lo[:, e % NR, :], s_ring[:, e % 2, :], s_hi[:, e % NR, :].bitcast(F32),
                                  ALU.subtract).then_inc(F["lo"], 1)

            def ffn(F, b, peeled, tail=False):
                for e in range(NE):
                    if e == 9 and (tail or not peeled):
                        wait(eng, F["back"], b)
                        eng.tensor_tensor(X[:, b - 1, :, :], bank(7).rearrange("p (r d) -> p r d", r=NT),
                                          X[:, b - 1, :, :], ALU.add).then_inc(F["x"], 1)
                    if not tail:
                        wait(eng, F["lo"], NE * b + e + 1 - 2)
                        wait(eng, F["act"], NE * b + e + 1)
                        wait(eng, F["rb"], NE * b + e + 1)
                        eng.scalar_tensor_tensor(out=s_ring[:, e % 2, :], in0=act_ring[:, e % 2, :],
                                                 scalar=top_col[:, 0:1], in1=bank(4 + e % 2), op0=ALU.min,
                                                 op1=ALU.mult).then_inc(F["s"], 1)
                        if e:
                            split(F, b, e - 1)
                    if e == 0 and (tail or not peeled):
                        split(F, b - 1, NE - 1)

            eng.wait_ge(prep2_sb, 10)
            ffn(F1, 0, True)
            ffn(F1, 1, False)
            with eng.Fori(2, NB) as b:
                ffn(F1, b, False)
            ffn(F1, NB, False, True)
            eng.wait_ge(prep3_sb, PREP3)
            eng.tensor_scalar(neg_A[:, :], neg_A[:, :], -1.0, None, ALU.mult).then_inc(taps_ready, 1)

            eng.wait_ge(F1["x"], NB)

            def ssm_stats(b):
                for r in range(NT):
                    eng.bn_stats(ln1_st[:, r, :], X[:, b, r, :]).then_inc(M["stats"], 1)
                eng.wait_ge(M["stats"], NT * b + NT).then_inc(gate_dve, 1)
                for r in range(NT):
                    eng.bn_aggr(ln1_mv[:, r, :], ln1_st[:, r, :]).then_inc(M["aggr"], 1)

            def ssm_xn(b):
                wait(eng, M["rstd"], 2 * b + 2)
                wait(eng, M["uT_ps"], b)
                for r in range(NT):
                    eng.tensor_scalar(xn[:, r, :], X[:, b, r, :], ln1_mv[:, r, 0:1], ln1_rs[:, r:r + 1],
                                      ALU.subtract, ALU.mult).then_inc(M["xn"], 1)

            def conv_taps_of(b, k):
                j = DVE_TILES[k]
                wait(eng, M["tap"], 2 * b + k + 1)
                for s in range(1, CONV_W):
                    eng.scalar_tensor_tensor(out=conv_acc[:, j, s:], in0=bank(6 + k)[:, 0:SEQ - s],
                                             scalar=conv_taps[:, j, CONV_W - 1 - s:CONV_W - s], in1=conv_acc[:, j, s:],
                                             op0=ALU.mult, op1=ALU.add).then_inc(M["conv"], 1)
                    if s < CONV_W - 1:
                        wait(eng, M["conv"], 6 * b + 3 * k + s)

            def dt_arg(b):
                wait(eng, M["dt_ps"], b + 1)
                eng.tensor_tensor(dt_tmp[:, 0, :].rearrange("p (c h) -> p c h", h=NH),
                                  bank(4)[:, 0:NT * NH].rearrange("p (c h) -> p c h", h=NH),
                                  vecs[:, VDT:VDT + NH].unsqueeze(1).to_broadcast([P, NT, NH]), ALU.add).then_inc(M["dt_x"], 1)
                wait(eng, M["dt_x"], b + 1)
                eng.scalar_tensor_tensor(out=dt_tmp[:, 1, :], in0=dt_tmp[:, 0, :], scalar=-1.0, in1=dt_tmp[:, 0, :],
                                         op0=ALU.mult, op1=ALU.min).then_inc(M["dt_m"], 1)

            def softplus(b, par):
                x_, m_, u_, w_, z_, z2, q_ = (dt_tmp[:, k, :] for k in range(7))
                n = [0]

                def link(ins):
                    ins.then_inc(M["log"], 1)
                    n[0] += 1
                    wait(eng, M["log"], 13 * b + n[0])

                wait(eng, M["dt_u"], b + 1)
                link(eng.tensor_scalar(w_, u_, 2.0, None, ALU.add))
                link(eng.reciprocal(w_, w_))
                link(eng.tensor_tensor(z_, u_, w_, ALU.mult))
                link(eng.tensor_tensor(z2, z_, z_, ALU.mult))
                link(eng.tensor_scalar(q_, z2, 1.0 / 15, None, ALU.mult))
                for k in (13, 11, 9, 7, 5, 3):
                    link(eng.scalar_tensor_tensor(out=q_, in0=q_, scalar=1.0 / k, in1=z2, op0=ALU.add, op1=ALU.mult))
                link(eng.scalar_tensor_tensor(out=q_, in0=q_, scalar=1.0, in1=z_, op0=ALU.add, op1=ALU.mult))
                link(eng.tensor_scalar(x_, x_, 0.0, None, ALU.max))
                wait(eng, M["gram"], NH * NT * (b - 1))
                wait(eng, M["ramp"], NT * (b - 1))
                wait(eng, M["dk_ps"], b - 1)
                eng.scalar_tensor_tensor(out=dt_a[:, par, 0, :, :].rearrange("p c h -> p (c h)"), in0=q_, scalar=2.0, in1=x_,
                                         op0=ALU.mult, op1=ALU.add).then_inc(M["dt"], 1)
                wait(eng, M["dt"], b + 1)
                eng.tensor_tensor(dt_a[:, par, 1, :, :], dt_a[:, par, 0, :, :],
                                  neg_A[:, :].unsqueeze(1).to_broadcast([P, NT, NH]), ALU.mult).then_inc(M["a"], 1)

            def grams(b, par, c):
                n = NT * b + c
                wait(eng, M["cb_ps"], n + 1)
                eng.tensor_tensor(cb[:, c % 2, :], bank(0)[:, 0:P], upto[:, :], ALU.mult).then_inc(M["cb"], 1)
                wait(eng, M["segs"], n + 1)
                wait(eng, M["xw"], (NT - 1) * b + max(c - 1, 0))
                eng.tensor_tensor(to_end[:, c % 2, :], segs[:, c % 2, :, P - 1], dt_a[:, par, 0, c, :],
                                  ALU.mult).then_inc(M["end"], 1)
                wait(eng, M["cb"], n + 1)
                wait(eng, M["y_ps"], n - 1)
                for h in range(NH):
                    eng.scalar_tensor_tensor(out=gram[:, c % 2, h, :], in0=segs[:, c % 2, h, :],
                                             scalar=dt_a[:, par, 0, c, h:h + 1], in1=cb[:, c % 2, :], op0=ALU.mult,
                                             op1=ALU.mult).then_inc(M["gram"], 1)

            def states(b, c):
                k = (NT - 1) * b + c
                wait(eng, M["st_ps"], k + 1)
                if c == 0:
                    wait(eng, M["y_ps"], NT * b)
                    eng.tensor_copy(state[:, 0, :], bank(4)[:, 0:DI]).then_inc(M["state"], 1)
                else:
                    wait(eng, M["state_d"], (NT - 2) * b + c)
                    eng.tensor_tensor(state[:, c % 2, :], bank(4)[:, 0:DI], state_d[:, :], ALU.add).then_inc(M["state"], 1)

            def ys(b, par, c):
                n = NT * b + c
                wait(eng, M["y_ps"], n + 1)
                if c == 0:
                    wait(eng, M["g"], n - 1)
                    eng.tensor_copy(y[:, c % 2, :], bank(3)[:, 0:DI]).then_inc(M["y"], 1)
                    return
                k = (NT - 1) * b + c
                wait(eng, M["decay"], b + 1)
                eng.tensor_tensor(y_off[:, :].rearrange("t (h p) -> t h p", h=NH),
                                  bank(3)[:, DI:2 * DI].rearrange("t (h p) -> t h p", h=NH),
                                  decay[:, par, 0, c, :].unsqueeze(2).to_broadcast([P, NH, HD]), ALU.mult).then_inc(M["y_off"], 1)
                wait(eng, M["y_off"], k)
                wait(eng, M["g"], n - 1)
                eng.tensor_tensor(y[:, c % 2, :], bank(3)[:, 0:DI], y_off[:, :], ALU.add).then_inc(M["y"], 1)

            def norms(b, c):
                n = NT * b + c
                wait(eng, M["rms"], 2 * n + 2)
                wait(eng, M["gT_ps"], n - 1)
                eng.tensor_scalar(gn[:, c % 2, :], g[:, c % 2, :], g_rs[:, 1, c:c + 1], None, ALU.mult).then_inc(M["gn"], 1)

            def x3_out(b):
                wait(eng, M["o_ps"], b + 1)
                eng.tensor_tensor(X[:, b, :, :], bank(4).rearrange("p (r d) -> p r d", r=NT), X[:, b, :, :],
                                  ALU.add).then_inc(M["x"], 1)

            def step(i, odd, first, second, third, fourth):
                if first:
                    ssm_stats(i + 1)
                if third:
                    norms(i - 1, 3)
                if first:
                    ssm_xn(i + 1)
                if second:
                    grams(i, odd, 0)
                if third:
                    x3_out(i - 1)
                if second:
                    grams(i, odd, 1)
                    states(i, 0)
                    ys(i, odd, 0)
                if first:
                    conv_taps_of(i + 1, 0)
                if fourth:
                    router_lg(R2, i - 2, bank(5)[:, 0:NT * NE])
                if first:
                    dt_arg(i + 1)
                if second:
                    norms(i, 0)
                if third:
                    router_stats(R2, i - 1, M["x"])
                if second:
                    states(i, 1)
                    ys(i, odd, 1)
                if first:
                    conv_taps_of(i + 1, 1)
                if second:
                    grams(i, odd, 2)
                    norms(i, 1)
                if first:
                    softplus(i + 1, 1 - odd)
                if second:
                    states(i, 2)
                    ys(i, odd, 2)
                    grams(i, odd, 3)
                if fourth:
                    router_top(R2, i - 2)
                if second:
                    norms(i, 2)
                if fourth:
                    router_weights(R2, i - 2)
                if second:
                    ys(i, odd, 3)
                if third:
                    router_norm(R2, i - 1)
            skew_pairs(eng, step)

            ffn(F2, 0, True)
            ffn(F2, 1, False)
            with eng.Fori(2, NB) as b:
                ffn(F2, b, False)
            ffn(F2, NB, False, True)

        @block.tensor
        def _(eng):
            eng.wait_ge(consts, N_CONST + 1)
            eng.wait_ge(w_attn, 3 * 16)
            eng.matmul(bank(0)[:, 0:D], qkv_rows[:, 0, :], qkv_rows[:, 1, :], start=True, stop=True).then_inc(prep_ps, 1)
            eng.transpose(bank(1)[:, 0:D], qkv_rows[:, 2, :], ident[:, :])
            eng.transpose(bank(1)[:, D:2 * D], proj_rows[:, :], ident[:, :])
            eng.transpose(bank(1)[:, 2 * D:2 * D + NE], gate_rows[:, :], ident[0:NE, 0:NE]).then_inc(prep_ps, 1)
            eng.wait_ge(w_vecs, 6 * 16)
            eng.matmul(bank(2)[:, 0:VEND], ones[0:1, :], vec_row[0:1, 0:VEND], start=True, stop=True).then_inc(prep_ps, 1)
            eng.wait_ge(prep_sb, 3)

            def scores(b, par):
                wait(eng, S1["q"], b + 1)
                wait(eng, S1["pT"], NT * b)
                for r in range(NT):
                    eng.matmul(bank(r), qT[:, par, r * P:(r + 1) * P], xnT[:, par, :], start=True,
                               stop=True).then_inc(S1["scores"], 1)

            def xn_turn(b):
                wait(eng, S1["xn"], NT * b + NT)
                wait(eng, S1["q"], b)
                for r in range(NT):
                    mm = eng.transpose(bank(4)[:, r * P:(r + 1) * P], xn[:, r, :], ident[:, :])
                mm.then_inc(S1["xnT_ps"], 1)

            def qv(b, par):
                wait(eng, S1["xnT"], b + 1)
                eng.matmul(bank(4), a_qk[:, :], xnT[:, par, :], start=True, stop=True).then_inc(S1["q_ps"], 1)
                wait(eng, S1["x1"], b - 1)
                for t in range(NT):
                    mm = eng.matmul(bank(6)[:, t * D:(t + 1) * D], xnT[:, par, t * P:(t + 1) * P], wvT, start=True, stop=True)
                mm.then_inc(S1["v_ps"], 1)

            def p_turn(b):
                for r in range(NT):
                    wait(eng, S1["probs"], NT * b + r + 1)
                    for t in range(NT):
                        mm = eng.transpose(bank(r)[:, t * P:(t + 1) * P], probs[:, r, t * P:(t + 1) * P], ident[:, :])
                    mm.then_inc(S1["pT_ps"], 1)

            def pv(b, par, rs):
                wait(eng, S1["v"], b + 1)
                wait(eng, S1["o"], NT * b)
                for r in rs:
                    wait(eng, S1["pT"], NT * b + r + 1)
                    for t in range(NT):
                        mm = eng.matmul(bank(5)[:, r * D:(r + 1) * D], probsT[:, r, t, :], v[:, par, t, :],
                                        start=(t == 0), stop=(t == NT - 1))
                    if r == NT - 1:
                        mm.then_inc(S1["o_ps"], 1)

            def project(b):
                wait(eng, S1["o"], NT * b + NT)
                wait(eng, S1["v"], least(b + 2, NB))
                for r in range(NT):
                    mm = eng.matmul(bank(6)[:, r * D:(r + 1) * D], attn[:, r, :], wpT, start=True, stop=True)
                mm.then_inc(S1["y_ps"], 1)

            def router_turn(R, b, at, bank_free):
                wait(eng, R["t0"], NT * b + NT)
                bank_free()
                for r in range(NT):
                    mm = eng.transpose(bank(at)[:, r * P:(r + 1) * P], t0[:, r, :], ident[:, :])
                mm.then_inc(R["t_ps"], 1)

            def router_logits(R, b, lg_bank, bank_free):
                wait(eng, R["t"], b + 1)
                bank_free()
                for r in range(NT):
                    mm = eng.matmul(lg_bank[:, r * NE:(r + 1) * NE], tT[:, r * P:(r + 1) * P], gateT, start=True, stop=True)
                mm.then_inc(R["lg_ps"], 1)

            def router_parts(R, b, rt_bank, bank_free):
                wait(eng, R["lo"], b + 1)
                bank_free()
                for r in range(NT):
                    mm = eng.transpose(rt_bank.bitcast(BF16)[0:PARTS * PSTEP, r * P:(r + 1) * P],
                                       rt_parts[:, r, :, :].rearrange("p g e -> p (g e)"), ident_b[:, :])
                mm.then_inc(R["rt_ps"], 1)

            def step(i, odd, first, second, third, fourth):
                if second:
                    scores(i, odd)
                if third:
                    project(i - 1)
                if fourth:
                    router_turn(R1, i - 2, 7, lambda: wait(eng, R1["route"], i - 2))
                if second:
                    p_turn(i)
                if first:
                    xn_turn(i + 1)
                if fourth:
                    router_logits(R1, i - 2, bank(7), lambda: None)
                if second:
                    pv(i, odd, (0, 1))
                if first:
                    qv(i + 1, 1 - odd)
                if second:
                    pv(i, odd, (2, 3))
                if fourth:
                    router_parts(R1, i - 2, bank(7), lambda: wait(eng, R1["lg"], i - 1))

            def expert_weights_1():
                eng.wait_ge(w_ffn, 96)
                eng.wait_ge(S1["pT"], NT * NB)
                for quad in range(NE // 4):
                    for k in range(4):
                        mm = eng.transpose(bank(quad)[:, k * P:(k + 1) * P], w1_rows[:, 4 * quad + k, :], ident[:, :])
                    mm.then_inc(prep2_ps, 1)

            def expert_weights_2():
                for quad in range(NE // 4):
                    eng.wait_ge(prep2_sb, quad + 1)
                    for k in range(4):
                        mm = eng.transpose(bank(quad)[:, k * P:(k + 1) * P], w2_rows[:, 4 * quad + k, :], ident[:, :])
                    mm.then_inc(prep2_ps, 1)

                eng.wait_ge(taps_ready, PH * CONV_W)
                eng.wait_ge(prep2_sb, NE // 2)
                for k in range(PH):
                    for w in range(CONV_W):
                        mm = eng.transpose(bank(k)[:, w * P:(w + 1) * P], tap_rows[:, k, w, :], ident[:, :])
                    mm.then_inc(prep3_ps, 1)
                for k, j in enumerate((2 + DVE_TILES[0], 2 + DVE_TILES[1], 0, 1)):
                    mm = eng.transpose(bank(2)[:, k * P:(k + 1) * P], in_rows[:, j, :], ident[:, :])
                mm.then_inc(prep3_ps, 1)
                eng.transpose(bank(3)[:, 0:NH], dt_rows[:, :], ident[0:NH, 0:NH])
                eng.transpose(bank(3)[:, NH:NH + NJ + 2], col_rows[:, :], ident[0:NJ + 2, 0:NJ + 2])
                for j in range(2):
                    mm = eng.transpose(bank(3)[:, (j + 1) * P:(j + 2) * P], out_rows[:, j * P:(j + 1) * P], ident[:, :])
                mm.then_inc(prep3_ps, 1)

            skew_pairs(eng, step, tail=(expert_weights_1, expert_weights_2))

            eng.wait_ge(R1["route"], NB)
            eng.transpose(bank(4)[:, 0:NE], b1_rows[:, 0:2 * I:2], ident[0:NE, 0:NE]).then_inc(prep2_ps, 1)

            def ffn_out(F, b, e):
                wait(eng, F["lo"], NE * b + e + 1)
                if e == 0:
                    wait(eng, F["acc_sb"], b)
                    for g in range(PARTS):
                        eng.matmul(bank(6), b2_parts[:, g, :], route[:, b, :], start=(g == 0), stop=False)
                eng.matmul(bank(6), w2_hi[:, e, :], s_hi[:, e % NR, :], start=False, stop=False)
                eng.matmul(bank(6), w2_hi[:, e, :], s_lo[:, e % NR, :], start=False, stop=False)
                eng.matmul(bank(6), w2_lo[:, e, :], s_hi[:, e % NR, :], start=False, stop=(e == NE - 1)).then_inc(F["out"], 1)

            LAG = 3

            def ffn(F, b, peeled, tail=False):
                for e in range(NE):
                    if not tail:
                        wait(eng, F["act"], NE * b + e + 1 - 4)
                        eng.matmul(bank(e % 4), w1_hi[:, e, :], ffn_hi[:, b, :], start=True, stop=False)
                        eng.matmul(bank(e % 4), w1_hi[:, e, :], ffn_lo[:, b, :], start=False, stop=False)
                        eng.matmul(bank(e % 4), w1_lo[:, e, :], ffn_hi[:, b, :], start=False, stop=True).then_inc(F["h"], 1)
                        wait(eng, F["s"], NE * b + e + 1 - 2)
                        eng.matmul(bank(4 + e % 2), pick[:, e, :], route[:, b, :], start=True,
                                   stop=True).then_inc(F["rb"], 1)
                    if e >= LAG:
                        if not tail:
                            ffn_out(F, b, e - LAG)
                    elif tail or not peeled:
                        ffn_out(F, b - 1, NE - LAG + e)
                    if e == 6 and (tail or not peeled):
                        wait(eng, F["acc_sb"], b)
                        wait(eng, F["x"], b - 1)
                        for r in range(NT):
                            mm = eng.transpose(bank(7)[:, r * P:(r + 1) * P], acc_sb[:, r * P:(r + 1) * P], ident[:, :])
                        mm.then_inc(F["back"], 1)

            eng.wait_ge(prep2_sb, 10)
            eng.wait_ge(b2_split, 4)
            eng.wait_ge(R1["stash"], NB)
            ffn(F1, 0, True)
            ffn(F1, 1, False)
            with eng.Fori(2, NB) as b:
                ffn(F1, b, False)
            ffn(F1, NB, False, True)
            eng.wait_ge(F1["act"], NE * NB)
            eng.wait_ge(F1["s"], NE * NB)
            eng.wait_ge(F1["acc_sb"], NB)
            eng.wait_ge(F1["x"], NB)
            eng.wait_ge(prep3_sb, PREP3)

            def u_turn(b):
                wait(eng, M["xn"], NT * b + NT)
                wait(eng, M["z_raw"], 2 * b)
                for r in range(NT):
                    mm = eng.transpose(bank(7)[:, r * P:(r + 1) * P], xn[:, r, :], ident[:, :])
                mm.then_inc(M["uT_ps"], 1)

            def project_in(b, k):
                wait(eng, M["uT"], b + 1)
                if k == 0:
                    wait(eng, R2["t"], b - 2)
                eng.matmul(bank(6 + k), bcT[:, k, :], uT[:, :], start=True, stop=True).then_inc(M["cv_ps"], 1)

            def conv(b, k):
                wait(eng, M["conv"], 6 * b + 3 * (k + 1))
                for s in range(CONV_W):
                    mm = eng.matmul(bank(6 + k)[:, s:], tapT[:, k, CONV_W - 1 - s, :], uT[:, 0:SEQ - s],
                                    start=(s == 0), stop=(s == CONV_W - 1), skip_group_check=True)
                mm.then_inc(M["cv_ps"], 1)

            def z_proj(b, k):
                wait(eng, M["raw"], 2 * b + k + 1)
                for c in range(2):
                    mm = eng.matmul(bank(6 + k)[:, c * DI:(c + 1) * DI], uT[:, (2 * k + c) * P:(2 * k + c + 1) * P], zT[:, :],
                                    start=True, stop=True)
                mm.then_inc(M["z_ps"], 1)

            def dt_proj(b):
                wait(eng, M["state"], (NT - 1) * (b - 1) + 1)
                for c in range(NT):
                    mm = eng.matmul(bank(4)[:, c * NH:(c + 1) * NH], uT[:, c * P:(c + 1) * P], dtT[:, :],
                                    start=True, stop=True)
                mm.then_inc(M["dt_ps"], 1)

            def decay_sums(b, par):
                wait(eng, M["a"], b + 1)
                wait(eng, M["state"], (NT - 1) * b)
                a_all = dt_a[:, par, 1, :, :].rearrange("p c h -> p (c h)")
                eng.matmul(bank(4)[:, 0:NT * NH], upto[:, :], a_all, start=True, stop=True)
                eng.matmul(bank(4)[:, NT * NH:2 * NT * NH], ones[:, :], a_all, start=True,
                           stop=True).then_inc(M["dk_ps"], 1)

            def front(b, par, c):
                n = NT * b + c
                at = slice(c * P, (c + 1) * P)
                if c == 0:
                    wait(eng, M["xs"], b + 1)
                wait(eng, M["cb"], n)
                eng.matmul(bank(0)[:, 0:P], xs[:, par, 2, at], xs[:, par, 3, at], start=True,
                           stop=True).then_inc(M["cb_ps"], 1)
                wait(eng, M["xb"], n)
                for j in range(3):
                    mm = eng.transpose(bank(1)[:, j * P:(j + 1) * P], xs[:, par, j, at], ident[:, :])
                mm.then_inc(M["xb_ps"], 1)
                wait(eng, M["segs"], n)
                wait(eng, M["ramp"], n + 1)
                eng.matmul(bank(2), after[:, :], ramp[:, c % 2, :, :].rearrange("k h t -> k (h t)"), start=True,
                           stop=True).then_inc(M["seg_ps"], 1)

            def back(b, par, c):
                n = NT * b + c
                at = slice(c * P, (c + 1) * P)
                wait(eng, M["y"], n)
                for j in range(2):
                    eng.matmul(bank(3)[:, j * P:(j + 1) * P], xs[:, par, j, at], skip_diag[:, j, :], start=(j == 0), stop=False,
                               skip_group_check=True)
                if c:
                    wait(eng, M["state"], (NT - 1) * b + c)
                    eng.matmul(bank(3)[:, DI:2 * DI], xs[:, par, 3, at], state[:, (c - 1) % 2, :], start=False, stop=True,
                               skip_group_check=True)
                wait(eng, M["gram"], NH * (n + 1))
                for h in range(NH):
                    mm = eng.matmul(bank(3)[:, h * HD:(h + 1) * HD], gram[:, c % 2, h, :],
                                    xb_tok[:, c % 2, h // 2, (h % 2) * HD:(h % 2 + 1) * HD], start=False, stop=(h == NH - 1),
                                    skip_group_check=True)
                mm.then_inc(M["y_ps"], 1)
                if c < NT - 1:
                    k = (NT - 1) * b + c
                    if c == 0:
                        wait(eng, M["x"], b)
                        wait(eng, M["decay"], b + 1)
                    if c == 1:
                        wait(eng, M["dt_x"], least(b + 2, NB))
                    wait(eng, M["state"], k)
                    wait(eng, M["xw"], k + 1)
                    eng.matmul(bank(4)[:, 0:DI], xb_tok[:, c % 2, 2, :], xw[:, c % 2, :], start=True,
                               stop=True).then_inc(M["st_ps"], 1)

            def g_turn(b, c):
                n = NT * b + c
                wait(eng, M["gn"], n + 1)
                wait(eng, M["gT"], n)
                if c == 0:
                    wait(eng, R2["lg"], b - 1)
                if c == NT - 1:
                    wait(eng, R2["route"], b - 1)
                for j in range(2):
                    mm = eng.transpose(bank(5)[:, j * P:(j + 1) * P], gn[:, c % 2, j * P:(j + 1) * P], ident[:, :])
                mm.then_inc(M["gT_ps"], 1)

            def out_proj(b):
                wait(eng, M["gT"], NT * b + NT)
                wait(eng, M["x"], b)
                wait(eng, M["decay"], least(b + 2, NB))
                wait(eng, M["state"], (NT - 1) * (b + 1))
                for r in range(NT):
                    for j in range(2):
                        mm = eng.matmul(bank(4)[:, r * D:(r + 1) * D], gT[:, j, r:SEQ:NT], outT[:, j, :], start=(j == 0),
                                        stop=(j == 1))
                mm.then_inc(M["o_ps"], 1)

            def step(i, odd, first, second, third, fourth):
                if second:
                    front(i, odd, 0)
                if fourth:
                    router_turn(R2, i - 2, 6, lambda: (wait(eng, M["z_raw"], least(2 * i + 1, 2 * NB - 1)), wait(eng, R2["t"], i - 2)))
                if third:
                    g_turn(i - 1, 3)
                    out_proj(i - 1)
                if second:
                    front(i, odd, 1)
                if first:
                    u_turn(i + 1)
                if second:
                    back(i, odd, 0)
                if first:
                    project_in(i + 1, 0)
                    project_in(i + 1, 1)
                    dt_proj(i + 1)
                if fourth:
                    router_logits(R2, i - 2, bank(5), lambda: wait(eng, M["gT"], least(NT * i, NT * NB)))
                if second:
                    front(i, odd, 2)
                    back(i, odd, 1)
                    g_turn(i, 0)
                if first:
                    conv(i + 1, 0)
                if second:
                    front(i, odd, 3)
                    back(i, odd, 2)
                    g_turn(i, 1)
                if first:
                    z_proj(i + 1, 0)
                    conv(i + 1, 1)
                    decay_sums(i + 1, 1 - odd)
                if second:
                    back(i, odd, 3)
                if first:
                    z_proj(i + 1, 1)
                if second:
                    g_turn(i, 2)
                if fourth:
                    router_parts(R2, i - 2, bank(5), lambda: wait(eng, M["gT"], least(NT * i + 3, NT * NB)))
            skew_pairs(eng, step)

            eng.wait_ge(R2["stash"], NB)
            eng.wait_ge(R2["route"], NB)
            eng.wait_ge(R2["xn"], NT * NB)
            eng.wait_ge(M["x"], NB)
            eng.wait_ge(M["y"], NB * NT)
            ffn(F2, 0, True)
            ffn(F2, 1, False)
            with eng.Fori(2, NB) as b:
                ffn(F2, b, False)
            ffn(F2, NB, False, True)


_INS = ['L0_attn_a_x', 'L0_attn_a_w_qkv', 'L0_attn_a_w_proj', 'L0_attn_a_b_proj', 'L0_attn_b_W_in', 'L0_attn_b_conv_w',
        'L0_attn_b_conv_b', 'L0_attn_b_dt_bias', 'L0_attn_b_A_log', 'L0_attn_b_D', 'L0_attn_b_norm_w', 'L0_attn_b_W_out',
        'L0_ffn_scale', 'L0_ffn_gate_w', 'L0_ffn_gate_b', 'L0_ffn_mlp1_w', 'L0_ffn_mlp1_b', 'L0_ffn_mlp2_w', 'L0_ffn_mlp2_b']


def kernel(**inputs):
    import concourse.bacc as bacc
    from concourse.bass_utils import run_bass_kernel_spmd
    nc = bacc.Bacc("TRN2", target_bir_lowering=False, num_devices=1)
    ins = {name: np.ascontiguousarray(np.asarray(inputs[name])) for name in _INS}
    drams = [nc.dram_tensor(f"in_{name}_dram", ins[name].shape, F32, kind="ExternalInput").ap() for name in _INS]
    out = nc.dram_tensor("out_dram", (NB, SEQ, D), F32, kind="ExternalOutput").ap()
    build(nc, *drams, out)
    arrays = {f"in_{name}_dram": ins[name] for name in _INS}
    return run_bass_kernel_spmd(nc, [arrays], core_ids=[0]).results[0]["out_dram"]
```

```python
from contextlib import ExitStack

import numpy as np
import concourse.bass as bass
from concourse import mybir

F32 = mybir.dt.float32
F32R = mybir.dt.float32r
BF16 = mybir.dt.bfloat16
ALU = mybir.AluOpType
ACT = mybir.ActivationFunctionType
AX = mybir.AxisListType

P = 128
NB = 8
SEQ = 512
NT = SEQ // P
D = 128
NE = 16
TOPK = 4
I = 128
HEAD = 8
LN_EPS = 1e-5
ALPHA = 1.702
LIMIT = 7.0
CONV_W = 4
PAD = CONV_W
NH = 4
HD = 64
DI = NH * HD
NJ = 4
PARTS = 3
PSTEP = 32
LOWEST = -3.0e38
PE_TILES = (0, 1)
DVE_TILES = (2, 3)


def build(nc, x, w_qkv, w_proj, b_proj, W_in, conv_w, conv_b, dt_bias, A_log, Dskip, norm_w, W_out,
          ffn_scale, gate_w, gate_b, mlp1_w, mlp1_b, mlp2_w, mlp2_b, out):
    with ExitStack() as ctx:
        def sb(name, shape, dt=F32):
            return ctx.enter_context(nc.sbuf_tensor(name, shape, dt))

        def sem(name):
            return ctx.enter_context(nc.semaphore(name))

        X = sb("X", [P, NB, NT, D])
        ffn_hi = sb("ffn_hi", [P, NB, SEQ], F32R)
        ffn_lo = sb("ffn_lo", [P, NB, SEQ], F32R)
        route = sb("route", [PARTS * PSTEP, NB, SEQ], BF16)
        ident = sb("ident", [P, P])
        ident_b = sb("ident_b", [P, P], BF16)
        ones = sb("ones", [P, P])
        upto = sb("upto", [P, P])
        after = sb("after", [P, P])
        pick = sb("pick", [PARTS * PSTEP, NE, P], BF16)
        eps4 = sb("eps4", [P, NT])
        mhalf4 = sb("mhalf4", [P, NT])
        limit_col = sb("limit_col", [P, 1])
        top_col = sb("top_col", [P, 1])
        gate_rows = sb("gate_rows", [NE, D])
        vec_row = sb("vec_row", [1, 160])
        scale_col = sb("scale_col", [P, 1])
        b1_rows = sb("b1_rows", [NE, 2 * I])
        b2_rows = sb("b2_rows", [PARTS * PSTEP, D])
        a_qk = sb("a_qk", [P, D])
        vpg = sb("vpg", [P, 2 * D + NE])
        wvT, wpT, gateT = vpg[:, 0:D], vpg[:, D:2 * D], vpg[:, 2 * D:]
        vecs = sb("vecs", [P, 160])
        w1_hi = sb("w1_hi", [P, NE, I], F32R)
        w1_lo = sb("w1_lo", [P, NE, I], F32R)
        w2_hi = sb("w2_hi", [P, NE, D], F32R)
        w2_lo = sb("w2_lo", [P, NE, D], F32R)
        b1T = sb("b1T", [P, NE])
        b2_parts = sb("b2_parts", [PARTS * PSTEP, PARTS, D], BF16)
        ln1_st = sb("ln1_st", [P, NT, 6])
        ln1_mv = sb("ln1_mv", [P, NT, 2])
        ln1_ve = sb("ln1_ve", [P, NT])
        ln1_rs = sb("ln1_rs", [P, NT])
        xn = sb("xn", [P, NT, D])
        rt_st = sb("rt_st", [P, NT, 6])
        rt_mv = sb("rt_mv", [P, NT, 2])
        rt_small = sb("rt_small", [P, 9, NT])
        t0 = sb("t0", [P, NT, D])
        tT = sb("tT", [P, SEQ])
        acc_sb = tT
        logits = sb("logits", [P, NT, NE + TOPK])
        replaced = sb("replaced", [P, NT, NE + TOPK])
        top8 = sb("top8", [P, NT, 8])
        rt_tmp = sb("rt_tmp", [P, 6, NT, NE])
        rt_sum = sb("rt_sum", [P, 2, NT])
        rt_parts = sb("rt_parts", [P, NT, PARTS, PSTEP], BF16)
        in_rows = sb("in_rows", [P, 6, D])
        dt_rows = sb("dt_rows", [NH, D])
        out_rows = sb("out_rows", [P, DI])
        conv_taps = sb("conv_taps", [P, NJ, CONV_W])
        col_rows = sb("col_rows", [NJ + 2, P])
        cols = sb("cols", [P, NJ + 2])
        conv_bias, norm_col = cols[:, 0:NJ], cols[:, NJ:]
        tapT = sb("tapT", [P, 2, len(PE_TILES), CONV_W, P], F32R)
        bcT = sb("bcT", [P, 2, len(DVE_TILES), P], F32R)
        zT = sb("zT", [P, 2, DI], F32R)
        dtT = sb("dtT", [P, 2, NH], F32R)
        outT = sb("outT", [P, 2, D])
        skip_diag = sb("skip_diag", [P, 2, P])
        neg_A = sb("neg_A", [P, NH])

        with ExitStack() as stage:
            def own(name, shape, dt=F32):
                return stage.enter_context(nc.sbuf_tensor(name, shape, dt))

            proj_rows = own("proj_rows", [P, D])
            qkv_rows = own("qkv_rows", [P, 3, D])
            xnT = own("xnT", [P, 2, SEQ])
            qT = own("qT", [P, 2, SEQ])
            v = own("v", [P, 2, NT, D])
            probs = own("probs", [P, NT, SEQ])
            probsT = own("probsT", [P, NT, NT, P])
            attn = own("attn", [P, NT, D])
            w2_rows = own("w2_rows", [P, NE, I])
            w1_rows = own("w1_rows", [P, NE, D])
            tap_rows = w1_rows.rearrange("p (k w) d -> p k w d", w=CONV_W)
            neg_max = own("neg_max", [P, NT])
            row_sum = own("row_sum", [P, NT])
            row_rec = own("row_rec", [P, NT])
        with ExitStack() as stage:
            NR = 4
            act_ring = own("act_ring", [P, 2, SEQ])
            s_ring = own("s_ring", [P, 2, SEQ])
            s_hi = own("s_hi", [P, NR, SEQ], F32R)
            s_lo = own("s_lo", [P, NR, SEQ], F32R)
            b2_rest = own("b2_rest", [PARTS * PSTEP, 2, D])
        with ExitStack() as stage:
            uT = own("uT", [P, 2, PAD + SEQ], F32R)
            conv_acc = own("conv_acc", [P, NJ, SEQ])
            xs = own("xs", [P, 2, NJ, SEQ])
            zs = own("zs", [P, 2, NT, DI])
            dt_tmp = own("dt_tmp", [P, 7, NT * NH])
            dt_a = own("dt_a", [P, 2, 2, NT, NH])
            decay = own("decay", [P, 2, 2, NT, NH])
            ramp = own("ramp", [P, 2, NH, P])
            segs = own("segs", [P, 2, NH, P])
            cb = own("cb", [P, 2, P])
            gram = own("gram", [P, 2, NH, P])
            xb_tok = own("xb_tok", [P, 2, 3, P])
            to_end = own("to_end", [P, 2, NH])
            xw = own("xw", [P, 2, DI])
            state = own("state", [P, 2, DI])
            state_d = own("state_d", [P, DI])
            y_off = own("y_off", [P, DI])
            y = own("y", [P, 2, DI])
            g = own("g", [P, 2, DI])
            g_sq = own("g_sq", [P, DI])
            table_col = own("table_col", [P, 2])
            g_ss = own("g_ss", [P, NT])
            g_rs = own("g_rs", [P, 2, NT])
            gn = own("gn", [P, 2, DI])
            gT = own("gT", [P, 2, SEQ])

        ps = ctx.enter_context(nc.psum_tensor("ps", [P, 8, 512], F32))

        def bank(i):
            return ps[:, i, :]

        x_first = sem("x_first")
        x_rest = sem("x_rest")
        w_attn = sem("w_attn")
        w_vecs = sem("w_vecs")
        w_ffn = sem("w_ffn")
        consts = sem("consts")
        consts_late = sem("consts_late")
        cleared = sem("cleared")
        prep_ps = sem("prep_ps")
        prep_sb = sem("prep_sb")
        prep2_ps = sem("prep2_ps")
        prep2_sb = sem("prep2_sb")
        prep2_hi = sem("prep2_hi")
        b2_split = sem("b2_split")
        stored = sem("stored")
        gate_pool = sem("gate_pool")
        gate_dve = sem("gate_dve")
        gate_act = sem("gate_act")
        table = sem("table")
        N_CONST = 5
        N_LATE = 6

        VB, VG, VDT, VA, VD = 0, D, D + NE, D + NE + NH, D + NE + 2 * NH
        VEND = VD + NH
        b_proj_all = vecs[:, VB:VB + D]
        gate_b_all = vecs[:, VG:VG + NE]

        S1 = {n: sem("attn_" + n) for n in (
            "stats", "aggr", "rstd", "xn", "xnT_ps", "xnT", "q_ps", "q", "v_ps", "v", "scores", "max", "probs",
            "pT_ps", "pT", "o_ps", "rec", "o", "y_ps", "xb", "x1")}

        def router_sems(tag):
            return {n: sem(tag + n) for n in (
                "stats", "aggr", "pool", "t0", "xn", "t_ps", "t", "t_hi", "stash", "lg_ps", "lg", "max", "cut", "shift",
                "rep", "mask", "exp", "em", "weights", "lo", "rt_ps", "route")}

        def ffn_sems(tag):
            return {n: sem(tag + n) for n in ("h", "rb", "act", "s", "hi", "lo", "out", "acc_sb", "back", "x")}

        R1, R2 = router_sems("router1_"), router_sems("router2_")
        F1, F2 = ffn_sems("ffn1_"), ffn_sems("ffn2_")
        M = {n: sem("ssm_" + n) for n in (
            "stats", "aggr", "rstd", "xn", "uT_ps", "uT", "u_lo", "cv_ps", "tap", "conv", "raw", "xs", "z_ps",
            "z_raw", "zs", "dt_ps", "dt_x", "dt_m", "dt_u", "log", "dt", "a", "dk_ps", "decay", "ramp", "cb_ps", "cb",
            "xb_ps", "xb", "seg_ps", "segs", "gram", "end", "xw", "st_ps", "state_d", "state", "y_ps", "y_off", "y",
            "g", "sq", "rms", "gn", "gT_ps", "gT", "o_ps", "x")}
        w_ssm = sem("w_ssm")
        taps_ready = sem("taps_ready")
        prep3_ps = sem("prep3_ps")
        prep3_sb = sem("prep3_sb")
        prep3_hi = sem("prep3_hi")

        block = ctx.enter_context(nc.Block())

        PREP3 = 6
        B1 = NH + NJ + 2
        PH = len(PE_TILES)

        def wait(eng, s, value):
            if isinstance(value, int) and value <= 0:
                return
            eng.wait_ge(s, value)

        def skew_pairs(eng, step, before={}):
            for i in range(-1, 3):
                if i in before:
                    before[i]()
                step(i, i % 2, True, i >= 0, i >= 1, i >= 2)
            with eng.Fori(3, NB - 2, 2) as i:
                step(i, 1, True, True, True, True)
                step(i + 1, 0, True, True, True, True)
            step(NB - 1, (NB - 1) % 2, False, True, True, True)

        def least(a, cap):
            return min(a, cap) if isinstance(a, int) else a

        @block.sync
        def _(eng):
            eng.dma_start(X[:, 0, :, :], x[0].rearrange("(p r) d -> p r d", r=NT)).then_inc(x_first, 16)
            eng.dma_start(qkv_rows[:, :, :], w_qkv.rearrange("(m p) d -> p m d", p=P)).then_inc(w_attn, 16)
            eng.dma_start(proj_rows[:, :], w_proj).then_inc(w_attn, 16)
            eng.dma_start(gate_rows[:, :], gate_w).then_inc(w_attn, 16)
            eng.dma_start(X[:, 1:NB, :, :], x[1:NB].rearrange("b (p r) d -> p b r d", r=NT)).then_inc(x_rest, 16)
            eng.dma_start(w1_rows[:, :, :], mlp1_w.rearrange("e (i two) d -> i two e d", two=2)[:, 0]).then_inc(w_ffn, 16)
            eng.dma_start(w2_rows[:, :, :], mlp2_w.rearrange("e h i -> h e i")).then_inc(w_ffn, 16)
            eng.dma_start(b1_rows[:, :], mlp1_b).then_inc(w_ffn, 16)
            eng.dma_start(in_rows[:, :, :], W_in[0:6 * P].rearrange("(m p) d -> p m d", p=P)).then_inc(w_ssm, 16)
            eng.dma_start(dt_rows[:, :], W_in[6 * P:]).then_inc(w_ssm, 16)
            eng.dma_start(out_rows[:, :], W_out).then_inc(w_ssm, 16)
            eng.dma_start(conv_taps[:, :, :], conv_w.rearrange("(j p) w -> p j w", p=P)).then_inc(w_ssm, 16)
            eng.dma_start(col_rows[0:NJ, :], conv_b.rearrange("(j p) -> j p", p=P)).then_inc(w_ssm, 16)
            eng.dma_start(col_rows[NJ:NJ + 2, :], norm_w.rearrange("(j p) -> j p", p=P)).then_inc(w_ssm, 16)
            eng.wait_ge(cleared, 6)
            for g in range(PARTS):
                eng.dma_start(b2_rows[g * PSTEP:g * PSTEP + NE, :], mlp2_b).then_inc(w_ffn, 16)
            with eng.Fori(0, NB) as b:
                eng.wait_ge(F2["x"], b + 1)
                eng.dma_start(out[b].rearrange("(p r) d -> p r d", r=NT), X[:, b, :, :]).then_inc(stored, 16)
            eng.wait_ge(stored, 16 * NB)

        @block.gpsimd
        def _(eng):
            c = [0, 0]

            def const(ins, late=0):
                ins.then_inc((consts, consts_late)[late], 1)
                c[late] += 1

            const(eng.memset(ident[:, :], 0.0))
            const(eng.memset(ones[:, :], 1.0))
            const(eng.memset(eps4[:, :], LN_EPS))
            const(eng.memset(mhalf4[:, :], -0.5))
            eng.wait_ge(consts, c[0])
            const(eng.affine_select(out=ident[:, :], in_=ident[:, :], compare_op=ALU.not_equal, fill=1.0, base=0,
                                    pattern=[[-1, P]], channel_multiplier=1))
            assert c[0] == N_CONST

            def late_constants():
                const(eng.affine_select(out=upto[:, :], in_=ones[:, :], compare_op=ALU.is_ge, fill=0.0, base=0,
                                        pattern=[[1, P]], channel_multiplier=-1), 1)
                const(eng.affine_select(out=after[:, :], in_=ones[:, :], compare_op=ALU.is_gt, fill=0.0, base=0,
                                        pattern=[[-1, P]], channel_multiplier=1), 1)
                eng.wait_ge(cleared, 6)
                const(eng.affine_select(out=ident_b[:, :], in_=ident_b[:, :], compare_op=ALU.not_equal, fill=1.0, base=0,
                                        pattern=[[-1, P]], channel_multiplier=1), 1)
                for part in range(PARTS):
                    eng.wait_ge(consts_late, c[1])
                    const(eng.affine_select(out=pick[:, :, :], in_=pick[:, :, :], compare_op=ALU.not_equal, fill=1.0,
                                            base=-part * PSTEP, pattern=[[-1, NE], [0, P]], channel_multiplier=1), 1)
                assert c[1] == N_LATE

            def ssm_weights():
                eng.wait_ge(w_ssm, 96)
                eng.wait_ge(prep_sb, 3)
                eng.wait_ge(prep2_ps, NE // 4)
                for k, j in enumerate(PE_TILES):
                    eng.tensor_tensor(tap_rows[:, k, :, :], in_rows[:, 2 + j, :].unsqueeze(1).to_broadcast([P, CONV_W, D]),
                                      conv_taps[:, j, :].unsqueeze(2).to_broadcast([P, CONV_W, D]),
                                      ALU.mult).then_inc(taps_ready, 1)
                for j in range(2):
                    eng.tensor_tensor(skip_diag[:, j, :].rearrange("c (h p) -> c h p", h=2),
                                      ident[:, :].rearrange("c (h p) -> c h p", h=2),
                                      vecs[:, VD + 2 * j:VD + 2 * j + 2].unsqueeze(2).to_broadcast([P, 2, HD]),
                                      ALU.mult).then_inc(taps_ready, 1)

            def router_chain(R, b):
                n = [0]

                def tt(o, a, bb, op):
                    eng.tensor_tensor(o, a, bb, op).then_inc(R["pool"], 1)
                    n[0] += 1
                    wait(eng, R["pool"], 9 * b + n[0])

                var = rt_mv[:, :, 1]
                wait(eng, R["aggr"], NT * b + NT)
                wait(eng, R["xn"], NT * b)
                tt(rt_small[:, 0, :], var, eps4[:, :], ALU.add)
                tt(rt_small[:, 1, :], rt_small[:, 0, :], mhalf4[:, :], ALU.pow)
                tt(rt_small[:, 2, :], rt_small[:, 1, :], rt_small[:, 1, :], ALU.mult)
                tt(rt_small[:, 3, :], rt_small[:, 2, :], var, ALU.mult)
                tt(rt_small[:, 4, :], rt_small[:, 3, :], eps4[:, :], ALU.add)
                tt(rt_small[:, 5, :], rt_small[:, 4, :], mhalf4[:, :], ALU.pow)
                tt(rt_small[:, 6, :], rt_small[:, 5, :], rt_small[:, 1, :], ALU.mult)
                tt(rt_small[:, 7, :], rt_small[:, 1, :], ones[:, 0:NT], ALU.add)
                eng.tensor_tensor(rt_small[:, 8, :], rt_small[:, 1, :], rt_mv[:, :, 0], ALU.mult).then_inc(R["pool"], 1)

            def router_stash(R, b):
                eng.wait_ge(R["t"], b + 1).then_inc(gate_pool, 1)
                eng.wait_ge(R["t_hi"], b + 1).then_inc(gate_pool, 1)
                eng.tensor_tensor(ffn_lo[:, b, :], tT[:, :], ffn_hi[:, b, :].bitcast(F32),
                                  ALU.subtract).then_inc(R["stash"], 1)

            def ln1_chain(b):
                wait(eng, S1["aggr"], NT * b + NT)
                wait(eng, S1["xn"], NT * b)
                eng.tensor_tensor(ln1_ve[:, :], ln1_mv[:, :, 1], eps4[:, :], ALU.add).then_inc(S1["rstd"], 1)
                wait(eng, S1["rstd"], 2 * b + 1)
                eng.tensor_tensor(ln1_rs[:, :], ln1_ve[:, :], mhalf4[:, :], ALU.pow).then_inc(S1["rstd"], 1)

            def add_bias(b):
                eng.wait_ge(S1["xn"], NT * b + NT).then_inc(gate_pool, 1)
                if isinstance(b, int) and b == 0:
                    eng.wait_ge(prep_sb, 3)
                eng.tensor_tensor(X[:, b, :, :], X[:, b, :, :],
                                  b_proj_all.unsqueeze(1).to_broadcast([P, NT, D]), ALU.add).then_inc(S1["xb"], 1)

            eng.wait_ge(consts, N_CONST)

            def step(i, odd, first, second, third, fourth):
                if first:
                    ln1_chain(i + 1)
                if third:
                    router_chain(R1, i - 1)
                if first:
                    add_bias(i + 1)
                if fourth:
                    router_stash(R1, i - 2)
            skew_pairs(eng, step, before={1: late_constants, 2: ssm_weights})

            def router_end(R):
                router_stash(R, NB - 2)
                router_chain(R, NB - 1)
                router_stash(R, NB - 1)

            router_end(R1)

            def ssm_norm(b):
                wait(eng, M["aggr"], NT * b + NT)
                wait(eng, M["xn"], NT * b)
                eng.tensor_tensor(ln1_ve[:, :], ln1_mv[:, :, 1], eps4[:, :], ALU.add).then_inc(M["rstd"], 1)
                wait(eng, M["rstd"], 2 * b + 1)
                eng.tensor_tensor(ln1_rs[:, :], ln1_ve[:, :], mhalf4[:, :], ALU.pow).then_inc(M["rstd"], 1)

            def ramps(b, par, c):
                n = NT * b + c
                wait(eng, M["seg_ps"], n - 1)
                wait(eng, M["a"], b + 1)
                eng.tensor_tensor(ramp[:, c % 2, :, :], upto[:, :].unsqueeze(1).to_broadcast([P, NH, P]),
                                  dt_a[:, par, 1, c, :].unsqueeze(2).to_broadcast([P, NH, P]),
                                  ALU.mult).then_inc(M["ramp"], 1)

            def weigh(b, par, c):
                n = NT * b + c
                k = (NT - 1) * b + c
                wait(eng, M["xb"], n + 1)
                wait(eng, M["st_ps"], k - 1)
                wait(eng, M["end"], n + 1)
                eng.tensor_tensor(xw[:, c % 2, :].rearrange("s (h p) -> s h p", h=NH),
                                  xb_tok[:, c % 2, 0:2, :].rearrange("s j (h p) -> s (j h) p", p=HD),
                                  to_end[:, c % 2, :].unsqueeze(2).to_broadcast([P, NH, HD]),
                                  ALU.mult).then_inc(M["xw"], 1)
                if c:
                    wait(eng, M["state"], k)
                    eng.tensor_tensor(state_d[:, :].rearrange("n (h p) -> n h p", h=NH),
                                      state[:, (c - 1) % 2, :].rearrange("n (h p) -> n h p", h=NH),
                                      decay[:, par, 1, c, :].unsqueeze(2).to_broadcast([P, NH, HD]),
                                      ALU.mult).then_inc(M["state_d"], 1)

            def gate(b, par, c):
                n = NT * b + c
                wait(eng, M["y"], n + 1)
                wait(eng, M["gn"], n - 1)
                wait(eng, M["zs"], b + 1)
                eng.tensor_tensor(g[:, c % 2, :], y[:, c % 2, :], zs[:, par, c, :], ALU.mult).then_inc(M["g"], 1)

            def rms(b, c):
                n = NT * b + c
                wait(eng, M["sq"], n + 1)
                eng.tensor_tensor(g_rs[:, 0, c:c + 1], g_ss[:, c:c + 1], eps4[:, 0:1], ALU.add).then_inc(M["rms"], 1)
                wait(eng, M["rms"], 2 * n + 1)
                wait(eng, M["gn"], n - 3)
                eng.tensor_tensor(g_rs[:, 1, c:c + 1], g_rs[:, 0, c:c + 1], mhalf4[:, 0:1], ALU.pow).then_inc(M["rms"], 1)

            eng.wait_ge(prep3_sb, PREP3)

            def step(i, odd, first, second, third, fourth):
                if first:
                    ssm_norm(i + 1)
                if second:
                    weigh(i, odd, 0)
                    ramps(i, odd, 2)
                    gate(i, odd, 0)
                    weigh(i, odd, 1)
                    rms(i, 0)
                    ramps(i, odd, 3)
                if fourth:
                    router_stash(R2, i - 2)
                if second:
                    gate(i, odd, 1)
                    rms(i, 1)
                    weigh(i, odd, 2)
                    gate(i, odd, 2)
                if first:
                    ramps(i + 1, 1 - odd, 0)
                if second:
                    rms(i, 2)
                if third:
                    router_chain(R2, i - 1)
                if first:
                    ramps(i + 1, 1 - odd, 1)
                if second:
                    gate(i, odd, 3)
                    rms(i, 3)
            skew_pairs(eng, step)
            router_end(R2)

        @block.scalar
        def _(eng):
            for at, src in ((VB, b_proj), (VG, gate_b), (VDT, dt_bias), (VA, A_log), (VD, Dskip)):
                eng.dma_start(vec_row[0:1, at:at + src.shape[0]], src.rearrange("(a n) -> a n", a=1)).then_inc(w_vecs, 16)
            eng.dma_start(scale_col[:, :], ffn_scale.rearrange("(p a) -> p a", a=1)).then_inc(w_vecs, 16)
            eng.wait_ge(prep_ps, 1)
            eng.activation(a_qk[:, :], bank(0)[:, 0:D], ACT.Copy, scale=float(HEAD) ** -0.5).then_inc(prep_sb, 1)
            eng.wait_ge(prep_ps, 2)
            eng.activation(vpg[:, :], bank(1)[:, 0:2 * D + NE], ACT.Copy).then_inc(prep_sb, 1)
            eng.wait_ge(prep_ps, 3)
            eng.activation(vecs[:, 0:VEND], bank(2)[:, 0:VEND], ACT.Copy).then_inc(prep_sb, 1)

            def exps(b, rs):
                for r in rs:
                    wait(eng, S1["max"], NT * b + r + 1)
                    if r == 0:
                        wait(eng, S1["rec"], b)
                    wait(eng, S1["pT_ps"], NT * (b - 1) + r + 1)
                    eng.activation(probs[:, r, :], bank(r), ACT.Exp, bias=neg_max[:, r:r + 1],
                                   accum_out=row_sum[:, r:r + 1]).then_inc(S1["probs"], 1)

            def pT(b, rs):
                for r in rs:
                    wait(eng, S1["pT_ps"], NT * b + r + 1)
                    wait(eng, S1["o_ps"], b)
                    eng.activation(probsT[:, r, :, :], bank(r).rearrange("k (t q) -> k t q", t=NT),
                                   ACT.Copy).then_inc(S1["pT"], 1)

            def xnT_out(b, par):
                wait(eng, S1["xnT_ps"], b + 1)
                wait(eng, S1["v_ps"], b - 1)
                wait(eng, S1["scores"], NT * (b - 1))
                eng.activation(xnT[:, par, :].rearrange("d (p r) -> d r p", r=NT),
                               bank(4).rearrange("d (r p) -> d r p", r=NT), ACT.Copy).then_inc(S1["xnT"], 1)

            def q_out(b, par):
                wait(eng, S1["q_ps"], b + 1)
                wait(eng, S1["scores"], NT * (b - 1))
                eng.activation(qT[:, par, :], bank(4), ACT.Copy).then_inc(S1["q"], 1)

            def v_out(b, par):
                wait(eng, S1["v_ps"], b + 1)
                wait(eng, S1["o_ps"], b - 1)
                eng.activation(v[:, par, :, :], bank(6).rearrange("k (t h) -> k t h", t=NT), ACT.Copy).then_inc(S1["v"], 1)

            def attn_out(b):
                wait(eng, S1["rec"], b + 1)
                wait(eng, S1["o_ps"], b + 1)
                wait(eng, S1["y_ps"], b)
                for r in range(NT):
                    eng.activation(attn[:, r, :], bank(5)[:, r * D:(r + 1) * D], ACT.Copy,
                                   scale=row_rec[:, r:r + 1]).then_inc(S1["o"], 1)

            def router_t(R, b, at):
                wait(eng, R["t_ps"], b + 1)
                wait(eng, R["lg_ps"], b)
                wait(eng, R["stash"], b)
                eng.activation(tT[:, :], bank(at), ACT.Copy, scale=scale_col[:, 0:1]).then_inc(R["t"], 1)
                eng.wait_ge(R["t"], b + 1).then_inc(gate_act, 1)
                eng.activation(ffn_hi[:, b, :], tT[:, :], ACT.Copy).then_inc(R["t_hi"], 1)

            def router_exp(R, b):
                wait(eng, R["shift"], b + 1)
                wait(eng, R["em"], b)
                eng.activation(rt_tmp[:, 1, :, :], rt_tmp[:, 0, :, :], ACT.Exp).then_inc(R["exp"], 1)

            def router_out(R, b, rt_bank):
                eng.wait_ge(R["rt_ps"], b + 1).then_inc(gate_act, 1)
                eng.activation(route[:, b, :], rt_bank.bitcast(BF16)[0:PARTS * PSTEP, 0:SEQ],
                               ACT.Copy).then_inc(R["route"], 1)

            def step(i, odd, first, second, third, fourth):
                if second:
                    exps(i, (0, 1))
                    exps(i, (2, 3))
                if fourth:
                    router_t(R1, i - 2, 7)
                if second:
                    pT(i, range(NT))
                if first:
                    xnT_out(i + 1, 1 - odd)
                if fourth:
                    router_exp(R1, i - 2)
                if first:
                    q_out(i + 1, 1 - odd)
                if second:
                    attn_out(i)
                if fourth:
                    router_out(R1, i - 2, bank(7))
                if first:
                    v_out(i + 1, 1 - odd)

            def expert_weights_1():
                for quad in range(NE // 4):
                    eng.wait_ge(prep2_ps, quad + 1)
                    eng.activation(w1_hi[:, 4 * quad:4 * quad + 4, :], bank(quad).rearrange("d (e i) -> d e i", e=4),
                                   ACT.Copy).then_inc(prep2_hi, 1)

            def expert_weights_2():
                for quad in range(NE // 4):
                    eng.wait_ge(prep2_ps, 4 + quad + 1)
                    eng.activation(w2_hi[:, 4 * quad:4 * quad + 4, :], bank(quad).rearrange("i (e h) -> i e h", e=4),
                                   ACT.Copy, scale=(LIMIT + 1.0) / ALPHA).then_inc(prep2_hi, 1)

                for k in range(PH):
                    eng.wait_ge(prep3_ps, k + 1)
                    eng.activation(tapT[:, 0, k, :, :], bank(k).rearrange("d (w c) -> d w c", w=CONV_W),
                                   ACT.Copy).then_inc(prep3_hi, 1)
                eng.wait_ge(prep3_ps, PH + 1)
                eng.activation(bcT[:, 0, :, :], bank(2)[:, 0:2 * P].rearrange("d (j c) -> d j c", j=2),
                               ACT.Copy).then_inc(prep3_hi, 1)
                eng.activation(zT[:, 0, :], bank(2)[:, 2 * P:4 * P], ACT.Copy).then_inc(prep3_hi, 1)
                eng.wait_ge(prep3_ps, PH + 2)
                eng.activation(dtT[:, 0, :], bank(3)[:, 0:NH], ACT.Copy).then_inc(prep3_hi, 1)
                eng.activation(b1T[:, :], bank(3)[:, B1:B1 + NE], ACT.Copy, scale=ALPHA).then_inc(prep3_hi, 1)
                eng.activation(cols[:, :], bank(3)[:, NH:NH + NJ + 2], ACT.Copy).then_inc(prep3_hi, 1)
                eng.wait_ge(prep3_hi, PH + 5)
                for j in range(2):
                    eng.activation(outT[:, j, :], bank(3)[:, P * (j + 1):P * (j + 2)], ACT.Copy,
                                   scale=norm_col[:, j:j + 1]).then_inc(prep3_hi, 1)
                eng.activation(neg_A[:, :], vecs[:, VA:VA + NH], ACT.Exp).then_inc(prep3_sb, 1)

            skew_pairs(eng, step, before={1: expert_weights_1, 2: expert_weights_2})

            def router_rest(R, e):
                if e == 4:
                    router_out(R, NB - 2, bank(7))
                elif e == 9:
                    router_t(R, NB - 1, 7)
                elif e == 12:
                    router_exp(R, NB - 1)
                elif e == 15:
                    router_out(R, NB - 1, bank(7))

            router_t(R1, NB - 2, 7)
            router_exp(R1, NB - 2)
            eng.wait_ge(cleared, 6)
            eng.activation(top_col[:, :], limit_col[:, :], ACT.Silu, scale=ALPHA).then_inc(prep2_sb, 1)

            def split(F, b, e):
                wait(eng, F["s"], NE * b + e + 1)
                wait(eng, F["out"], NE * b + e + 1 - NR)
                wait(eng, F["lo"], NE * b + e + 1 - NR)
                eng.activation(s_hi[:, e % NR, :], s_ring[:, e % 2, :], ACT.Copy).then_inc(F["hi"], 1)

            def ffn(F, b, peeled, tail=False, after_expert=None):
                for e in range(NE):
                    if e == 3 and (tail or not peeled):
                        wait(eng, F["out"], NE * b)
                        wait(eng, F["back"], b - 1)
                        eng.activation(acc_sb[:, :], bank(6), ACT.Copy).then_inc(F["acc_sb"], 1)
                    if not tail:
                        wait(eng, F["h"], NE * b + e + 1)
                        wait(eng, F["s"], NE * b + e + 1 - 2)
                        eng.activation(act_ring[:, e % 2, :], bank(e % 4), ACT.Silu, bias=b1T[:, e:e + 1],
                                       scale=ALPHA).then_inc(F["act"], 1)
                        if e:
                            split(F, b, e - 1)
                    if e == 0 and (tail or not peeled):
                        split(F, b - 1, NE - 1)
                    if after_expert:
                        after_expert(e)

            eng.wait_ge(prep2_sb, 9)
            eng.wait_ge(prep3_sb, PREP3)
            ffn(F1, 0, True, after_expert=lambda e: router_rest(R1, e))
            ffn(F1, 1, False)
            with eng.Fori(2, NB) as b:
                ffn(F1, b, False)
            ffn(F1, NB, False, True)
            eng.wait_ge(prep3_sb, PREP3)

            def u_out(b):
                wait(eng, M["uT_ps"], b + 1)
                wait(eng, M["cv_ps"], NJ * b)
                wait(eng, M["dt_ps"], b)
                wait(eng, M["z_ps"], 2 * b)
                eng.activation(uT[:, 0, PAD:].rearrange("d (p r) -> d r p", r=NT),
                               bank(7).rearrange("d (r p) -> d r p", r=NT), ACT.Copy).then_inc(M["uT"], 1)

            def conv_first(b, k):
                j = DVE_TILES[k]
                wait(eng, M["cv_ps"], NJ * b + k + 1)
                wait(eng, M["xs"], 3 * b)
                eng.activation(conv_acc[:, j, :], bank(7 - k), ACT.Identity, bias=conv_bias[:, j:j + 1],
                               scale=conv_taps[:, j, CONV_W - 1:CONV_W]).then_inc(M["tap"], 1)

            def conv_out(b):
                j = PE_TILES[0]
                wait(eng, M["cv_ps"], NJ * b + 3)
                wait(eng, M["xs"], 3 * b)
                eng.activation(conv_acc[:, j, :], bank(7), ACT.Identity, bias=conv_bias[:, j:j + 1]).then_inc(M["raw"], 1)

            def xs_silu(b, par):
                wait(eng, M["conv"], 6 * b + 6)
                wait(eng, M["raw"], b + 1)
                wait(eng, M["y_ps"], NT * (b - 1))
                for first, count in ((PE_TILES[0], 1), (DVE_TILES[0], len(DVE_TILES))):
                    eng.activation(xs[:, par, first:first + count, :], conv_acc[:, first:first + count, :],
                                   ACT.Silu).then_inc(M["xs"], 1)

            def xs_last(b, par):
                j = PE_TILES[1]
                wait(eng, M["cv_ps"], NJ * b + 4)
                wait(eng, M["y_ps"], NT * (b - 1))
                eng.activation(xs[:, par, j, :], bank(6), ACT.Silu, bias=conv_bias[:, j:j + 1]).then_inc(M["xs"], 1)

            def z_out(b, par, k):
                wait(eng, M["z_ps"], 2 * b + k + 1)
                wait(eng, M["g"], NT * (b - 1))
                eng.activation(zs[:, par, 2 * k:2 * k + 2, :], bank(6 + k).rearrange("t (c e) -> t c e", c=2),
                               ACT.Copy).then_inc(M["z_raw"], 1)

            def z_silu(b, par):
                wait(eng, M["z_raw"], 2 * b + 2)
                eng.activation(zs[:, par, :, :], zs[:, par, :, :], ACT.Silu).then_inc(M["zs"], 1)

            def table_of(func, at):
                eng.activation(table_col[:, at:at + 1], ones[:, 0:1], func).then_inc(table, 1)

            def dt_exp(b):
                wait(eng, M["dt_m"], b + 1)
                wait(eng, M["a"], b)
                eng.activation(dt_tmp[:, 2, :], dt_tmp[:, 1, :], ACT.Exp).then_inc(M["dt_u"], 1)

            def decays(b, par):
                wait(eng, M["dk_ps"], b + 1)
                wait(eng, M["y_off"], (NT - 1) * (b - 1))
                wait(eng, M["state_d"], (NT - 2) * (b - 1))
                eng.activation(decay[:, par, :, :, :],
                               bank(4)[:, 0:2 * NT * NH].rearrange("p (k c h) -> p k c h", k=2, c=NT),
                               ACT.Exp).then_inc(M["decay"], 1)

            def xb_out(b, c):
                n = NT * b + c
                k = (NT - 1) * b + max(c - 1, 0)
                wait(eng, M["xb_ps"], n + 1)
                wait(eng, M["y_ps"], n - 1)
                wait(eng, M["st_ps"], k)
                wait(eng, M["xw"], k)
                eng.activation(xb_tok[:, c % 2, :, :], bank(1)[:, 0:3 * P].rearrange("t (j c) -> t j c", j=3),
                               ACT.Copy).then_inc(M["xb"], 1)

            def seg_exp(b, c):
                n = NT * b + c
                wait(eng, M["seg_ps"], n + 1)
                wait(eng, M["gram"], NH * (n - 1))
                wait(eng, M["end"], n - 1)
                eng.activation(segs[:, c % 2, :, :], bank(2).rearrange("s (h t) -> s h t", h=NH),
                               ACT.Exp).then_inc(M["segs"], 1)

            def square(b, c):
                n = NT * b + c
                wait(eng, M["g"], n + 1)
                wait(eng, M["sq"], n)
                wait(eng, M["rms"], 2 * (n - 3))
                eng.activation(g_sq[:, :], g[:, c % 2, :], ACT.Square, scale=float(DI) ** -0.5,
                               accum_out=g_ss[:, c:c + 1]).then_inc(M["sq"], 1)

            def gT_out(b, c):
                n = NT * b + c
                wait(eng, M["gT_ps"], n + 1)
                wait(eng, M["o_ps"], b)
                eng.activation(gT[:, :, c * P:(c + 1) * P], bank(5)[:, 0:2 * P].rearrange("e (j t) -> e j t", j=2),
                               ACT.Copy).then_inc(M["gT"], 1)

            def step(i, odd, first, second, third, fourth):
                if second:
                    seg_exp(i, 0)
                    xb_out(i, 0)
                    seg_exp(i, 1)
                    xb_out(i, 1)
                if third:
                    gT_out(i - 1, 3)
                if first:
                    u_out(i + 1)
                    conv_first(i + 1, 0)
                if second:
                    square(i, 0)
                if first:
                    conv_first(i + 1, 1)
                if fourth:
                    router_t(R2, i - 2, 5)
                if second:
                    xb_out(i, 2)
                    seg_exp(i, 2)
                if first:
                    dt_exp(i + 1)
                if second:
                    square(i, 1)
                if first:
                    conv_out(i + 1)
                if second:
                    xb_out(i, 3)
                    seg_exp(i, 3)
                if first:
                    z_out(i + 1, 1 - odd, 0)
                if second:
                    square(i, 2)
                if first:
                    z_out(i + 1, 1 - odd, 1)
                if second:
                    gT_out(i, 0)
                    gT_out(i, 1)
                if first:
                    decays(i + 1, 1 - odd)
                if fourth:
                    router_exp(R2, i - 2)
                if first:
                    xs_silu(i + 1, 1 - odd)
                    table_of(ACT.Silu, 0)
                    z_silu(i + 1, 1 - odd)
                    xs_last(i + 1, 1 - odd)
                if second:
                    gT_out(i, 2)
                if first:
                    table_of(ACT.Exp, 1)
                if second:
                    square(i, 3)
                if fourth:
                    router_out(R2, i - 2, bank(5))
            skew_pairs(eng, step)
            router_t(R2, NB - 2, 7)
            gT_out(NB - 1, NT - 1)
            router_exp(R2, NB - 2)

            ffn(F2, 0, True, after_expert=lambda e: router_rest(R2, e))
            ffn(F2, 1, False)
            with eng.Fori(2, NB) as b:
                ffn(F2, b, False)
            ffn(F2, NB, False, True)

        @block.vector
        def _(eng):
            def ln1_stats(b):
                if isinstance(b, int) and b == 1:
                    eng.wait_ge(x_rest, 16)
                for r in range(NT):
                    eng.bn_stats(ln1_st[:, r, :], X[:, b, r, :]).then_inc(S1["stats"], 1)
                eng.wait_ge(S1["stats"], NT * b + NT).then_inc(gate_dve, 1)
                for r in range(NT):
                    eng.bn_aggr(ln1_mv[:, r, :], ln1_st[:, r, :]).then_inc(S1["aggr"], 1)

            def xn_out(b):
                wait(eng, S1["rstd"], 2 * b + 2)
                wait(eng, S1["xnT_ps"], b)
                for r in range(NT):
                    eng.tensor_scalar(xn[:, r, :], X[:, b, r, :], ln1_mv[:, r, 0:1], ln1_rs[:, r:r + 1],
                                      ALU.subtract, ALU.mult).then_inc(S1["xn"], 1)

            def maxes(b):
                for r in range(NT):
                    wait(eng, S1["scores"], NT * b + r + 1)
                    wait(eng, S1["probs"], NT * (b - 1) + r + 1)
                    eng.tensor_reduce(neg_max[:, r:r + 1], bank(r), AX.X, ALU.max, negate=True).then_inc(S1["max"], 1)

            def recip(b):
                wait(eng, S1["probs"], NT * b + NT)
                wait(eng, S1["o"], NT * b)
                eng.reciprocal(row_rec[:, :], row_sum[:, :]).then_inc(S1["rec"], 1)

            def x1_out(b):
                wait(eng, S1["xb"], b + 1)
                wait(eng, S1["y_ps"], b + 1)
                eng.tensor_tensor(X[:, b, :, :], bank(6).rearrange("p (r d) -> p r d", r=NT), X[:, b, :, :],
                                  ALU.add).then_inc(S1["x1"], 1)

            def router_stats(R, b, before):
                eng.wait_ge(before, b + 1).then_inc(gate_dve, 1)
                for r in range(NT):
                    eng.bn_stats(rt_st[:, r, :], X[:, b, r, :]).then_inc(R["stats"], 1)
                eng.wait_ge(R["stats"], NT * b + NT).then_inc(gate_dve, 1)
                for r in range(NT):
                    eng.bn_aggr(rt_mv[:, r, :], rt_st[:, r, :]).then_inc(R["aggr"], 1)

            def router_norm(R, b):
                wait(eng, R["pool"], 9 * b + 9)
                wait(eng, R["t_ps"], b)
                for r in range(NT):
                    eng.tensor_scalar(t0[:, r, :], X[:, b, r, :], rt_mv[:, r, 0:1], rt_small[:, 6, r:r + 1],
                                      ALU.subtract, ALU.mult).then_inc(R["t0"], 1)
                eng.wait_ge(R["t0"], NT * b + NT).then_inc(gate_dve, 1)
                for r in range(NT):
                    eng.tensor_scalar(X[:, b, r, :], X[:, b, r, :], rt_small[:, 7, r:r + 1], rt_small[:, 8, r:r + 1],
                                      ALU.mult, ALU.subtract).then_inc(R["xn"], 1)

            def router_lg(R, b, lg_bank):
                if isinstance(b, int) and b == 0:
                    eng.wait_ge(prep_sb, 3)
                wait(eng, R["lg_ps"], b + 1)
                eng.tensor_tensor(logits[:, :, 0:NE], lg_bank.rearrange("p (r e) -> p r e", r=NT),
                                  gate_b_all.unsqueeze(1).to_broadcast([P, NT, NE]), ALU.add).then_inc(R["lg"], 1)

            def router_top(R, b):
                sh, ex, mk, em, rt, rest = (rt_tmp[:, k, :, :] for k in range(6))
                eng.wait_ge(R["lg"], b + 1).then_inc(gate_dve, 1)
                for r in range(NT):
                    eng.max(top8[:, r, :], logits[:, r, 0:NE]).then_inc(R["max"], 1)
                wait(eng, R["max"], NT * b + NT)
                eng.memset(top8[:, :, TOPK:], LOWEST).then_inc(R["cut"], 1)
                wait(eng, R["exp"], b)
                eng.tensor_tensor(sh, logits[:, :, 0:NE], top8[:, :, 0:1].to_broadcast([P, NT, NE]),
                                  ALU.subtract).then_inc(R["shift"], 1)
                eng.wait_ge(R["cut"], b + 1).then_inc(gate_dve, 1)
                for r in range(NT):
                    eng.match_replace(replaced[:, r, :], top8[:, r, :], logits[:, r, :], LOWEST).then_inc(R["rep"], 1)
                wait(eng, R["rep"], NT * b + NT)
                eng.tensor_tensor(mk, replaced[:, :, 0:NE], logits[:, :, 0:NE], ALU.not_equal).then_inc(R["mask"], 1)

            def router_weights(R, b):
                sh, ex, mk, em, rt, rest = (rt_tmp[:, k, :, :] for k in range(6))
                wait(eng, R["mask"], b + 1)
                wait(eng, R["exp"], b + 1)
                eng.tensor_tensor(em, ex, mk, ALU.mult).then_inc(R["em"], 1)
                wait(eng, R["em"], b + 1)
                n = [0]

                def link(ins):
                    ins.then_inc(R["weights"], 1)
                    n[0] += 1
                    wait(eng, R["weights"], 6 * b + n[0])

                link(eng.tensor_reduce(rt_sum[:, 0, :], em, AX.X, ALU.add))
                link(eng.reciprocal(rt_sum[:, 1, :], rt_sum[:, 0, :]))
                link(eng.tensor_tensor(rt, em, rt_sum[:, 1, :].unsqueeze(2).to_broadcast([P, NT, NE]), ALU.mult))
                hi, mid, lo = (rt_parts[:, :, g, 0:NE] for g in range(PARTS))
                wait(eng, R["rt_ps"], b)
                link(eng.tensor_copy(hi, rt))
                link(eng.tensor_tensor(rest, rt, hi, ALU.subtract))
                link(eng.tensor_copy(mid, rest))
                eng.tensor_tensor(lo, rest, mid, ALU.subtract).then_inc(R["lo"], 1)

            for buffer, value in ((b2_rows[:, :], 0.0), (ident_b[:, :], 0.0), (limit_col[:, :], LIMIT),
                                  (logits[:, :, NE:], LOWEST), (rt_parts[:, :, :, :], 0.0), (pick[:, :, :], 0.0)):
                eng.memset(buffer, value).then_inc(cleared, 1)
            eng.wait_ge(x_first, 16)

            def step(i, odd, first, second, third, fourth):
                if first:
                    ln1_stats(i + 1)
                if second:
                    maxes(i)
                if third:
                    x1_out(i - 1)
                if first:
                    xn_out(i + 1)
                if third:
                    router_stats(R1, i - 1, S1["x1"])
                if second:
                    recip(i)
                if fourth:
                    router_lg(R1, i - 2, bank(7)[:, 0:NT * NE])
                    router_top(R1, i - 2)
                    router_weights(R1, i - 2)
                if third:
                    router_norm(R1, i - 1)

            def expert_weights_1():
                for quad in range(NE // 4):
                    eng.wait_ge(prep2_hi, quad + 1)
                    eng.tensor_tensor(w1_lo[:, 4 * quad:4 * quad + 4, :], bank(quad).rearrange("d (e i) -> d e i", e=4),
                                      w1_hi[:, 4 * quad:4 * quad + 4, :].bitcast(F32), ALU.subtract).then_inc(prep2_sb, 1)

            def expert_weights_2():
                for quad in range(NE // 4):
                    eng.wait_ge(prep2_hi, 4 + quad + 1)
                    eng.scalar_tensor_tensor(out=w2_lo[:, 4 * quad:4 * quad + 4, :],
                                             in0=bank(quad).rearrange("i (e h) -> i e h", e=4), scalar=(LIMIT + 1.0) / ALPHA,
                                             in1=w2_hi[:, 4 * quad:4 * quad + 4, :].bitcast(F32), op0=ALU.mult,
                                             op1=ALU.subtract).then_inc(prep2_sb, 1)

                for k in range(PH):
                    eng.wait_ge(prep3_hi, k + 1)
                    eng.tensor_tensor(tapT[:, 1, k, :, :], bank(k).rearrange("d (w c) -> d w c", w=CONV_W),
                                      tapT[:, 0, k, :, :].bitcast(F32), ALU.subtract).then_inc(prep3_sb, 1)
                eng.wait_ge(prep3_hi, PH + 3)
                eng.tensor_tensor(bcT[:, 1, :, :], bank(2)[:, 0:2 * P].rearrange("d (j c) -> d j c", j=2),
                                  bcT[:, 0, :, :].bitcast(F32), ALU.subtract).then_inc(prep3_sb, 1)
                eng.tensor_tensor(zT[:, 1, :], bank(2)[:, 2 * P:4 * P], zT[:, 0, :].bitcast(F32),
                                  ALU.subtract).then_inc(prep3_sb, 1)
                eng.wait_ge(prep3_hi, PH + 7)
                eng.tensor_tensor(dtT[:, 1, :], bank(3)[:, 0:NH], dtT[:, 0, :].bitcast(F32),
                                  ALU.subtract).then_inc(prep3_sb, 1)

            skew_pairs(eng, step, before={1: expert_weights_1, 2: expert_weights_2})

            def router_rest(R, e):
                if e == 1:
                    router_weights(R, NB - 2)
                elif e == 6:
                    router_norm(R, NB - 1)
                elif e == 11:
                    router_lg(R, NB - 1, bank(7)[:, 0:NT * NE])
                    router_top(R, NB - 1)
                elif e == 13:
                    router_weights(R, NB - 1)

            x1_out(NB - 1)
            router_stats(R1, NB - 1, S1["x1"])
            eng.wait_ge(w_ffn, 96)
            eng.tensor_copy(b2_parts[:, 0, :], b2_rows[:, :]).then_inc(b2_split, 1)
            eng.wait_ge(b2_split, 1)
            eng.tensor_tensor(b2_rest[:, 0, :], b2_rows[:, :], b2_parts[:, 0, :], ALU.subtract).then_inc(b2_split, 1)
            eng.wait_ge(b2_split, 2)
            eng.tensor_copy(b2_parts[:, 1, :], b2_rest[:, 0, :]).then_inc(b2_split, 1)
            eng.wait_ge(b2_split, 3)
            eng.tensor_tensor(b2_parts[:, 2, :], b2_rest[:, 0, :], b2_parts[:, 1, :], ALU.subtract).then_inc(b2_split, 1)
            router_lg(R1, NB - 2, bank(7)[:, 0:NT * NE])
            router_top(R1, NB - 2)

            def split(F, b, e):
                wait(eng, F["hi"], NE * b + e + 1)
                wait(eng, F["out"], NE * b + e + 1 - NR)
                eng.tensor_tensor(s_lo[:, e % NR, :], s_ring[:, e % 2, :], s_hi[:, e % NR, :].bitcast(F32),
                                  ALU.subtract).then_inc(F["lo"], 1)

            def ssm_stats(b, early=False):
                if isinstance(b, int) and b == 0 and not early:
                    return
                eng.wait_ge(F1["x"], b + 1).then_inc(gate_dve, 1)
                for r in range(NT):
                    eng.bn_stats(ln1_st[:, r, :], X[:, b, r, :]).then_inc(M["stats"], 1)
                eng.wait_ge(M["stats"], NT * b + NT).then_inc(gate_dve, 1)
                for r in range(NT):
                    eng.bn_aggr(ln1_mv[:, r, :], ln1_st[:, r, :]).then_inc(M["aggr"], 1)

            def ssm_xn(b, early=False):
                if isinstance(b, int) and b == 0 and not early:
                    return
                wait(eng, M["rstd"], 2 * b + 2)
                wait(eng, M["uT_ps"], b)
                for r in range(NT):
                    eng.tensor_scalar(xn[:, r, :], X[:, b, r, :], ln1_mv[:, r, 0:1], ln1_rs[:, r:r + 1],
                                      ALU.subtract, ALU.mult).then_inc(M["xn"], 1)

            def add_sum(F, b, at):
                wait(eng, F["back"], b + 1)
                eng.tensor_tensor(X[:, b, :, :], bank(at).rearrange("p (r d) -> p r d", r=NT),
                                  X[:, b, :, :], ALU.add).then_inc(F["x"], 1)

            def ffn(F, b, peeled, tail=False, after_expert=None):
                for e in range(NE):
                    if e == 9 and not tail and not peeled:
                        add_sum(F, b - 1, 7)
                    if not tail:
                        wait(eng, F["lo"], NE * b + e + 1 - 2)
                        wait(eng, F["act"], NE * b + e + 1)
                        wait(eng, F["rb"], NE * b + e + 1)
                        eng.scalar_tensor_tensor(out=s_ring[:, e % 2, :], in0=act_ring[:, e % 2, :],
                                                 scalar=top_col[:, 0:1], in1=bank(4 + e % 2), op0=ALU.min,
                                                 op1=ALU.mult).then_inc(F["s"], 1)
                        if e:
                            split(F, b, e - 1)
                    if e == 0 and (tail or not peeled):
                        split(F, b - 1, NE - 1)
                    if after_expert:
                        after_expert(e)

            eng.wait_ge(prep2_sb, 9)
            ffn(F1, 0, True, after_expert=lambda e: router_rest(R1, e))
            ffn(F1, 1, False)
            ssm_stats(0, early=True)
            with eng.Fori(2, NB) as b:
                ffn(F1, b, False)
            ssm_xn(0, early=True)
            ffn(F1, NB, False, True)
            eng.wait_ge(prep3_sb, PREP3)
            eng.tensor_scalar(neg_A[:, :], neg_A[:, :], -1.0, None, ALU.mult).then_inc(taps_ready, 1)


            def u_low(b):
                if isinstance(b, int) and b == 0:
                    eng.memset(uT[:, :, 0:PAD].bitcast(F32), 0.0).then_inc(taps_ready, 1)
                wait(eng, M["uT"], b + 1)
                wait(eng, M["cv_ps"], NJ * b)
                wait(eng, M["dt_ps"], b)
                wait(eng, M["z_ps"], 2 * b)
                eng.tensor_tensor(uT[:, 1, PAD:].rearrange("d (p r) -> d r p", r=NT),
                                  bank(7).rearrange("d (r p) -> d r p", r=NT),
                                  uT[:, 0, PAD:].bitcast(F32).rearrange("d (p r) -> d r p", r=NT),
                                  ALU.subtract).then_inc(M["u_lo"], 1)

            def conv_taps_of(b, k):
                j = DVE_TILES[k]
                wait(eng, M["tap"], 2 * b + k + 1)
                for s in range(1, CONV_W):
                    eng.scalar_tensor_tensor(out=conv_acc[:, j, s:], in0=bank(7 - k)[:, 0:SEQ - s],
                                             scalar=conv_taps[:, j, CONV_W - 1 - s:CONV_W - s], in1=conv_acc[:, j, s:],
                                             op0=ALU.mult, op1=ALU.add).then_inc(M["conv"], 1)
                    if s < CONV_W - 1:
                        wait(eng, M["conv"], 6 * b + 3 * k + s)

            def dt_arg(b):
                wait(eng, M["dt_ps"], b + 1)
                eng.tensor_tensor(dt_tmp[:, 0, :].rearrange("p (c h) -> p c h", h=NH),
                                  bank(4)[:, 0:NT * NH].rearrange("p (c h) -> p c h", h=NH),
                                  vecs[:, VDT:VDT + NH].unsqueeze(1).to_broadcast([P, NT, NH]), ALU.add).then_inc(M["dt_x"], 1)
                wait(eng, M["dt_x"], b + 1)
                eng.scalar_tensor_tensor(out=dt_tmp[:, 1, :], in0=dt_tmp[:, 0, :], scalar=-1.0, in1=dt_tmp[:, 0, :],
                                         op0=ALU.mult, op1=ALU.min).then_inc(M["dt_m"], 1)

            def softplus(b, par):
                x_, m_, u_, w_, z_, z2, q_ = (dt_tmp[:, k, :] for k in range(7))
                n = [0]

                def link(ins):
                    ins.then_inc(M["log"], 1)
                    n[0] += 1
                    wait(eng, M["log"], 13 * b + n[0])

                wait(eng, M["dt_u"], b + 1)
                link(eng.tensor_scalar(w_, u_, 2.0, None, ALU.add))
                link(eng.reciprocal(w_, w_))
                link(eng.tensor_tensor(z_, u_, w_, ALU.mult))
                link(eng.tensor_tensor(z2, z_, z_, ALU.mult))
                link(eng.tensor_scalar(q_, z2, 1.0 / 15, None, ALU.mult))
                for k in (13, 11, 9, 7, 5, 3):
                    link(eng.scalar_tensor_tensor(out=q_, in0=q_, scalar=1.0 / k, in1=z2, op0=ALU.add, op1=ALU.mult))
                link(eng.scalar_tensor_tensor(out=q_, in0=q_, scalar=1.0, in1=z_, op0=ALU.add, op1=ALU.mult))
                link(eng.tensor_scalar(x_, x_, 0.0, None, ALU.max))
                wait(eng, M["gram"], NH * NT * (b - 1))
                wait(eng, M["ramp"], NT * (b - 1))
                wait(eng, M["dk_ps"], b - 1)
                eng.scalar_tensor_tensor(out=dt_a[:, par, 0, :, :].rearrange("p c h -> p (c h)"), in0=q_, scalar=2.0, in1=x_,
                                         op0=ALU.mult, op1=ALU.add).then_inc(M["dt"], 1)
                wait(eng, M["dt"], b + 1)
                eng.tensor_tensor(dt_a[:, par, 1, :, :], dt_a[:, par, 0, :, :],
                                  neg_A[:, :].unsqueeze(1).to_broadcast([P, NT, NH]), ALU.mult).then_inc(M["a"], 1)

            def grams(b, par, c):
                n = NT * b + c
                wait(eng, M["cb_ps"], n + 1)
                eng.tensor_tensor(cb[:, c % 2, :], bank(0)[:, 0:P], upto[:, :], ALU.mult).then_inc(M["cb"], 1)
                wait(eng, M["segs"], n + 1)
                wait(eng, M["xw"], (NT - 1) * b + max(c - 1, 0))
                eng.tensor_tensor(to_end[:, c % 2, :], segs[:, c % 2, :, P - 1], dt_a[:, par, 0, c, :],
                                  ALU.mult).then_inc(M["end"], 1)
                wait(eng, M["cb"], n + 1)
                wait(eng, M["y_ps"], n - 1)
                for h in range(NH):
                    eng.scalar_tensor_tensor(out=gram[:, c % 2, h, :], in0=segs[:, c % 2, h, :],
                                             scalar=dt_a[:, par, 0, c, h:h + 1], in1=cb[:, c % 2, :], op0=ALU.mult,
                                             op1=ALU.mult).then_inc(M["gram"], 1)

            def states(b, c):
                k = (NT - 1) * b + c
                wait(eng, M["st_ps"], k + 1)
                if c == 0:
                    wait(eng, M["y_ps"], NT * b)
                    eng.tensor_copy(state[:, 0, :], bank(4)[:, 0:DI]).then_inc(M["state"], 1)
                else:
                    wait(eng, M["state_d"], (NT - 2) * b + c)
                    eng.tensor_tensor(state[:, c % 2, :], bank(4)[:, 0:DI], state_d[:, :], ALU.add).then_inc(M["state"], 1)

            def ys(b, par, c):
                n = NT * b + c
                wait(eng, M["y_ps"], n + 1)
                if c == 0:
                    wait(eng, M["g"], n - 1)
                    eng.tensor_copy(y[:, c % 2, :], bank(3)[:, 0:DI]).then_inc(M["y"], 1)
                    return
                k = (NT - 1) * b + c
                wait(eng, M["decay"], b + 1)
                eng.tensor_tensor(y_off[:, :].rearrange("t (h p) -> t h p", h=NH),
                                  bank(3)[:, DI:2 * DI].rearrange("t (h p) -> t h p", h=NH),
                                  decay[:, par, 0, c, :].unsqueeze(2).to_broadcast([P, NH, HD]), ALU.mult).then_inc(M["y_off"], 1)
                wait(eng, M["y_off"], k)
                wait(eng, M["g"], n - 1)
                eng.tensor_tensor(y[:, c % 2, :], bank(3)[:, 0:DI], y_off[:, :], ALU.add).then_inc(M["y"], 1)

            def norms(b, c):
                n = NT * b + c
                wait(eng, M["rms"], 2 * n + 2)
                wait(eng, M["gT_ps"], n - 1)
                eng.tensor_scalar(gn[:, c % 2, :], g[:, c % 2, :], g_rs[:, 1, c:c + 1], None, ALU.mult).then_inc(M["gn"], 1)

            def x3_out(b, at):
                wait(eng, M["o_ps"], b + 1)
                eng.tensor_tensor(X[:, b, :, :], bank(at).rearrange("p (r d) -> p r d", r=NT), X[:, b, :, :],
                                  ALU.add).then_inc(M["x"], 1)

            def step(i, odd, first, second, third, fourth):
                if first:
                    ssm_stats(i + 1)
                if second:
                    grams(i, odd, 0)
                if third:
                    norms(i - 1, 3)
                if first:
                    ssm_xn(i + 1)
                if fourth:
                    router_norm(R2, i - 2)
                if second:
                    grams(i, odd, 1)
                if third:
                    x3_out(i - 1, 4)
                if first:
                    u_low(i + 1)
                if second:
                    states(i, 0)
                    ys(i, odd, 0)
                if first:
                    conv_taps_of(i + 1, 0)
                    conv_taps_of(i + 1, 1)
                if second:
                    norms(i, 0)
                if first:
                    dt_arg(i + 1)
                if second:
                    states(i, 1)
                    ys(i, odd, 1)
                if fourth:
                    router_lg(R2, i - 2, bank(5)[:, 0:NT * NE])
                if second:
                    grams(i, odd, 2)
                if first:
                    softplus(i + 1, 1 - odd)
                if second:
                    ys(i, odd, 2)
                    norms(i, 1)
                    states(i, 2)
                if third:
                    router_stats(R2, i - 1, M["x"])
                if second:
                    grams(i, odd, 3)
                if fourth:
                    router_top(R2, i - 2)
                if second:
                    norms(i, 2)
                if fourth:
                    router_weights(R2, i - 2)
                if second:
                    ys(i, odd, 3)
            skew_pairs(eng, step, before={0: lambda: add_sum(F1, NB - 1, 0)})
            router_norm(R2, NB - 2)
            norms(NB - 1, NT - 1)
            router_lg(R2, NB - 2, bank(7)[:, 0:NT * NE])
            router_top(R2, NB - 2)
            x3_out(NB - 1, 3)
            router_stats(R2, NB - 1, M["x"])

            ffn(F2, 0, True, after_expert=lambda e: router_rest(R2, e))
            ffn(F2, 1, False)
            with eng.Fori(2, NB) as b:
                ffn(F2, b, False)
            ffn(F2, NB, False, True)
            add_sum(F2, NB - 1, 0)

        @block.tensor
        def _(eng):
            eng.wait_ge(consts, N_CONST)
            eng.wait_ge(w_attn, 3 * 16)
            eng.matmul(bank(0)[:, 0:D], qkv_rows[:, 0, :], qkv_rows[:, 1, :], start=True, stop=True).then_inc(prep_ps, 1)
            eng.transpose(bank(1)[:, 0:D], qkv_rows[:, 2, :], ident[:, :])
            eng.transpose(bank(1)[:, D:2 * D], proj_rows[:, :], ident[:, :])
            eng.transpose(bank(1)[:, 2 * D:2 * D + NE], gate_rows[:, :], ident[0:NE, 0:NE]).then_inc(prep_ps, 1)
            eng.wait_ge(w_vecs, 6 * 16)
            eng.matmul(bank(2)[:, 0:VEND], ones[0:1, :], vec_row[0:1, 0:VEND], start=True, stop=True).then_inc(prep_ps, 1)
            eng.wait_ge(prep_sb, 3)

            def scores(b, par):
                wait(eng, S1["q"], b + 1)
                wait(eng, S1["pT"], NT * b)
                if isinstance(b, int) and b == 1:
                    eng.wait_ge(prep2_sb, NE // 4)
                if isinstance(b, int) and b == 2:
                    eng.wait_ge(prep2_sb, NE // 2)
                    eng.wait_ge(prep3_sb, PREP3)
                for r in range(NT):
                    eng.matmul(bank(r), qT[:, par, r * P:(r + 1) * P], xnT[:, par, :], start=True,
                               stop=True).then_inc(S1["scores"], 1)

            def xn_turn(b):
                wait(eng, S1["xn"], NT * b + NT)
                wait(eng, S1["q"], b)
                for r in range(NT):
                    mm = eng.transpose(bank(4)[:, r * P:(r + 1) * P], xn[:, r, :], ident[:, :])
                mm.then_inc(S1["xnT_ps"], 1)

            def qv(b, par):
                wait(eng, S1["xnT"], b + 1)
                eng.matmul(bank(4), a_qk[:, :], xnT[:, par, :], start=True, stop=True).then_inc(S1["q_ps"], 1)
                wait(eng, S1["x1"], b - 1)
                for t in range(NT):
                    mm = eng.matmul(bank(6)[:, t * D:(t + 1) * D], xnT[:, par, t * P:(t + 1) * P], wvT, start=True, stop=True)
                mm.then_inc(S1["v_ps"], 1)

            def p_turn(b):
                for r in range(NT):
                    wait(eng, S1["probs"], NT * b + r + 1)
                    for t in range(NT):
                        mm = eng.transpose(bank(r)[:, t * P:(t + 1) * P], probs[:, r, t * P:(t + 1) * P], ident[:, :])
                    mm.then_inc(S1["pT_ps"], 1)

            def pv(b, par, rs):
                wait(eng, S1["v"], b + 1)
                wait(eng, S1["o"], NT * b)
                for r in rs:
                    wait(eng, S1["pT"], NT * b + r + 1)
                    for t in range(NT):
                        mm = eng.matmul(bank(5)[:, r * D:(r + 1) * D], probsT[:, r, t, :], v[:, par, t, :],
                                        start=(t == 0), stop=(t == NT - 1))
                    if r == NT - 1:
                        mm.then_inc(S1["o_ps"], 1)

            def project(b):
                wait(eng, S1["o"], NT * b + NT)
                wait(eng, S1["v"], least(b + 2, NB))
                for r in range(NT):
                    mm = eng.matmul(bank(6)[:, r * D:(r + 1) * D], attn[:, r, :], wpT, start=True, stop=True)
                mm.then_inc(S1["y_ps"], 1)

            def router_turn(R, b, at, bank_free):
                wait(eng, R["t0"], NT * b + NT)
                bank_free()
                for r in range(NT):
                    mm = eng.transpose(bank(at)[:, r * P:(r + 1) * P], t0[:, r, :], ident[:, :])
                mm.then_inc(R["t_ps"], 1)

            def router_logits(R, b, lg_bank, bank_free):
                wait(eng, R["t"], b + 1)
                bank_free()
                for r in range(NT):
                    mm = eng.matmul(lg_bank[:, r * NE:(r + 1) * NE], tT[:, r * P:(r + 1) * P], gateT, start=True, stop=True)
                mm.then_inc(R["lg_ps"], 1)

            def router_parts(R, b, rt_bank, bank_free):
                wait(eng, R["lo"], b + 1)
                bank_free()
                for r in range(NT):
                    mm = eng.transpose(rt_bank.bitcast(BF16)[0:PARTS * PSTEP, r * P:(r + 1) * P],
                                       rt_parts[:, r, :, :].rearrange("p g e -> p (g e)"), ident_b[:, :])
                mm.then_inc(R["rt_ps"], 1)

            def step(i, odd, first, second, third, fourth):
                if second:
                    scores(i, odd)
                if third:
                    project(i - 1)
                if fourth:
                    router_turn(R1, i - 2, 7, lambda: wait(eng, R1["route"], i - 2))
                if second:
                    p_turn(i)
                if fourth:
                    router_logits(R1, i - 2, bank(7), lambda: None)
                if first:
                    xn_turn(i + 1)
                if second:
                    pv(i, odd, (0, 1))
                if first:
                    qv(i + 1, 1 - odd)
                if second:
                    pv(i, odd, (2, 3))
                if fourth:
                    router_parts(R1, i - 2, bank(7), lambda: wait(eng, R1["lg"], i - 1))

            def expert_weights_1():
                eng.wait_ge(w_ffn, 96)
                eng.wait_ge(S1["pT"], NT)
                for quad in range(NE // 4):
                    for k in range(4):
                        mm = eng.transpose(bank(quad)[:, k * P:(k + 1) * P], w1_rows[:, 4 * quad + k, :], ident[:, :])
                    mm.then_inc(prep2_ps, 1)

            def expert_weights_2():
                eng.wait_ge(consts_late, N_LATE)
                eng.wait_ge(S1["pT"], NT * 2)
                for quad in range(NE // 4):
                    eng.wait_ge(prep2_sb, quad + 1)
                    for k in range(4):
                        mm = eng.transpose(bank(quad)[:, k * P:(k + 1) * P], w2_rows[:, 4 * quad + k, :], ident[:, :])
                    mm.then_inc(prep2_ps, 1)

                eng.wait_ge(taps_ready, PH)
                eng.wait_ge(prep2_sb, NE // 2)
                for k in range(PH):
                    for w in range(CONV_W):
                        mm = eng.transpose(bank(k)[:, w * P:(w + 1) * P], tap_rows[:, k, w, :], ident[:, :])
                    mm.then_inc(prep3_ps, 1)
                for k, j in enumerate((2 + DVE_TILES[0], 2 + DVE_TILES[1], 0, 1)):
                    mm = eng.transpose(bank(2)[:, k * P:(k + 1) * P], in_rows[:, j, :], ident[:, :])
                mm.then_inc(prep3_ps, 1)
                eng.transpose(bank(3)[:, 0:NH], dt_rows[:, :], ident[0:NH, 0:NH])
                eng.transpose(bank(3)[:, NH:NH + NJ + 2], col_rows[:, :], ident[0:NJ + 2, 0:NJ + 2])
                eng.transpose(bank(3)[:, B1:B1 + NE], b1_rows[:, 0:2 * I:2], ident[0:NE, 0:NE])
                for j in range(2):
                    mm = eng.transpose(bank(3)[:, (j + 1) * P:(j + 2) * P], out_rows[:, j * P:(j + 1) * P], ident[:, :])
                mm.then_inc(prep3_ps, 1)

            skew_pairs(eng, step, before={1: expert_weights_1, 2: expert_weights_2})

            def router_rest(R, e):
                if e == 3:
                    router_parts(R, NB - 2, bank(7), lambda: wait(eng, R["lg"], NB - 1))
                elif e == 8:
                    router_turn(R, NB - 1, 7, lambda: wait(eng, R["route"], NB - 1))
                elif e == 10:
                    router_logits(R, NB - 1, bank(7), lambda: None)
                elif e == 15:
                    router_parts(R, NB - 1, bank(7), lambda: wait(eng, R["lg"], NB))

            project(NB - 1)
            router_turn(R1, NB - 2, 7, lambda: wait(eng, R1["route"], NB - 2))
            router_logits(R1, NB - 2, bank(7), lambda: None)

            def ffn_out(F, b, e):
                wait(eng, F["lo"], NE * b + e + 1)
                if e == 0:
                    wait(eng, F["acc_sb"], b)
                    if isinstance(b, int) and b == 0:
                        eng.wait_ge(S1["x1"], NB)
                    for g in range(PARTS):
                        eng.matmul(bank(6), b2_parts[:, g, :], route[:, b, :], start=(g == 0), stop=False)
                eng.matmul(bank(6), w2_hi[:, e, :], s_hi[:, e % NR, :], start=False, stop=False)
                eng.matmul(bank(6), w2_hi[:, e, :], s_lo[:, e % NR, :], start=False, stop=False)
                eng.matmul(bank(6), w2_lo[:, e, :], s_hi[:, e % NR, :], start=False, stop=(e == NE - 1)).then_inc(F["out"], 1)

            LAG = 3

            def turn_sum(F, b, at):
                wait(eng, F["acc_sb"], b + 1)
                wait(eng, F["x"], b)
                for r in range(NT):
                    mm = eng.transpose(bank(at)[:, r * P:(r + 1) * P], acc_sb[:, r * P:(r + 1) * P], ident[:, :])
                mm.then_inc(F["back"], 1)

            def ffn(F, b, peeled, tail=False, after_expert=None):
                for e in range(NE):
                    if not tail:
                        wait(eng, F["act"], NE * b + e + 1 - 4)
                        if F is F2 and e == 3 and isinstance(b, int) and b == 0:
                            eng.wait_ge(M["x"], NB)
                        eng.matmul(bank(e % 4), w1_hi[:, e, :], ffn_hi[:, b, :], start=True, stop=False)
                        eng.matmul(bank(e % 4), w1_hi[:, e, :], ffn_lo[:, b, :], start=False, stop=False)
                        eng.matmul(bank(e % 4), w1_lo[:, e, :], ffn_hi[:, b, :], start=False, stop=True).then_inc(F["h"], 1)
                        wait(eng, F["s"], NE * b + e + 1 - 2)
                        eng.matmul(bank(4 + e % 2), pick[:, e, :], route[:, b, :], start=True,
                                   stop=True).then_inc(F["rb"], 1)
                    if e >= LAG:
                        if not tail:
                            ffn_out(F, b, e - LAG)
                    elif tail or not peeled:
                        ffn_out(F, b - 1, NE - LAG + e)
                    if e == 6 and not tail and not peeled:
                        turn_sum(F, b - 1, 7)
                    if after_expert:
                        after_expert(e)

            eng.wait_ge(prep2_sb, NE // 2)
            eng.wait_ge(b2_split, 4)
            eng.wait_ge(R1["stash"], 1)
            eng.wait_ge(R1["route"], 1)
            ffn(F1, 0, True, after_expert=lambda e: router_rest(R1, e))
            eng.wait_ge(R1["stash"], NB)
            eng.wait_ge(R1["route"], NB)
            ffn(F1, 1, False)
            with eng.Fori(2, NB) as b:
                ffn(F1, b, False)
            ffn(F1, NB, False, True)
            eng.wait_ge(F1["act"], NE * NB)
            eng.wait_ge(F1["s"], NE * NB)
            eng.wait_ge(F1["x"], NB - 1)

            def product(out, w, a, first=True, last=True):
                eng.matmul(out, w[0], a[0], start=first, stop=False)
                eng.matmul(out, w[0], a[1], start=False, stop=False)
                return eng.matmul(out, w[1], a[0], start=False, stop=last)

            def parts_of(t, *at):
                return t[(slice(None), 0, *at)], t[(slice(None), 1, *at)]

            def u_turn(b):
                wait(eng, M["xn"], NT * b + NT)
                wait(eng, M["z_raw"], 2 * b)
                for r in range(NT):
                    mm = eng.transpose(bank(7)[:, r * P:(r + 1) * P], xn[:, r, :], ident[:, :])
                mm.then_inc(M["uT_ps"], 1)

            def project_in(b, k):
                wait(eng, M["u_lo"], b + 1)
                if k == 1:
                    wait(eng, F1["acc_sb"], NB)
                    wait(eng, M["xs"], 3 * b)
                product(bank(7 - k), parts_of(bcT, k, slice(None)), parts_of(uT, slice(PAD, None))).then_inc(M["cv_ps"], 1)

            def conv(b, k):
                if isinstance(b, int) and b == 0:
                    eng.wait_ge(taps_ready, PH + 4)
                if k == 0:
                    wait(eng, M["conv"], 6 * b + 3)
                else:
                    wait(eng, M["z_raw"], 2 * b + 1)
                for s in range(CONV_W):
                    mm = product(bank(7 - k), parts_of(tapT, k, CONV_W - 1 - s, slice(None)),
                                 parts_of(uT, slice(PAD - s, PAD - s + SEQ)), s == 0, s == CONV_W - 1)
                mm.then_inc(M["cv_ps"], 1)

            def z_proj(b, k):
                if k == 0:
                    wait(eng, M["conv"], 6 * b + 6)
                else:
                    wait(eng, M["raw"], b + 1)
                for c in range(2):
                    at = PAD + (2 * k + c) * P
                    mm = product(bank(6 + k)[:, c * DI:(c + 1) * DI], parts_of(uT, slice(at, at + P)), parts_of(zT, slice(None)))
                mm.then_inc(M["z_ps"], 1)

            def dt_proj(b):
                wait(eng, M["state"], (NT - 1) * (b - 1) + 1)
                for c in range(NT):
                    at = PAD + c * P
                    mm = product(bank(4)[:, c * NH:(c + 1) * NH], parts_of(uT, slice(at, at + P)), parts_of(dtT, slice(None)))
                mm.then_inc(M["dt_ps"], 1)

            def decay_sums(b, par):
                wait(eng, M["a"], b + 1)
                wait(eng, M["state"], (NT - 1) * b)
                a_all = dt_a[:, par, 1, :, :].rearrange("p c h -> p (c h)")
                eng.matmul(bank(4)[:, 0:NT * NH], upto[:, :], a_all, start=True, stop=True)
                eng.matmul(bank(4)[:, NT * NH:2 * NT * NH], ones[:, :], a_all, start=True,
                           stop=True).then_inc(M["dk_ps"], 1)

            def front(b, par, c):
                n = NT * b + c
                at = slice(c * P, (c + 1) * P)
                if c == 0:
                    wait(eng, M["xs"], 3 * b + 3)
                wait(eng, M["cb"], n)
                eng.matmul(bank(0)[:, 0:P], xs[:, par, 2, at], xs[:, par, 3, at], start=True,
                           stop=True).then_inc(M["cb_ps"], 1)
                wait(eng, M["xb"], n)
                for j in range(3):
                    mm = eng.transpose(bank(1)[:, j * P:(j + 1) * P], xs[:, par, j, at], ident[:, :])
                mm.then_inc(M["xb_ps"], 1)
                wait(eng, M["segs"], n)
                wait(eng, M["ramp"], n + 1)
                eng.matmul(bank(2), after[:, :], ramp[:, c % 2, :, :].rearrange("k h t -> k (h t)"), start=True,
                           stop=True).then_inc(M["seg_ps"], 1)

            def back(b, par, c):
                n = NT * b + c
                at = slice(c * P, (c + 1) * P)
                wait(eng, M["y"], n)
                for j in range(2):
                    eng.matmul(bank(3)[:, j * P:(j + 1) * P], xs[:, par, j, at], skip_diag[:, j, :], start=(j == 0), stop=False,
                               skip_group_check=True)
                if c:
                    wait(eng, M["state"], (NT - 1) * b + c)
                    eng.matmul(bank(3)[:, DI:2 * DI], xs[:, par, 3, at], state[:, (c - 1) % 2, :], start=False, stop=True,
                               skip_group_check=True)
                wait(eng, M["gram"], NH * (n + 1))
                for h in range(NH):
                    mm = eng.matmul(bank(3)[:, h * HD:(h + 1) * HD], gram[:, c % 2, h, :],
                                    xb_tok[:, c % 2, h // 2, (h % 2) * HD:(h % 2 + 1) * HD], start=False, stop=(h == NH - 1),
                                    skip_group_check=True)
                mm.then_inc(M["y_ps"], 1)
                if c < NT - 1:
                    k = (NT - 1) * b + c
                    if c == 0:
                        wait(eng, M["x"], b)
                        wait(eng, M["decay"], b + 1)
                    if c == 1:
                        wait(eng, M["dt_x"], least(b + 2, NB))
                    wait(eng, M["state"], k)
                    wait(eng, M["xw"], k + 1)
                    eng.matmul(bank(4)[:, 0:DI], xb_tok[:, c % 2, 2, :], xw[:, c % 2, :], start=True,
                               stop=True).then_inc(M["st_ps"], 1)

            def g_turn(b, c):
                n = NT * b + c
                wait(eng, M["gn"], n + 1)
                wait(eng, M["gT"], n)
                if c == 0:
                    wait(eng, R2["lg"], b - 1)
                if c == NT - 1:
                    wait(eng, R2["route"], b - 1)
                for j in range(2):
                    mm = eng.transpose(bank(5)[:, j * P:(j + 1) * P], gn[:, c % 2, j * P:(j + 1) * P], ident[:, :])
                mm.then_inc(M["gT_ps"], 1)

            def out_proj(b, at):
                wait(eng, M["gT"], NT * b + NT)
                wait(eng, M["x"], b)
                wait(eng, M["decay"], least(b + 2, NB))
                wait(eng, M["state"], (NT - 1) * (b + 1))
                for r in range(NT):
                    for j in range(2):
                        mm = eng.matmul(bank(at)[:, r * D:(r + 1) * D], gT[:, j, r:SEQ:NT], outT[:, j, :], start=(j == 0),
                                        stop=(j == 1))
                mm.then_inc(M["o_ps"], 1)

            def first_chunks():
                turn_sum(F1, NB - 1, 0)
                eng.wait_ge(F1["x"], NB)

            def step(i, odd, first, second, third, fourth):
                if second:
                    front(i, odd, 0)
                    front(i, odd, 1)
                if third:
                    g_turn(i - 1, 3)
                if first:
                    u_turn(i + 1)
                if third:
                    out_proj(i - 1, 4)
                if second:
                    back(i, odd, 0)
                if first:
                    project_in(i + 1, 0)
                if fourth:
                    router_turn(R2, i - 2, 5, lambda: wait(eng, M["gT"], least(NT * i, NT * NB)))
                if first:
                    project_in(i + 1, 1)
                    dt_proj(i + 1)
                if second:
                    front(i, odd, 2)
                    back(i, odd, 1)
                if fourth:
                    router_logits(R2, i - 2, bank(5), lambda: None)
                if first:
                    conv(i + 1, 0)
                if second:
                    back(i, odd, 2)
                    g_turn(i, 0)
                    front(i, odd, 3)
                if first:
                    z_proj(i + 1, 0)
                    z_proj(i + 1, 1)
                if second:
                    g_turn(i, 1)
                if first:
                    decay_sums(i + 1, 1 - odd)
                    conv(i + 1, 1)
                if second:
                    back(i, odd, 3)
                    g_turn(i, 2)
                if fourth:
                    router_parts(R2, i - 2, bank(5), lambda: wait(eng, M["gT"], least(NT * i + 3, NT * NB)))
            skew_pairs(eng, step, before={0: first_chunks})
            router_turn(R2, NB - 2, 7, lambda: wait(eng, M["z_raw"], 2 * NB))
            router_logits(R2, NB - 2, bank(7), lambda: None)
            g_turn(NB - 1, NT - 1)
            eng.wait_ge(M["y"], NB * NT)
            out_proj(NB - 1, 3)
            eng.wait_ge(R2["stash"], 1)
            eng.wait_ge(R2["route"], NB - 2)
            eng.wait_ge(R2["lg"], NB - 2)
            ffn(F2, 0, True, after_expert=lambda e: router_rest(R2, e))
            eng.wait_ge(R2["stash"], NB)
            eng.wait_ge(R2["route"], NB)
            ffn(F2, 1, False)
            with eng.Fori(2, NB) as b:
                ffn(F2, b, False)
            ffn(F2, NB, False, True)
            turn_sum(F2, NB - 1, 0)


_INS = ['L0_attn_a_x', 'L0_attn_a_w_qkv', 'L0_attn_a_w_proj', 'L0_attn_a_b_proj', 'L0_attn_b_W_in', 'L0_attn_b_conv_w',
        'L0_attn_b_conv_b', 'L0_attn_b_dt_bias', 'L0_attn_b_A_log', 'L0_attn_b_D', 'L0_attn_b_norm_w', 'L0_attn_b_W_out',
        'L0_ffn_scale', 'L0_ffn_gate_w', 'L0_ffn_gate_b', 'L0_ffn_mlp1_w', 'L0_ffn_mlp1_b', 'L0_ffn_mlp2_w', 'L0_ffn_mlp2_b']


def kernel(**inputs):
    import concourse.bacc as bacc
    from concourse.bass_utils import run_bass_kernel_spmd
    nc = bacc.Bacc("TRN2", target_bir_lowering=False, num_devices=1)
    ins = {name: np.ascontiguousarray(np.asarray(inputs[name])) for name in _INS}
    drams = [nc.dram_tensor(f"in_{name}_dram", ins[name].shape, F32, kind="ExternalInput").ap() for name in _INS]
    out = nc.dram_tensor("out_dram", (NB, SEQ, D), F32, kind="ExternalOutput").ap()
    build(nc, *drams, out)
    arrays = {f"in_{name}_dram": ins[name] for name in _INS}
    return run_bass_kernel_spmd(nc, [arrays], core_ids=[0]).results[0]["out_dram"]
```
